# Optimizing a Trainium2 kernel written in Bass

```python
import numpy as np
import jax
import jax.numpy as jnp

def _softmax(x, axis=-1):
    return jax.nn.softmax(x, axis=axis)

def _gelu(x):
    return jax.nn.gelu(x, approximate=True)

def _silu(x):
    return jax.nn.silu(x)

def _sigmoid(x):
    return jax.nn.sigmoid(x)

def _layernorm(x, axis=-1, eps=1e-05):
    m = jnp.mean(x, axis=axis, keepdims=True)
    v = jnp.var(x, axis=axis, keepdims=True)
    return (x - m) / jnp.sqrt(v + eps)

def _scatter_add(tgt, idx, src, axis=0):
    return tgt.at[idx].add(src)

def _segment_sum(src, seg, n):
    return jax.ops.segment_sum(src, seg, n)
kernel_name = 'mk_early_fusion_d2_tok_img1024_r4_2afa81'

def setup_inputs(seed: int=0):
    np.random.seed(seed)
    _w = jnp.asarray

    def _rec_inputs():
        import jax
        import jax.numpy as jnp
        _rk = jax.random.key(seed)
        x = -0.000392918 + 0.999932 * jax.random.normal(jax.random.fold_in(_rk, 1), (8, 256, 256, 1), jnp.float32)
        txt = -0.000282583 + 0.544222 * jax.random.normal(jax.random.fold_in(_rk, 2), (8, 32, 256), jnp.float32)
        return (x, txt)
    x, txt = _rec_inputs()

    def _L0_tok_setup():
        import jax, jax.numpy as jnp
        import numpy as np
        INV_SQRT2 = 0.7071067811865476
        LEVEL = 3

        def _split(x, axis):
            ax = axis % x.ndim
            sl0 = [slice(None)] * x.ndim
            sl0[ax] = slice(0, None, 2)
            sl1 = [slice(None)] * x.ndim
            sl1[ax] = slice(1, None, 2)
            x0, x1 = (x[tuple(sl0)], x[tuple(sl1)])
            return ((x0 + x1) * INV_SQRT2, (x0 - x1) * INV_SQRT2)

        def _merge(lo, hi, axis):
            ax = axis % lo.ndim
            e = (lo + hi) * INV_SQRT2
            o = (lo - hi) * INV_SQRT2
            s = jnp.stack([e, o], axis=ax + 1)
            shape = list(lo.shape)
            shape[ax] *= 2
            return s.reshape(shape)

        def _dwt2(x):
            lo, hi = _split(x, -1)
            a, h = _split(lo, -2)
            v, d = _split(hi, -2)
            return (a, h, v, d)

        def _idwt2(a, h, v, d):
            lo = _merge(a, h, -2)
            hi = _merge(v, d, -2)
            return _merge(lo, hi, -1)
        key = jax.random.key(seed)
        ks = jax.random.split(key, 8)
        B, H, W = (16, 256, 256)
        x = jax.random.normal(ks[0], (B, H, W, 1), dtype=jnp.float32)
        na = H // 8 * (W // 8)
        n2 = H // 4 * (W // 4)
        n1 = H // 2 * (W // 2)
        scale = 0.02
        Wa = jax.random.normal(ks[1], (na, 1), dtype=jnp.float32) * scale
        ba = jnp.zeros((1,), jnp.float32)
        Wd1 = jax.random.normal(ks[2], (3 * na, 3), dtype=jnp.float32) * scale
        bd1 = jnp.zeros((3,), jnp.float32)
        Wd2 = jax.random.normal(ks[3], (3 * n2, 3), dtype=jnp.float32) * scale
        bd2 = jnp.zeros((3,), jnp.float32)
        Wd3 = jax.random.normal(ks[4], (3 * n1, 3), dtype=jnp.float32) * scale
        bd3 = jnp.zeros((3,), jnp.float32)
        return {'x': x, 'Wa': Wa, 'ba': ba, 'Wd1': Wd1, 'bd1': bd1, 'Wd2': Wd2, 'bd2': bd2, 'Wd3': Wd3, 'bd3': bd3}
    _L0_tok_all = _L0_tok_setup()
    _L0_tok_in = {k: v for k, v in _L0_tok_all.items() if k in ('Wa', 'ba', 'Wd1', 'bd1', 'Wd2', 'bd2', 'Wd3', 'bd3')}
    del _L0_tok_all

    def _L0_attn_setup():
        import jax, jax.numpy as jnp
        import numpy as np
        S, B, E = (512, 8, 256)
        GAMMA = 0.5
        key = jax.random.key(seed)
        ks = jax.random.split(key, 4)
        w_scale = 1.0 / E
        inputs = jax.random.normal(ks[0], (S, B, E), dtype=jnp.float32)
        Wq = jax.random.normal(ks[1], (E, E), dtype=jnp.float32) * w_scale
        Wk = jax.random.normal(ks[2], (E, E), dtype=jnp.float32) * w_scale
        Wv = jax.random.normal(ks[3], (E, E), dtype=jnp.float32) * w_scale
        bq = jnp.zeros((E,), jnp.float32)
        bk = jnp.zeros((E,), jnp.float32)
        bv = jnp.zeros((E,), jnp.float32)
        return {'inputs': inputs, 'Wq': Wq, 'bq': bq, 'Wk': Wk, 'bk': bk, 'Wv': Wv, 'bv': bv}
    _L0_attn_all = _L0_attn_setup()
    _L0_attn_in = {k: v for k, v in _L0_attn_all.items() if k in ('Wq', 'bq', 'Wk', 'bk', 'Wv', 'bv')}
    del _L0_attn_all

    def _L0_ffn_setup():
        import jax, jax.numpy as jnp
        import numpy as np
        B, S, H = (2, 1024, 256)
        I = 128
        E = 8
        TOPK = 2
        NGROUP = 2
        TOPK_GROUP = 1
        ROUTED_SCALE = 1.0

        def _silu(x):
            return x * jax.nn.sigmoid(x)
        key = jax.random.key(seed)
        ks = jax.random.split(key, 9)

        def w(k, shape, s=0.05):
            return jax.random.normal(k, shape, dtype=jnp.float32) * s
        return {'hidden_states': jax.random.normal(ks[0], (B, S, H), dtype=jnp.float32), 'router_weight': w(ks[1], (E, H)), 'correction_bias': w(ks[2], (E,)), 'w_gate': w(ks[3], (E, H, I)), 'w_up': w(ks[4], (E, H, I)), 'w_down': w(ks[5], (E, I, H)), 'sw_gate': w(ks[6], (H, I)), 'sw_up': w(ks[7], (H, I)), 'sw_down': w(ks[8], (I, H))}
    _L0_ffn_all = _L0_ffn_setup()
    _L0_ffn_in = {k: v for k, v in _L0_ffn_all.items() if k in ('router_weight', 'correction_bias', 'w_gate', 'w_up', 'w_down', 'sw_gate', 'sw_up', 'sw_down')}
    del _L0_ffn_all

    def _L1_attn_setup():
        import jax, jax.numpy as jnp
        import numpy as np
        B, N, D = (2, 512, 256)
        H, G = (16, 4)
        HD = D // H
        key = jax.random.key(seed)
        ks = jax.random.split(key, 9)
        s = 0.02
        return {'x': jax.random.normal(ks[0], (B, N, D), dtype=jnp.float32), 'Wq': jax.random.normal(ks[1], (D, D), dtype=jnp.float32) * s, 'bq': jax.random.normal(ks[2], (D,), dtype=jnp.float32) * s, 'Wk': jax.random.normal(ks[3], (G * HD, D), dtype=jnp.float32) * s, 'bk': jax.random.normal(ks[4], (G * HD,), dtype=jnp.float32) * s, 'Wv': jax.random.normal(ks[5], (G * HD, D), dtype=jnp.float32) * s, 'bv': jax.random.normal(ks[6], (G * HD,), dtype=jnp.float32) * s, 'Wo': jax.random.normal(ks[7], (D, D), dtype=jnp.float32) * s, 'bo': jax.random.normal(ks[8], (D,), dtype=jnp.float32) * s}
    _L1_attn_all = _L1_attn_setup()
    _L1_attn_in = {k: v for k, v in _L1_attn_all.items() if k in ('Wq', 'bq', 'Wk', 'bk', 'Wv', 'bv', 'Wo', 'bo')}
    del _L1_attn_all

    def _L1_ffn_setup():
        import jax, jax.numpy as jnp
        import numpy as np
        H = 256
        I = 128
        E = 8
        K = 2
        SI = I * 2
        B, S = (2, 256)

        def _mlp(x, gw, uw, dw):
            return jax.nn.silu(x @ gw.T) * (x @ uw.T) @ dw.T
        key = jax.random.key(seed)
        ks = jax.random.split(key, 9)
        s = 0.02
        return {'x': jax.random.normal(ks[0], (B, S, H), jnp.float32), 'gate_w': jax.random.normal(ks[1], (E, H), jnp.float32) * s, 'lb_bias': jnp.zeros((E,), jnp.float32), 'expert_gate_w': jax.random.normal(ks[2], (E, I, H), jnp.float32) * s, 'expert_up_w': jax.random.normal(ks[3], (E, I, H), jnp.float32) * s, 'expert_down_w': jax.random.normal(ks[4], (E, H, I), jnp.float32) * s, 'shared_gate_w': jax.random.normal(ks[5], (SI, H), jnp.float32) * s, 'shared_up_w': jax.random.normal(ks[6], (SI, H), jnp.float32) * s, 'shared_down_w': jax.random.normal(ks[7], (H, SI), jnp.float32) * s}
    _L1_ffn_all = _L1_ffn_setup()
    _L1_ffn_in = {k: v for k, v in _L1_ffn_all.items() if k in ('gate_w', 'lb_bias', 'expert_gate_w', 'expert_up_w', 'expert_down_w', 'shared_gate_w', 'shared_up_w', 'shared_down_w')}
    del _L1_ffn_all
    return {'x': x, 'txt': txt, 'L0_tok_Wa': _L0_tok_in['Wa'], 'L0_tok_ba': _L0_tok_in['ba'], 'L0_tok_Wd1': _L0_tok_in['Wd1'], 'L0_tok_bd1': _L0_tok_in['bd1'], 'L0_tok_Wd2': _L0_tok_in['Wd2'], 'L0_tok_bd2': _L0_tok_in['bd2'], 'L0_tok_Wd3': _L0_tok_in['Wd3'], 'L0_tok_bd3': _L0_tok_in['bd3'], 'L0_attn_Wq': _L0_attn_in['Wq'], 'L0_attn_bq': _L0_attn_in['bq'], 'L0_attn_Wk': _L0_attn_in['Wk'], 'L0_attn_bk': _L0_attn_in['bk'], 'L0_attn_Wv': _L0_attn_in['Wv'], 'L0_attn_bv': _L0_attn_in['bv'], 'L0_ffn_router_weight': _L0_ffn_in['router_weight'], 'L0_ffn_correction_bias': _L0_ffn_in['correction_bias'], 'L0_ffn_w_gate': _L0_ffn_in['w_gate'], 'L0_ffn_w_up': _L0_ffn_in['w_up'], 'L0_ffn_w_down': _L0_ffn_in['w_down'], 'L0_ffn_sw_gate': _L0_ffn_in['sw_gate'], 'L0_ffn_sw_up': _L0_ffn_in['sw_up'], 'L0_ffn_sw_down': _L0_ffn_in['sw_down'], 'L1_attn_Wq': _L1_attn_in['Wq'], 'L1_attn_bq': _L1_attn_in['bq'], 'L1_attn_Wk': _L1_attn_in['Wk'], 'L1_attn_bk': _L1_attn_in['bk'], 'L1_attn_Wv': _L1_attn_in['Wv'], 'L1_attn_bv': _L1_attn_in['bv'], 'L1_attn_Wo': _L1_attn_in['Wo'], 'L1_attn_bo': _L1_attn_in['bo'], 'L1_ffn_gate_w': _L1_ffn_in['gate_w'], 'L1_ffn_lb_bias': _L1_ffn_in['lb_bias'], 'L1_ffn_expert_gate_w': _L1_ffn_in['expert_gate_w'], 'L1_ffn_expert_up_w': _L1_ffn_in['expert_up_w'], 'L1_ffn_expert_down_w': _L1_ffn_in['expert_down_w'], 'L1_ffn_shared_gate_w': _L1_ffn_in['shared_gate_w'], 'L1_ffn_shared_up_w': _L1_ffn_in['shared_up_w'], 'L1_ffn_shared_down_w': _L1_ffn_in['shared_down_w']}

def reference(x, txt, L0_tok_Wa, L0_tok_ba, L0_tok_Wd1, L0_tok_bd1, L0_tok_Wd2, L0_tok_bd2, L0_tok_Wd3, L0_tok_bd3, L0_attn_Wq, L0_attn_bq, L0_attn_Wk, L0_attn_bk, L0_attn_Wv, L0_attn_bv, L0_ffn_router_weight, L0_ffn_correction_bias, L0_ffn_w_gate, L0_ffn_w_up, L0_ffn_w_down, L0_ffn_sw_gate, L0_ffn_sw_up, L0_ffn_sw_down, L1_attn_Wq, L1_attn_bq, L1_attn_Wk, L1_attn_bk, L1_attn_Wv, L1_attn_bv, L1_attn_Wo, L1_attn_bo, L1_ffn_gate_w, L1_ffn_lb_bias, L1_ffn_expert_gate_w, L1_ffn_expert_up_w, L1_ffn_expert_down_w, L1_ffn_shared_gate_w, L1_ffn_shared_up_w, L1_ffn_shared_down_w):
    import jax
    import jax.numpy as jnp

    def _L0_tok_ref(x, Wa, ba, Wd1, bd1, Wd2, bd2, Wd3, bd3):
        import jax, jax.numpy as jnp
        import numpy as np
        INV_SQRT2 = 0.7071067811865476
        LEVEL = 3

        def _split(x, axis):
            ax = axis % x.ndim
            sl0 = [slice(None)] * x.ndim
            sl0[ax] = slice(0, None, 2)
            sl1 = [slice(None)] * x.ndim
            sl1[ax] = slice(1, None, 2)
            x0, x1 = (x[tuple(sl0)], x[tuple(sl1)])
            return ((x0 + x1) * INV_SQRT2, (x0 - x1) * INV_SQRT2)

        def _merge(lo, hi, axis):
            ax = axis % lo.ndim
            e = (lo + hi) * INV_SQRT2
            o = (lo - hi) * INV_SQRT2
            s = jnp.stack([e, o], axis=ax + 1)
            shape = list(lo.shape)
            shape[ax] *= 2
            return s.reshape(shape)

        def _dwt2(x):
            lo, hi = _split(x, -1)
            a, h = _split(lo, -2)
            v, d = _split(hi, -2)
            return (a, h, v, d)

        def _idwt2(a, h, v, d):
            lo = _merge(a, h, -2)
            hi = _merge(v, d, -2)
            return _merge(lo, hi, -1)
        img = x[..., 0]
        B = img.shape[0]
        details = []
        cur = img
        for _ in range(LEVEL):
            cur, h, v, d = _dwt2(cur)
            details.append((h, v, d))
        aw = jax.nn.sigmoid(cur.reshape(B, -1) @ Wa + ba)
        rec = cur * aw[:, :, None]
        det_params = [(Wd1, bd1), (Wd2, bd2), (Wd3, bd3)]
        for (h, v, d), (Wd, bd) in zip(reversed(details), det_params):
            flat = jnp.stack([h, v, d], axis=1).reshape(B, -1)
            w = jax.nn.softmax(flat @ Wd + bd, axis=-1)
            rec = _idwt2(rec, h * w[:, 0, None, None], v * w[:, 1, None, None], d * w[:, 2, None, None])
        return rec

    def _L0_attn_ref(inputs, Wq, bq, Wk, bk, Wv, bv):
        import jax, jax.numpy as jnp
        import numpy as np
        S, B, E = (512, 8, 256)
        GAMMA = 0.5
        q = inputs @ Wq.T + bq
        k = inputs @ Wk.T + bk
        v = inputs @ Wv.T + bv
        q2 = jnp.sum(q * q, axis=-1)
        k2 = jnp.sum(k * k, axis=-1)
        qk = jnp.einsum('tbe,jbe->tjb', q, k)
        d2 = q2[:, None, :] + k2[None, :, :] - 2.0 * qk
        d2 = jnp.maximum(d2, 0.0)
        sim = jax.nn.softmax(-GAMMA * d2, axis=1)
        return jnp.einsum('tjb,jbe->tbe', sim, v)

    def _L0_ffn_ref(hidden_states, router_weight, correction_bias, w_gate, w_up, w_down, sw_gate, sw_up, sw_down):
        import jax, jax.numpy as jnp
        import numpy as np
        B, S, H = (2, 1024, 256)
        I = 128
        E = 8
        TOPK = 2
        NGROUP = 2
        TOPK_GROUP = 1
        ROUTED_SCALE = 1.0

        def _silu(x):
            return x * jax.nn.sigmoid(x)
        b, s, h = hidden_states.shape
        x = hidden_states.reshape(-1, h)
        logits = x @ router_weight.T
        scores = jax.nn.sigmoid(logits)
        scores_for_choice = scores + correction_bias[None, :]
        e_per_g = E // NGROUP
        group_scores = jax.lax.top_k(scores_for_choice.reshape(-1, NGROUP, e_per_g), 2)[0].sum(-1)
        group_idx = jax.lax.top_k(group_scores, TOPK_GROUP)[1]
        group_mask = jax.nn.one_hot(group_idx, NGROUP, dtype=scores.dtype).sum(1)
        score_mask = jnp.repeat(group_mask, e_per_g, axis=1)
        masked = jnp.where(score_mask > 0, scores_for_choice, 0.0)
        topk_idx = jax.lax.top_k(masked, TOPK)[1]
        topk_w = jnp.take_along_axis(scores, topk_idx, axis=1)
        topk_w = topk_w / (topk_w.sum(-1, keepdims=True) + 1e-20)
        topk_w = topk_w * ROUTED_SCALE
        comb = (jax.nn.one_hot(topk_idx, E, dtype=x.dtype) * topk_w[..., None]).sum(1)
        g = jnp.einsum('th,ehi->tei', x, w_gate)
        u = jnp.einsum('th,ehi->tei', x, w_up)
        y = jnp.einsum('tei,eih->teh', _silu(g) * u, w_down)
        routed = jnp.einsum('teh,te->th', y, comb).reshape(b, s, h)
        shared = _silu(hidden_states @ sw_gate) * (hidden_states @ sw_up) @ sw_down
        return routed + shared

    def _L1_attn_ref(x, Wq, bq, Wk, bk, Wv, bv, Wo, bo):
        import jax, jax.numpy as jnp
        import numpy as np
        B, N, D = (2, 512, 256)
        H, G = (16, 4)
        HD = D // H
        b, n, d = x.shape
        hpg = H // G
        q = (x @ Wq.T + bq).reshape(b, n, G, hpg, HD)
        k = (x @ Wk.T + bk).reshape(b, n, G, HD)
        v = (x @ Wv.T + bv).reshape(b, n, G, HD)
        scale = 1.0 / jnp.sqrt(jnp.float32(HD))
        scores = jnp.einsum('bqghd,bkgd->bghqk', q, k) * scale
        attn = jax.nn.softmax(scores, axis=-1)
        y = jnp.einsum('bghqk,bkgd->bqghd', attn, v).reshape(b, n, d)
        return y @ Wo.T + bo

    def _L1_ffn_ref(x, gate_w, lb_bias, expert_gate_w, expert_up_w, expert_down_w, shared_gate_w, shared_up_w, shared_down_w):
        import jax, jax.numpy as jnp
        import numpy as np
        H = 256
        I = 128
        E = 8
        K = 2
        SI = I * 2
        B, S = (2, 256)

        def _mlp(x, gw, uw, dw):
            return jax.nn.silu(x @ gw.T) * (x @ uw.T) @ dw.T
        b, s, h = x.shape
        xf = x.reshape(-1, h)
        logits = xf @ gate_w.T + lb_bias
        scores = jax.nn.sigmoid(logits.astype(jnp.float32))
        topw, topi = jax.lax.top_k(scores, K)
        topw = (topw / (topw.sum(-1, keepdims=True) + 1e-08)).astype(x.dtype)
        out = jnp.zeros_like(xf)
        for e in range(E):
            m = topi == e
            sel = m.any(axis=-1)
            cnt = m.sum()
            wmean = (topw * m).sum() / jnp.maximum(cnt, 1).astype(topw.dtype)
            y = _mlp(xf, expert_gate_w[e], expert_up_w[e], expert_down_w[e])
            out = out + jnp.where(sel[:, None], y * wmean, jnp.zeros((), x.dtype))
        out = out.reshape(b, s, h)
        out = out + _mlp(x, shared_gate_w, shared_up_w, shared_down_w)
        return out
    h = _L0_tok_ref(x, L0_tok_Wa, L0_tok_ba, L0_tok_Wd1, L0_tok_bd1, L0_tok_Wd2, L0_tok_bd2, L0_tok_Wd3, L0_tok_bd3)
    h = jnp.concatenate([h, txt], axis=1)
    h = h + _L0_attn_ref(_layernorm(h, axis=-1), L0_attn_Wq, L0_attn_bq, L0_attn_Wk, L0_attn_bk, L0_attn_Wv, L0_attn_bv)
    h = h + _L0_ffn_ref(_layernorm(h, axis=-1), L0_ffn_router_weight, L0_ffn_correction_bias, L0_ffn_w_gate, L0_ffn_w_up, L0_ffn_w_down, L0_ffn_sw_gate, L0_ffn_sw_up, L0_ffn_sw_down)
    h = h + _L1_attn_ref(_layernorm(h, axis=-1), L1_attn_Wq, L1_attn_bq, L1_attn_Wk, L1_attn_bk, L1_attn_Wv, L1_attn_bv, L1_attn_Wo, L1_attn_bo)
    h = h + _L1_ffn_ref(_layernorm(h, axis=-1), L1_ffn_gate_w, L1_ffn_lb_bias, L1_ffn_expert_gate_w, L1_ffn_expert_up_w, L1_ffn_expert_down_w, L1_ffn_shared_gate_w, L1_ffn_shared_up_w, L1_ffn_shared_down_w)
    return h

_drawn_inputs = setup_inputs


def setup_inputs(seed=0):
    import zlib

    import numpy as np

    out = dict(_drawn_inputs(seed))
    spreads = {'L0_tok_bd1': (0.0, 0.1),
     'L0_tok_bd2': (0.0, 0.339),
     'L0_tok_bd3': (0.0, 0.306),
     'L0_attn_bq': (0.0, 0.352),
     'L0_attn_bk': (0.0, 0.622),
     'L0_attn_bv': (0.0, 0.1),
     'L1_ffn_lb_bias': (0.0, 0.8)}
    factors = {'L0_attn_Wq': 6.609,
     'L1_attn_Wq': 8.0,
     'L1_attn_bq': 8.0,
     'L1_attn_Wk': 8.0,
     'L1_attn_bk': 64.0,
     'L1_attn_bv': 4.348,
     'L1_ffn_gate_w': 4.537,
     'L1_ffn_expert_gate_w': 3.896,
     'L1_ffn_expert_up_w': 3.838,
     'L1_ffn_expert_down_w': 3.812,
     'L1_ffn_shared_gate_w': 2.813,
     'L1_ffn_shared_up_w': 2.766,
     'L1_ffn_shared_down_w': 2.775}
    for name, (base, spread) in spreads.items():
        noise = np.random.default_rng([zlib.crc32(name.encode()), seed]).standard_normal(out[name].shape)
        drawn = base * np.exp(spread * noise) if base else spread * noise
        out[name] = jnp.asarray(drawn.astype(out[name].dtype))
    for name, factor in factors.items():
        out[name] = (out[name] * factor).astype(out[name].dtype)
    return out
```

```python
from contextlib import ExitStack

import concourse.bass as bass
from concourse import mybir

ALU = mybir.AluOpType
ACT = mybir.ActivationFunctionType
AX_X = mybir.AxisListType.X
F32 = mybir.dt.float32
F32R = mybir.dt.float32r
ds = bass.ds

P = 128
IMGS = 8
RG = P // IMGS
SIDE = 256
D = 256
KC = D // P
ROWS = SIDE // RG
TXT_T = 2
NT = ROWS + TXT_T
TOK = NT * P
POS = TOK // IMGS
GT = 3
NG = NT // GT
GW = GT * P
NE = 8
LN_EPS = 1e-5
BIG = 3.0e38
NGQ, HPG, HD = 4, 4, 16
HQ = HPG * POS
KT = 96
NKT = POS // KT
CW = 384
NCH = NGQ * NKT * (HQ // CW)
NU = NCH // 2
RING = 12
NS = NGQ * HQ // P
STK = 3 * HD
NAV = NGQ * NKT
WCOLS = {0: (9 * KC * P, 9 * KC * P, 9 * D), 1: (10 * KC * P, 10 * KC * P, 10 * D)}


def wait(eng, sem, value):
    if isinstance(value, int) and value <= 0:
        return
    eng.wait_ge(sem, value)


class Own:

    def __init__(self, eng, sem):
        self.eng, self.sem, self.n, self.base = eng, sem, 0, 0

    def __call__(self, ins):
        ins.then_inc(self.sem, 1)
        self.n += 1

    def settle(self):
        self.eng.wait_ge(self.sem, self.base + self.n)

    def loop(self, lo, hi, per, body):
        start = self.base + self.n
        with self.eng.Fori(lo, hi) as i:
            self.base, self.n = start + (i - lo) * per, 0
            body(i)
            assert self.n == per, (self.n, per)
        self.base, self.n = start + (hi - lo) * per, 0


def build(nc, A, out):
    ctx = ExitStack()
    base0 = 16512
    end = 229344
    top = [base0]

    def at(name, shape, dt, off):
        size = 4
        for n in shape[1:]:
            size *= n
        assert off % 32 == 0 and off + size <= end, (name, off, size, end)
        return nc.alloc_sbuf_tensor_at(name, shape, dt, offset=off)

    def keep(name, shape, dt=F32):
        size = 4
        for n in shape[1:]:
            size *= n
        t = at(name, shape, dt, top[0])
        top[0] += (size + 31) // 32 * 32
        return t

    h = keep("h", [P, NT, D])
    xTh = keep("xTh", [P, KC, TOK], F32R)
    xTl = keep("xTl", [P, KC, TOK], F32R)
    ident = keep("ident", [P, P])
    same_img = keep("same_img", [P, P])
    far_mask = keep("far_mask", [P, P])
    ones = keep("ones", [P, P])
    sel16 = keep("sel16", [P, P])
    lt = keep("lt", [P, NE * NE])
    stats = keep("stats", [P, NT, 6])
    mv = keep("mv", [P, NT, 2])
    mt = keep("mt", [P, 4, NT])
    rstd = keep("rstd", [P, NT])
    eps = keep("eps", [P, 1])
    bqk0 = keep("bqk0", [P, 4])
    bv0 = keep("bv0", [P, D])
    bq1 = keep("bq1", [P, 3])
    bo1 = keep("bo1", [P, D])
    cb0 = keep("cb0", [P, NE])
    lb1 = keep("lb1", [P, NE])
    rw = [keep(f"rw{x}", [P, KC, NE]) for x in range(2)]
    rwh = [keep(f"rwh{x}", [P, KC, NE], F32R) for x in range(2)]
    rwl = [keep(f"rwl{x}", [P, KC, NE], F32R) for x in range(2)]
    cmb = keep("cmb", [P, NT, 10])
    R1 = top[0]

    o = [R1]

    def seq(name, shape, dt=F32, cur=o):
        size = 4
        for n in shape[1:]:
            size *= n
        t = at(name, shape, dt, cur[0])
        cur[0] += (size + 31) // 32 * 32
        return t

    NLV = 3
    rows = [ROWS >> (n + 1) for n in range(NLV)]
    cols = [SIDE >> (n + 1) for n in range(NLV)]
    x_in = seq("x_in", [P, ROWS, SIDE])
    lo = [seq(f"lo{n}", [P, 2 * rows[n], cols[n]]) for n in range(NLV)]
    hi = [seq(f"hi{n}", [P, 2 * rows[n], cols[n]]) for n in range(NLV)]
    app = [seq(f"app{n}", [P, rows[n], cols[n]]) for n in range(NLV)]
    det = [seq(f"det{n}", [P, 3, rows[n], cols[n]]) for n in range(NLV)]
    dsc = [seq(f"dsc{n}", [P, rows[n], cols[n]]) for n in range(NLV)]
    sizes = [3 * rows[n] * cols[n] for n in range(NLV)]
    wd = [seq(f"wd{n}", [P, 3, sizes[n]]) for n in range(NLV)]
    wa = seq("wa", [P, rows[2] * cols[2]])
    junk = seq("junk", [P, sizes[0]])
    dots = seq("dots", [P, 10])
    lg = seq("lg", [P, 10])
    lbias = seq("lbias", [P, 10])
    wmx = seq("wmx", [P, NLV])
    wex = seq("wex", [P, 10])
    wsm = seq("wsm", [P, 4])
    wts = seq("wts", [P, 10])

    wb = [base0 + NT * D * 4]
    qkv_raw = seq("qkv_raw", [P, 3, KC, D], cur=wb)
    qkv_h = seq("qkv_h", [P, 3, KC, D], F32R, cur=wb)
    qkv_l = seq("qkv_l", [P, 3, KC, D], F32R, cur=wb)
    assert wb[0] <= base0 + NT * D * 4 + 2 * KC * TOK * 4
    FW = 3 * 10 * D * 4
    wk = [R1 + 3 * FW]
    xwh = seq("xwh", [P, KC, GW], F32R, cur=wk)
    xwl = seq("xwl", [P, KC, GW], F32R, cur=wk)
    xn = seq("xn", [P, GT, D], cur=wk)
    qT = seq("qT", [P, KC, GW], cur=wk)
    km2 = seq("km2", [P, KC, GW], cur=wk)
    qsq = seq("qsq", [P, KC, GW], cur=wk)
    ksq = seq("ksq", [P, KC, GW], cur=wk)
    qs = seq("qs", [P, GW], cur=wk)
    ks = seq("ks", [P, GW], cur=wk)
    v_sb = seq("v_sb", [P, GT, D], cur=wk)
    dm = seq("dm", [P, GT, P], cur=wk)
    Pm = seq("Pm", [P, GT, P], cur=wk)
    PT = seq("PT", [P, GT, P], cur=wk)
    mn = seq("mn", [P, GT], cur=wk)
    hb = seq("hb", [P, GT], cur=wk)
    rs = seq("rs", [P, GT], cur=wk)
    ri = seq("ri", [P, GT], cur=wk)

    W_raw, W_h, W_l = [], [], []
    for L in range(2):
        n = sum(WCOLS[L])
        W_h.append(at(f"W{L}h", [P, n], F32R, R1))
        W_l.append(at(f"W{L}l", [P, n], F32R, R1 + FW))
        W_raw.append(at(f"W{L}raw", [P, n], F32, R1 + 2 * FW))

    def w_part(t, L, part):
        ne = 9 + L
        a = sum(WCOLS[L][:part])
        v = t[:, a:a + WCOLS[L][part]]
        return v.rearrange("p (e k i) -> p e k i", e=ne, k=KC) if part < 2 else v.rearrange("p (e d) -> p e d", e=ne)

    fk = [R1 + 3 * FW]
    xnc = seq("xnc", [P, 2, D], cur=fk)
    lgT = seq("lgT", [NE, TOK], cur=fk)
    sc = seq("sc", [P, NT, NE], cur=fk)
    sv = seq("sv", [P, NT, NE], cur=fk)
    ra = seq("ra", [P, NT, NE, NE], cur=fk)
    rb_ = seq("rb_", [P, NT, NE, NE], cur=fk)
    t1 = seq("t1", [P, NT, NE], cur=fk)
    t2 = seq("t2", [P, NT, NE], cur=fk)
    t3 = seq("t3", [P, NT, NE], cur=fk)
    tot = seq("tot", [P, 2 * NE], cur=fk)
    hk = [fk[0]]
    sg = seq("sg", [P, 2, GW], cur=hk)
    aa = seq("aa", [P, 2, GW], cur=hk)
    ah = seq("ah", [P, 2, GW], F32R, cur=hk)
    al = seq("al", [P, 2, GW], F32R, cur=hk)

    k1 = [R1]
    QS = [seq(f"QS{p}", [STK + 2, NGQ * HQ], F32R, cur=k1) for p in range(2)]
    KS = [seq(f"KS{p}", [STK + 2, NGQ * POS], F32R, cur=k1) for p in range(2)]
    PR = seq("PR", [KT, RING, CW], cur=k1)
    VA = [seq(f"VA{p}", [KT, NKT, NGQ, 32], cur=k1) for p in range(2)]
    qf = seq("qf", [P, 3, POS], cur=k1)
    qh = seq("qh", [P, 3, POS], F32R, cur=k1)
    ql = seq("ql", [P, 3, POS], F32R, cur=k1)
    MX = seq("MX", [P, P], cur=k1)
    Mh = seq("Mh", [NS, P], F32R, cur=k1)
    Ml = seq("Ml", [NS, P], F32R, cur=k1)
    neg1 = seq("neg1", [2, NGQ * POS], cur=k1)
    yr = seq("yr", [P, POS], cur=k1)
    yrec = seq("yrec", [P, POS], cur=k1)
    yT = seq("yT", [P, NGQ, TOK], cur=k1)
    wo = seq("wo", [P, NGQ, D], cur=k1)
    a1raw = seq("a1raw", [P, KC, 3 * P], cur=k1)
    a1h = seq("a1h", [P, KC, 3 * P], F32R, cur=k1)
    a1l = seq("a1l", [P, KC, 3 * P], F32R, cur=k1)
    xn1 = seq("xn1", [P, 2, D], cur=k1)

    PS = ctx.enter_context(nc.psum_tensor("PS", [P, 8, 512], F32))
    scrH = nc.dram_tensor("scrH", (IMGS, P, 3, POS), F32, kind="Internal").ap()
    scrL = nc.dram_tensor("scrL", (IMGS, P, 3, POS), F32, kind="Internal").ap()
    scrM = nc.dram_tensor("scrM", (IMGS, 2, NS, P), F32, kind="Internal").ap()

    S = {}

    def sem(name):
        if name not in S:
            S[name] = ctx.enter_context(nc.semaphore(name))
        return S[name]

    names = """d_x d_txt d_const d_wd d_bias d_qkv d_small d_w0 d_w1 d_a1 d_wo d_out
        dve_own act_own pool_own
        pool_hi dots_ready dots_sum wex_in wex_ready wts_ready dsc_ready img_done
        st_ready0 st_ready1 st_ready2 st_ready3 std_ready0 std_ready1 std_ready2 std_ready3
        rstd_ready0 rstd_ready1 rstd_ready2 rstd_ready3
        const_pool qkv_hi qkv_split rw_split0 rw_split1
        b_xn b_T b_hi b_x b_qk b_dqk b_aqk b_qs b_hb b_v b_vev b_d2 b_dm b_exp b_pt b_ptev b_av b_res
        w_hi0 w_split0 w_hi1 w_split1
        c_scan
        e_kv_const e_a1h e_a1 e_bo
        e_pr e_prev e_split e_out e_in0 e_in1 e_vt e_va e_s e_mx e_mT e_msplit e_mout e_min
        e_st e_exp e_avt e_yr e_sb e_rec e_y
        g_wo g_res""".split()
    for n in names:
        sem(n)
    for c in "cep":
        for n in ("xn", "T", "hi", "lo"):
            sem(f"{c}_{n}")
    for L in range(2):
        for n in ("lg", "lgT", "lgt", "sig", "lraw", "tot", "sum", "cmb", "gu", "silu", "mul", "ah", "al", "dn", "acc"):
            sem(f"f{L}_{n}")
    assert len(S) < 200, len(S)
    s = S
    block = ctx.enter_context(nc.Block())

    def img(t, i):
        return t.rearrange("p (j c) -> p j c", j=NT)[:, :, ds(i * RG, RG)]

    @block.sync
    def _(sp):
        for n in range(2):
            sp.dma_start(x_in[:, n * 8:n * 8 + 8, :], A["x"][:, n * 8:n * 8 + 8, :]).then_inc(s["d_x"], 16)
        sp.dma_start(h[:, ROWS:NT, :], A["txt"]).then_inc(s["d_txt"], 16)
        for n, t in enumerate((ident, same_img, far_mask, sel16)):
            sp.dma_start(t[:, :], A["consts"][:, n, :]).then_inc(s["d_const"], 16)
        sp.dma_start(lt[:, :], A["lt"].broadcast_to([P, NE * NE])).then_inc(s["d_const"], 16)
        sp.dma_start(lbias[:, :], A["lbias"].broadcast_to([P, 10])).then_inc(s["d_bias"], 16)
        sp.dma_start(qkv_raw[:, :, :, :], A["qkv0"]).then_inc(s["d_qkv"], 16)
        sp.dma_start(bqk0[:, :], A["bqk0"]).then_inc(s["d_small"], 16)
        sp.dma_start(bv0[:, :], A["bv0"].broadcast_to([P, D])).then_inc(s["d_small"], 16)
        sp.dma_start(bq1[:, :], A["bq1"]).then_inc(s["d_small"], 16)
        sp.dma_start(bo1[:, :], A["bo1"].broadcast_to([P, D])).then_inc(s["d_small"], 16)
        sp.dma_start(cb0[:, :], A["cb0"].broadcast_to([P, NE])).then_inc(s["d_small"], 16)
        sp.dma_start(lb1[:, :], A["lb1"].broadcast_to([P, NE])).then_inc(s["d_small"], 16)
        for L in range(2):
            sp.dma_start(rw[L][:, :, :], A[f"rw{L}"]).then_inc(s["d_small"], 16)
        sp.wait_ge(s["img_done"], 1)
        sp.dma_start(W_raw[0][:, :], A["w0"]).then_inc(s["d_w0"], 16)
        sp.wait_ge(s["f0_acc"], NG * 9)
        sp.dma_start(a1raw[:, :, :], A["a1"]).then_inc(s["d_a1"], 16)
        sp.dma_start(wo[:, :, :], A["wo1"]).then_inc(s["d_wo"], 16)
        sp.wait_ge(s["e_kv_const"], 1)
        for p in range(2):
            sp.dma_start(KS[p][STK:STK + 2, :].bitcast(F32), neg1[:, :]).then_inc(s["d_wo"], 16)

        def stack_out(i):
            sp.wait_ge(s["e_split"], 2 * (i + 1))
            sp.dma_start(scrH[ds(i, 1)].rearrange("o p m q -> (o p) m q"), qh[:, :, :].bitcast(F32)).then_inc(s["e_out"], 16)
            sp.dma_start(scrL[ds(i, 1)].rearrange("o p m q -> (o p) m q"), ql[:, :, :].bitcast(F32)).then_inc(s["e_out"], 16)

        def stack_in(i, p, m):
            if m == 0:
                sp.wait_ge(s["e_out"], 32 * (i + 1))
            if not (isinstance(i, int) and i < 2):
                sp.wait_ge(s["e_st"], (i - 2) * NU + NU // 2 * (m + 1))
            for n, src in enumerate((scrH, scrH, scrL)):
                sp.dma_start(QS[p][n * HD:n * HD + HD, m * 8 * POS:(m + 1) * 8 * POS].bitcast(F32).rearrange("d (h q) -> d h q", h=8),
                             src[ds(i, 1), :, m, :].rearrange("o (h d) q -> d (o h) q", d=HD)).then_inc(s[f"e_in{m}"], 16)
            for n, src in enumerate((scrH, scrL, scrH)):
                sp.dma_start(KS[p][n * HD:n * HD + HD, m * 2 * POS:(m + 1) * 2 * POS].bitcast(F32).rearrange("d (g q) -> d g q", g=2),
                             src[ds(i, 1), m * 2 * HD:(m + 1) * 2 * HD, 2, :].rearrange("o (g d) q -> d (o g) q", d=HD)).then_inc(s[f"e_in{m}"], 16)

        def max_rows(i, p):
            sp.wait_ge(s["e_msplit"], i + 1)
            for n, src in enumerate((Mh, Ml)):
                sp.dma_start(scrM[ds(i, 1), n].rearrange("o c r -> (o c) r"), src[:, :].bitcast(F32)).then_inc(s["e_mout"], 16)
            sp.wait_ge(s["e_mout"], 32 * (i + 1))
            sp.dma_start(QS[p][STK:STK + 2, :].bitcast(F32), scrM[ds(i, 1)].rearrange("o n c r -> (o n) (c r)")).then_inc(s["e_min"], 16)

        def turn(it, p, pr, sp_, st):
            if pr:
                stack_out(it)
                stack_in(it, p, 0)
            if sp_:
                max_rows(it - 1, 1 - p)
            if pr:
                stack_in(it, p, 1)

        turn(0, 0, True, False, False)
        turn(1, 1, True, True, False)
        turn(2, 0, True, True, True)
        turn(3, 1, True, True, True)
        with sp.Fori(2, 4) as r:
            turn(2 * r, 0, True, True, True)
            turn(2 * r + 1, 1, True, True, True)
        turn(8, 0, False, True, True)
        sp.wait_ge(s["g_wo"], NT)
        sp.dma_start(W_raw[1][:, :], A["w1"]).then_inc(s["d_w1"], 16)
        with sp.Fori(0, NG) as g:
            sp.wait_ge(s["f1_acc"], 10 * (g + 1))
            sp.dma_start(out[:, ds(g * GT, GT), :], h[:, ds(g * GT, GT), :]).then_inc(s["d_out"], 16)
        sp.wait_ge(s["d_out"], 16 * NG)

    @block.gpsimd
    def _(pool):
        own = Own(pool, s["pool_own"])
        nc.gpsimd.memset(ones[:, :], 1.0).then_inc(s["const_pool"], 1)
        nc.gpsimd.memset(eps[:, :], LN_EPS).then_inc(s["const_pool"], 1)
        nc.gpsimd.memset(cmb[:, :, :], 1.0).then_inc(s["const_pool"], 1)
        pool.wait_ge(s["d_x"], 32)
        xv = x_in[:, :, :].rearrange("p r (c t) -> p r c t", t=2)
        own(nc.gpsimd.tensor_tensor(hi[0][:, :, :], xv[:, :, :, 0], xv[:, :, :, 1], ALU.subtract))
        own.settle()
        hv = hi[0][:, :, :].rearrange("p (r t) c -> p r t c", t=2)
        nc.gpsimd.tensor_tensor(det[0][:, 1], hv[:, :, 0, :], hv[:, :, 1, :], ALU.add)
        nc.gpsimd.tensor_tensor(det[0][:, 2], hv[:, :, 0, :], hv[:, :, 1, :], ALU.subtract).then_inc(s["pool_hi"], 1)
        pool.wait_ge(s["qkv_hi"], 1)
        nc.gpsimd.tensor_tensor(qkv_l[:, :, :, :], qkv_raw[:, :, :, :], qkv_h[:, :, :, :].bitcast(F32), ALU.subtract).then_inc(s["qkv_split"], 1)
        pool.wait_ge(s["d_small"], 16 * 8)
        pool.wait_ge(s["qkv_hi"], 2)
        for L in range(2):
            nc.gpsimd.tensor_tensor(rwl[L][:, :, :], rw[L][:, :, :], rwh[L][:, :, :].bitcast(F32), ALU.subtract).then_inc(s["rw_split0"], 1)

        n0 = sum(WCOLS[0]) // NG

        def l0(i):
            pool.wait_ge(s["b_xn"], i + 1)
            for t in range(GT):
                nc.gpsimd.tensor_tensor(h[:, ds(i * GT + t, 1), :].squeeze(1), h[:, ds(i * GT + t, 1), :].squeeze(1), bv0[:, :], ALU.add).then_inc(s["b_hb"], 1)
            pool.wait_ge(s["b_aqk"], i + 1)
            wait(pool, s["b_d2"], i)
            nc.gpsimd.tensor_tensor(qs[:, :], qsq[:, 0], qsq[:, 1], ALU.add)
            nc.gpsimd.tensor_tensor(ks[:, :], ksq[:, 0], ksq[:, 1], ALU.add).then_inc(s["b_qs"], 1)
            pool.wait_ge(s["w_hi0"], i + 1)
            nc.gpsimd.tensor_tensor(W_l[0][:, ds(i * n0, n0)], W_raw[0][:, ds(i * n0, n0)], W_h[0][:, ds(i * n0, n0)].bitcast(F32), ALU.subtract).then_inc(s["w_split0"], 1)

        l0(0)
        with pool.Fori(1, NG) as i:
            l0(i)

        pool.wait_ge(s["f0_acc"], NG * 9)
        nc.gpsimd.memset(neg1[:, :], -1.0).then_inc(s["e_kv_const"], 1)
        nc.gpsimd.memset(MX[:, :], 0.0).then_inc(s["e_kv_const"], 1)
        for p in range(2):
            own(nc.gpsimd.memset(VA[p][:, :, :, HD:32], 0.0))
        own.settle()
        for p in range(2):
            nc.gpsimd.memset(VA[p][:, :, :, HD:HD + 1], 1.0).then_inc(s["e_kv_const"], 1)
        pool.wait_ge(s["e_a1h"], 1)
        nc.gpsimd.tensor_tensor(a1l[:, :, :], a1raw[:, :, :], a1h[:, :, :].bitcast(F32), ALU.subtract).then_inc(s["e_a1"], 1)
        pool.wait_ge(s["e_xn"], NT)
        with pool.Fori(0, NT) as j:
            nc.gpsimd.tensor_tensor(h[:, ds(j, 1), :].squeeze(1), h[:, ds(j, 1), :].squeeze(1), bo1[:, :], ALU.add).then_inc(s["e_bo"], 1)

        def turn(it, pr, st):
            if pr:
                pool.wait_ge(s["e_prev"], 3 * (it + 1))
                wait(pool, s["e_out"], 32 * it)
                nc.gpsimd.tensor_tensor(qh[:, :, :], qf[:, :, :], ones[:, 0:1].unsqueeze(2).broadcast_to([P, 3, POS]), ALU.mult).then_inc(s["e_split"], 1)
                pool.wait_ge(s["e_split"], 2 * it + 1)
                nc.gpsimd.tensor_tensor(ql[:, :, :], qf[:, :, :], qh[:, :, :].bitcast(F32), ALU.subtract).then_inc(s["e_split"], 1)
            if st:
                i = it - 2
                for g in range(NGQ):
                    pool.wait_ge(s["e_rec"], NGQ * i + g + 1)
                    nc.gpsimd.tensor_tensor(img(yT[:, g, :], i), yr[:, :].rearrange("p (j c) -> p j c", j=NT),
                                            yrec[:, :].rearrange("p (j c) -> p j c", j=NT), ALU.mult).then_inc(s["e_y"], 1)

        turn(0, True, False)
        turn(1, True, False)
        with pool.Fori(2, IMGS) as it:
            turn(it, True, True)
        turn(8, False, True)
        turn(9, False, True)
        n1 = sum(WCOLS[1]) // NG
        with pool.Fori(0, NG) as i:
            pool.wait_ge(s["w_hi1"], i + 1)
            nc.gpsimd.tensor_tensor(W_l[1][:, ds(i * n1, n1)], W_raw[1][:, ds(i * n1, n1)], W_h[1][:, ds(i * n1, n1)].bitcast(F32), ALU.subtract).then_inc(s["w_split1"], 1)

    @block.scalar
    def _(act):
        A_ = nc.scalar.activation
        for n in (2, 1, 0):
            for b in range(IMGS):
                act.dma_start(wd[n][b * RG:b * RG + RG, :, :], A[f"wd{n}"]).then_inc(s["d_wd"], 16)
        for b in range(IMGS):
            act.dma_start(wa[b * RG:b * RG + RG, :], A["wa"]).then_inc(s["d_wd"], 16)
        act.wait_ge(s["d_qkv"], 16)
        A_(qkv_h[:, :, :, :], qkv_raw[:, :, :, :], ACT.Copy).then_inc(s["qkv_hi"], 1)
        act.wait_ge(s["d_small"], 16 * 8)
        A_(rwh[0][:, :, :], rw[0][:, :, :], ACT.Copy)
        A_(rwh[1][:, :, :], rw[1][:, :, :], ACT.Copy).then_inc(s["qkv_hi"], 1)
        act.wait_ge(s["wex_in"], 1)
        A_(wex[:, 0:9], wex[:, 0:9], ACT.Exp)
        A_(wex[:, 9:10], lg[:, 9:10], ACT.Exp, scale=-1.0).then_inc(s["wex_ready"], 1)
        act.wait_ge(s["wts_ready"], 1)
        for n in (2, 1, 0):
            c = 3 * (2 - n) + 2
            A_(dsc[n][:, :, :], det[n][:, 2], ACT.Copy, scale=wts[:, c:c + 1]).then_inc(s["dsc_ready"], 1)

        def std(n):
            act.wait_ge(s[f"st_ready{n}"], 1)
            A_(rstd[:, :], mv[:, :, 1], ACT.Sqrt, bias=eps[:, 0:1]).then_inc(s[f"std_ready{n}"], 1)

        act.wait_ge(s["const_pool"], 3)
        std(0)
        n0 = sum(WCOLS[0]) // NG

        def ln_hi(i):
            act.wait_ge(s["b_T"], i + 1)
            wait(act, s["b_v"], i)
            A_(xwh[:, :, 0:2 * P].rearrange("p k (t c) -> p t k c", t=2), PS[:, 4, :].rearrange("p (t k c) -> p t k c", t=2, k=KC), ACT.Copy)
            A_(xwh[:, :, 2 * P:], PS[:, 5, 0:D].rearrange("p (k c) -> p k c", k=KC), ACT.Copy).then_inc(s["b_hi"], 1)

        def l0(i, prev, cur, nxt):
            if cur:
                act.wait_ge(s["b_dqk"], i + 1)
                wait(act, s["b_qs"], i)
                A_(qsq[:, :, :], qT[:, :, :], ACT.Square)
                A_(ksq[:, :, :], km2[:, :, :], ACT.Square, scale=0.5).then_inc(s["b_aqk"], 1)
            if prev:
                act.wait_ge(s["b_pt"], i)
                wait(act, s["b_av"], i - 1)
                A_(PT[:, :, :], PS[:, 7, 0:GW].rearrange("p (t c) -> p t c", t=GT), ACT.Copy).then_inc(s["b_ptev"], 1)
            if nxt:
                ln_hi(i + 1)
            if cur:
                act.wait_ge(s["b_v"], i + 1)
                wait(act, s["b_av"], i)
                A_(v_sb[:, 0:2, :], PS[:, 0, :].rearrange("p (t c) -> p t c", t=2), ACT.Copy)
                A_(v_sb[:, 2, :], PS[:, 1, 0:D], ACT.Copy).then_inc(s["b_vev"], 1)
                act.wait_ge(s["b_dm"], i + 1)
                wait(act, s["b_pt"], i)
                wait(act, s["b_res"], i)
                for t in range(GT):
                    ins = A_(Pm[:, t], dm[:, t], ACT.Exp, bias=hb[:, t:t + 1], scale=-0.5, accum_out=rs[:, t:t + 1])
                ins.then_inc(s["b_exp"], 1)
                if isinstance(i, int) and i == 0:
                    act.wait_ge(s["d_w0"], 16)
                A_(W_h[0][:, ds(i * n0, n0)], W_raw[0][:, ds(i * n0, n0)], ACT.Copy).then_inc(s["w_hi0"], 1)

        ln_hi(0)
        l0(0, False, True, True)
        with act.Fori(1, NG - 1) as i:
            l0(i, True, True, True)
        l0(NG - 1, True, True, False)
        l0(NG, True, False, False)

        def prep(c):
            def two(j):
                for u in range(2):
                    act.wait_ge(s[f"{c}_T"], j + u + 1)
                    A_(xTh[:, :, ds((j + u) * P, P)], PS[:, u, 0:D].rearrange("p (k c) -> p k c", k=KC), ACT.Copy).then_inc(s[f"{c}_hi"], 1)
            with act.Fori(0, NT // 2) as jj:
                two(jj * 2)

        def logits(L):
            def one(g, b):
                act.wait_ge(s[f"f{L}_lg"], g + 1)
                A_(lgT[:, ds(g * GW, GW)], PS[0:NE, 2 + b, 0:GW], ACT.Copy).then_inc(s[f"f{L}_lgT"], 1)
            with act.Fori(0, NG // 2) as r:
                one(2 * r, 0)
                one(2 * r + 1, 1)
            if L == 0:
                act.wait_ge(s["f0_lgt"], 1)
                A_(sc[:, :, :], PS[:, 4, 0:NT * NE].rearrange("p (j e) -> p j e", e=NE), ACT.Sigmoid).then_inc(s["f0_sig"], 1)
            else:
                act.wait_ge(s["f1_lraw"], 1)
                A_(sc[:, :, :], sc[:, :, :], ACT.Sigmoid).then_inc(s["f1_sig"], 1)

        def experts(L, gu):
            ne = 9 + L
            def body(r):
                for k in range(gu * ne):
                    n = r * (gu * ne) + k
                    b = k % 2
                    act.wait_ge(s[f"f{L}_gu"], n + 1)
                    A_(sg[:, b], PS[:, b, 0:GW], ACT.Silu).then_inc(s[f"f{L}_silu"], 1)
                    act.wait_ge(s[f"f{L}_mul"], n + 1)
                    wait(act, s[f"f{L}_dn"], n - 1)
                    A_(ah[:, b], aa[:, b], ACT.Copy).then_inc(s[f"f{L}_ah"], 1)
            turns = NG // gu
            body(0)
            with act.Fori(1, turns) as r:
                body(r)

        std(1)
        prep("c")
        logits(0)
        experts(0, 2)
        std(2)
        act.wait_ge(s["d_a1"], 16)
        A_(a1h[:, :, :], a1raw[:, :, :], ACT.Copy).then_inc(s["e_a1h"], 1)
        prep("e")

        def turn(it, p, pr, sp_, st):
            i = it - 2
            for U in range(NU):
                if st:
                    n = i * NU + U
                    act.wait_ge(s["e_st"], n + 1)
                    old = (2 * U + 1 - RING) // 3
                    wait(act, s["e_avt"], i * NAV + old + 1)
                    c0 = (2 * U) % RING
                    b = 2 * (U % 2)
                    A_(PR[:, c0:c0 + 2, :], PS[0:KT, b:b + 2, 0:CW], ACT.Exp).then_inc(s["e_exp"], 1)
                    if U in YR_AT:
                        y_raw(i, YR_AT.index(U))
                if sp_ and U == VT_U:
                    act.wait_ge(s["e_vt"], it)
                    wait(act, s["e_avt"], (it - 2) * NAV)
                    for kt in range(NKT):
                        ins = A_(VA[1 - p][:, kt, :, 0:HD], PS[0:KT, 7, kt * P + 64:kt * P + P].rearrange("p (g d) -> p g d", g=NGQ), ACT.Copy)
                    ins.then_inc(s["e_va"], 1)
            if st:
                y_raw(i, NGQ - 1)

        def y_raw(i, g):
            act.wait_ge(s["e_avt"], NAV * i + NKT * (g + 1))
            wait(act, s["e_y"], NGQ * i + g)
            A_(yr[:, :], PS[:, 6, 0:POS], ACT.Copy).then_inc(s["e_yr"], 1)

        act.wait_ge(s["e_kv_const"], 4)
        turn(0, 0, True, False, False)
        turn(1, 1, True, True, False)
        turn(2, 0, True, True, True)
        turn(3, 1, True, True, True)
        with act.Fori(2, 4) as r:
            turn(2 * r, 0, True, True, True)
            turn(2 * r + 1, 1, True, True, True)
        turn(8, 0, False, True, True)
        turn(9, 1, False, False, True)
        n1 = sum(WCOLS[1]) // NG
        act.wait_ge(s["d_w1"], 16)
        with act.Fori(0, NG) as i:
            A_(W_h[1][:, ds(i * n1, n1)], W_raw[1][:, ds(i * n1, n1)], ACT.Copy).then_inc(s["w_hi1"], 1)
        std(3)
        prep("p")
        logits(1)
        experts(1, 3)

    @block.vector
    def _(dve):
        V = nc.vector
        own = Own(dve, s["dve_own"])

        def moments():
            me, mo = stats[:, :, 1], stats[:, :, 4]
            own(V.tensor_tensor(mt[:, 0], me, mo, ALU.add))
            own(V.tensor_tensor(mt[:, 1], me, mo, ALU.subtract))
            own(V.tensor_tensor(mt[:, 2], stats[:, :, 2], stats[:, :, 5], ALU.add))
            own.settle()
            own(V.tensor_scalar(mv[:, :, 0], mt[:, 0], 0.5, None, ALU.mult))
            own(V.tensor_tensor(mt[:, 3], mt[:, 1], mt[:, 1], ALU.mult))
            own.settle()
            own(V.tensor_scalar(mt[:, 0], mt[:, 3], 0.25, None, ALU.mult))
            own.settle()
            own(V.scalar_tensor_tensor(out=mv[:, :, 1], in0=mt[:, 2], scalar=1.0 / D, in1=mt[:, 0], op0=ALU.mult, op1=ALU.add))
            own.settle()

        dve.wait_ge(s["d_x"], 32)
        src = x_in[:, :, :]
        for n in range(NLV):
            sv4 = src.rearrange("p r (c t) -> p r c t", t=2)
            own(V.tensor_tensor(lo[n][:, :, :], sv4[:, :, :, 0], sv4[:, :, :, 1], ALU.add))
            if n:
                own(V.tensor_tensor(hi[n][:, :, :], sv4[:, :, :, 0], sv4[:, :, :, 1], ALU.subtract))
            own.settle()
            lv = lo[n][:, :, :].rearrange("p (r t) c -> p r t c", t=2)
            hv = hi[n][:, :, :].rearrange("p (r t) c -> p r t c", t=2)
            own(V.tensor_tensor(app[n][:, :, :], lv[:, :, 0, :], lv[:, :, 1, :], ALU.add))
            own(V.tensor_tensor(det[n][:, 0], lv[:, :, 0, :], lv[:, :, 1, :], ALU.subtract))
            if n:
                own(V.tensor_tensor(det[n][:, 1], hv[:, :, 0, :], hv[:, :, 1, :], ALU.add))
                own(V.tensor_tensor(det[n][:, 2], hv[:, :, 0, :], hv[:, :, 1, :], ALU.subtract))
            own.settle()
            src = app[n][:, :, :]
        dve.wait_ge(s["pool_hi"], 1)
        dve.wait_ge(s["d_wd"], 16 * 4 * IMGS)
        own(V.tensor_tensor_reduce(junk[:, 0:rows[2] * cols[2]], app[2][:, :, :].rearrange("p r c -> p (r c)"), wa[:, :], 1.0, 0.0, ALU.mult, ALU.add, dots[:, 9:10]))
        for n in (2, 1, 0):
            for k in range(3):
                own.settle()
                own(V.tensor_tensor_reduce(junk[:, 0:sizes[n]], det[n][:, :, :, :].rearrange("p b r c -> p (b r c)"), wd[n][:, k, :], 1.0, 0.0,
                                           ALU.mult, ALU.add, dots[:, 3 * (2 - n) + k:3 * (2 - n) + k + 1]))
        own.settle()
        V.tensor_copy(lg[:, :], dots[:, :]).then_inc(s["dots_ready"], 1)
        dve.wait_ge(s["dots_sum"], 1)
        dve.wait_ge(s["d_bias"], 16)
        for n, (a, b, f) in enumerate(((0, 3, 0.125), (3, 6, 0.25), (6, 9, 0.5), (9, 10, 0.125))):
            own(V.scalar_tensor_tensor(out=lg[:, a:b], in0=PS[:, 0, a:b], scalar=f, in1=lbias[:, a:b], op0=ALU.mult, op1=ALU.add))
        own.settle()
        l3 = lg[:, 0:9].rearrange("p (n k) -> p n k", n=3)
        e3 = wex[:, 0:9].rearrange("p (n k) -> p n k", n=3)
        own(V.tensor_reduce(wmx[:, :], l3, AX_X, ALU.max))
        own.settle()
        V.tensor_tensor(e3, l3, wmx[:, :].unsqueeze(2).broadcast_to([P, 3, 3]), ALU.subtract).then_inc(s["wex_in"], 1)
        dve.wait_ge(s["wex_ready"], 1)
        own(V.tensor_reduce(wsm[:, 0:3], e3, AX_X, ALU.add))
        own(V.tensor_scalar(wsm[:, 3:4], wex[:, 9:10], 1.0, None, ALU.add))
        own.settle()
        own(V.reciprocal(wsm[:, :], wsm[:, :]))
        own.settle()
        for n, f in enumerate((1 / 64, 1 / 16, 1 / 4)):
            own(V.tensor_scalar(wts[:, 3 * n:3 * n + 3], wex[:, 3 * n:3 * n + 3], wsm[:, n:n + 1], f, ALU.mult, ALU.mult))
        own(V.tensor_scalar(wts[:, 9:10], wsm[:, 3:4], 1 / 64, None, ALU.mult))
        own.settle()
        V.tensor_scalar(app[2][:, :, :], app[2][:, :, :], wts[:, 9:10], None, ALU.mult).then_inc(s["wts_ready"], 1)
        dve.wait_ge(s["wts_ready"], 1)
        for n in (2, 1, 0):
            c = 3 * (2 - n)
            u = app[n][:, :, :]
            lv = lo[n][:, :, :].rearrange("p (r t) c -> p r t c", t=2)
            hv = hi[n][:, :, :].rearrange("p (r t) c -> p r t c", t=2)
            own(V.scalar_tensor_tensor(out=lv[:, :, 0, :], in0=det[n][:, 0], scalar=wts[:, c:c + 1], in1=u, op0=ALU.mult, op1=ALU.add))
            own(V.scalar_tensor_tensor(out=lv[:, :, 1, :], in0=det[n][:, 0], scalar=wts[:, c:c + 1], in1=u, op0=ALU.mult, op1=ALU.subtract, reverse1=True))
            dve.wait_ge(s["dsc_ready"], 3 - n)
            own(V.scalar_tensor_tensor(out=hv[:, :, 0, :], in0=det[n][:, 1], scalar=wts[:, c + 1:c + 2], in1=dsc[n][:, :, :], op0=ALU.mult, op1=ALU.add))
            own(V.scalar_tensor_tensor(out=hv[:, :, 1, :], in0=det[n][:, 1], scalar=wts[:, c + 1:c + 2], in1=dsc[n][:, :, :], op0=ALU.mult, op1=ALU.subtract))
            own.settle()
            dst = app[n - 1][:, :, :] if n else h[:, 0:ROWS, :]
            dv = dst.rearrange("p r (c t) -> p r c t", t=2)
            own(V.tensor_tensor(dv[:, :, :, 0], lo[n][:, :, :], hi[n][:, :, :], ALU.add))
            own(V.tensor_tensor(dv[:, :, :, 1], lo[n][:, :, :], hi[n][:, :, :], ALU.subtract))
            own.settle()
        dve.sem_inc(s["img_done"], 1)
        dve.wait_ge(s["d_txt"], 16)
        with dve.Fori(0, NT) as j:
            V.bn_stats(stats[:, ds(j, 1), :].squeeze(1), h[:, ds(j, 1), :].squeeze(1)).then_inc(s["c_scan"], 1)
        dve.wait_ge(s["c_scan"], NT)
        moments()
        dve.sem_inc(s["st_ready0"], 1)

        def rstd_(n):
            dve.wait_ge(s[f"std_ready{n}"], 1)
            V.reciprocal(rstd[:, :], rstd[:, :]).then_inc(s[f"rstd_ready{n}"], 1)
            dve.wait_ge(s[f"rstd_ready{n}"], 1)

        def normalise(dst, j):
            return V.tensor_scalar(dst, h[:, ds(j, 1), :].squeeze(1), mv[:, ds(j, 1), 0:1].squeeze(1),
                                   rstd[:, ds(j, 1)], ALU.subtract, ALU.mult)

        def xn_group(i):
            wait(dve, s["b_T"], i)
            for t in range(GT):
                ins = normalise(xn[:, t], i * GT + t)
            ins.then_inc(s["b_xn"], 1)

        def ln_lo(i):
            dve.wait_ge(s["b_hi"], i + 1)
            V.tensor_tensor(xwl[:, :, 0:2 * P].rearrange("p k (t c) -> p t k c", t=2), PS[:, 4, :].rearrange("p (t k c) -> p t k c", t=2, k=KC),
                            xwh[:, :, 0:2 * P].rearrange("p k (t c) -> p t k c", t=2).bitcast(F32), ALU.subtract)
            V.tensor_tensor(xwl[:, :, 2 * P:], PS[:, 5, 0:D].rearrange("p (k c) -> p k c", k=KC),
                            xwh[:, :, 2 * P:].bitcast(F32), ALU.subtract).then_inc(s["b_x"], 1)

        def l0(i, prev, cur, nxt):
            if nxt:
                xn_group(i + 1)
            if cur:
                dve.wait_ge(s["b_qk"], i + 1)
                wait(dve, s["b_d2"], i)
                for m in range(2):
                    V.tensor_scalar(qT[:, m], PS[:, m, 0:GW], bqk0[:, m:m + 1], None, ALU.add)
                for m in range(2):
                    ins = V.tensor_scalar(km2[:, m], PS[:, 2 + m, 0:GW], bqk0[:, 2 + m:3 + m], -2.0, ALU.add, ALU.mult)
                ins.then_inc(s["b_dqk"], 1)
            if nxt:
                ln_lo(i + 1)
            if prev:
                dve.wait_ge(s["b_exp"], i)
                own(V.reciprocal(ri[:, :], rs[:, :]))
                own.settle()
                dve.wait_ge(s["b_av"], i)
                dve.wait_ge(s["b_hb"], GT * i)
                for t in range(GT):
                    j = (i - 1) * GT + t
                    hj = h[:, ds(j, 1), :].squeeze(1)
                    own(V.scalar_tensor_tensor(out=hj, in0=PS[:, 2 + t // 2, (t % 2) * D:(t % 2) * D + D], scalar=ri[:, t:t + 1], in1=hj, op0=ALU.mult, op1=ALU.add))
                own.settle()
                dve.sem_inc(s["b_res"], 1)
                for t in range(GT):
                    j = (i - 1) * GT + t
                    own(V.bn_stats(stats[:, ds(j, 1), :].squeeze(1), h[:, ds(j, 1), :].squeeze(1)))
            if cur:
                dve.wait_ge(s["b_d2"], i + 1)
                wait(dve, s["b_exp"], i)
                for t in range(GT):
                    own(V.scalar_tensor_tensor(out=dm[:, t], in0=PS[:, 6, t * P:t * P + P], scalar=0.0, in1=far_mask[:, :], op0=ALU.max, op1=ALU.add))
                own.settle()
                own(V.tensor_reduce(mn[:, :], dm[:, :, :], AX_X, ALU.min))
                own.settle()
                V.tensor_scalar(hb[:, :], mn[:, :], 0.5, None, ALU.mult).then_inc(s["b_dm"], 1)

        rstd_(0)
        dve.wait_ge(s["d_small"], 16 * 8)
        dve.wait_ge(s["d_const"], 16 * 5)
        xn_group(0)
        ln_lo(0)
        l0(0, False, True, True)
        own.loop(1, NG - 1, 1 + 3 * GT + 1, lambda i: l0(i, True, True, True))
        l0(NG - 1, True, True, False)
        l0(NG, True, False, False)
        own.settle()
        moments()
        dve.sem_inc(s["st_ready1"], 1)

        def prep(c, n, buf):
            rstd_(n)
            def xn_(j, u):
                normalise(buf[:, u], j).then_inc(s[f"{c}_xn"], 1)

            def lo_(j, u):
                dve.wait_ge(s[f"{c}_hi"], j + 1)
                V.tensor_tensor(xTl[:, :, ds(j * P, P)], PS[:, u, 0:D].rearrange("p (k c) -> p k c", k=KC),
                                xTh[:, :, ds(j * P, P)].bitcast(F32), ALU.subtract).then_inc(s[f"{c}_lo"], 1)

            xn_(0, 0)
            xn_(1, 1)
            with dve.Fori(0, NT // 2 - 1) as r:
                for u in range(2):
                    lo_(2 * r + u, u)
                    xn_(2 * r + u + 2, u)
            lo_(NT - 2, 0)
            lo_(NT - 1, 1)

        def routing(L):
            s8 = [P, NT, NE, NE]
            if L == 0:
                dve.wait_ge(s["f0_sig"], 1)
                own(V.tensor_tensor(sv[:, :, :], sc[:, :, :], cb0[:, :].unsqueeze(1).broadcast_to([P, NT, NE]), ALU.add))
                own.settle()
                pr = sv[:, :, :].rearrange("p j (q t) -> p j q t", t=2)
                hiP, loP = t1[:, :, 0:4], t2[:, :, 0:4]
                own(V.tensor_tensor(hiP, pr[:, :, :, 0], pr[:, :, :, 1], ALU.max))
                own(V.tensor_tensor(loP, pr[:, :, :, 0], pr[:, :, :, 1], ALU.min))
                own.settle()
                hp = hiP.rearrange("p j (g t) -> p j g t", t=2)
                lp = loP.rearrange("p j (g t) -> p j g t", t=2)
                own(V.tensor_tensor(t3[:, :, 0:2], hp[:, :, :, 0], hp[:, :, :, 1], ALU.max))
                own(V.tensor_tensor(t3[:, :, 2:4], hp[:, :, :, 0], hp[:, :, :, 1], ALU.min))
                own(V.tensor_tensor(t3[:, :, 4:6], lp[:, :, :, 0], lp[:, :, :, 1], ALU.max))
                own.settle()
                own(V.tensor_tensor(t3[:, :, 6:8], t3[:, :, 2:4], t3[:, :, 4:6], ALU.max))
                own.settle()
                own(V.tensor_tensor(t1[:, :, 4:6], t3[:, :, 0:2], t3[:, :, 6:8], ALU.add))
                own.settle()
                own(V.tensor_tensor(t2[:, :, 4:5], t1[:, :, 4:5], t1[:, :, 5:6], ALU.is_ge))
                own(V.tensor_tensor(t2[:, :, 5:6], t1[:, :, 4:5], t1[:, :, 5:6], ALU.is_lt))
                own.settle()
                own(V.tensor_tensor(sv[:, :, :].rearrange("p j (g q) -> p j g q", g=2), sv[:, :, :].rearrange("p j (g q) -> p j g q", g=2),
                                    t2[:, :, 4:6].unsqueeze(3).broadcast_to([P, NT, 2, 4]), ALU.mult))
                own.settle()
                key = sv
            else:
                dve.wait_ge(s["f1_lgt"], 1)
                V.tensor_tensor(sc[:, :, :], PS[:, 4, 0:NT * NE].rearrange("p (j e) -> p j e", e=NE),
                                lb1[:, :].unsqueeze(1).broadcast_to([P, NT, NE]), ALU.add).then_inc(s["f1_lraw"], 1)
                dve.wait_ge(s["f1_sig"], 1)
                key = sc
            vf = key[:, :, :].unsqueeze(2).broadcast_to(s8)
            ve = key[:, :, :].unsqueeze(3).broadcast_to(s8)
            own(V.tensor_tensor(ra[:, :, :, :], vf, ve, ALU.is_equal))
            own(V.tensor_tensor(rb_[:, :, :, :], vf, ve, ALU.is_gt))
            own.settle()
            own(V.tensor_tensor(ra[:, :, :, :].rearrange("p j e f -> p j (e f)"), ra[:, :, :, :].rearrange("p j e f -> p j (e f)"),
                                lt[:, :].unsqueeze(1).broadcast_to([P, NT, NE * NE]), ALU.mult))
            own.settle()
            own(V.tensor_tensor(ra[:, :, :, :], ra[:, :, :, :], rb_[:, :, :, :], ALU.add))
            own.settle()
            own(V.tensor_reduce(t1[:, :, :], ra[:, :, :, :], AX_X, ALU.add))
            own.settle()
            own(V.tensor_scalar(t2[:, :, :], t1[:, :, :], 1.5, None, ALU.is_lt))
            own.settle()
            own(V.tensor_tensor(t3[:, :, :], t2[:, :, :], sc[:, :, :], ALU.mult))
            own.settle()
            own(V.tensor_reduce(t1[:, :, 0:1].squeeze(2), t3[:, :, :], AX_X, ALU.add))
            own.settle()
            own(V.tensor_scalar(t1[:, :, 1:2].squeeze(2), t1[:, :, 0:1].squeeze(2), (1e-20, 1e-8)[L], None, ALU.add))
            own.settle()
            own(V.reciprocal(t1[:, :, 2:3].squeeze(2), t1[:, :, 1:2].squeeze(2)))
            own.settle()
            rcp = t1[:, :, 2:3].broadcast_to([P, NT, NE])
            if L == 0:
                own(V.tensor_tensor(cmb[:, :, 0:NE], t3[:, :, :], rcp, ALU.mult))
                own.settle()
                return
            own(V.tensor_tensor(sv[:, :, :], t3[:, :, :], rcp, ALU.mult))
            own.settle()
            own(V.tensor_reduce(tot[:, 0:NE], t2[:, :, :].rearrange("p j e -> p e j"), AX_X, ALU.add))
            own(V.tensor_reduce(tot[:, NE:2 * NE], sv[:, :, :].rearrange("p j e -> p e j"), AX_X, ALU.add))
            own.settle()
            dve.sem_inc(s["f1_tot"], 1)
            dve.wait_ge(s["f1_sum"], 1)
            own(V.tensor_scalar(t1[:, 0, :], PS[:, 5, 0:NE], 1.0, None, ALU.max))
            own.settle()
            own(V.reciprocal(t1[:, 1, :], t1[:, 0, :]))
            own.settle()
            own(V.tensor_tensor(t1[:, 2, :], PS[:, 5, NE:2 * NE], t1[:, 1, :], ALU.mult))
            own.settle()
            own(V.tensor_tensor(cmb[:, :, 0:NE], t2[:, :, :], t1[:, 2:3, :].broadcast_to([P, NT, NE]), ALU.mult))
            own.settle()

        def experts(L, gu):
            ne = 9 + L
            per = gu * ne

            def gated(n, k):
                b = k % 2
                dve.wait_ge(s[f"f{L}_silu"], n + 1)
                wait(dve, s[f"f{L}_ah"], n - 1)
                V.tensor_tensor(aa[:, b], sg[:, b], PS[:, 2 + b, 0:GW], ALU.mult).then_inc(s[f"f{L}_mul"], 1)

            def low(n, k):
                b = k % 2
                dve.wait_ge(s[f"f{L}_ah"], n + 1)
                wait(dve, s[f"f{L}_dn"], n - 1)
                V.tensor_tensor(al[:, b], aa[:, b], ah[:, b].bitcast(F32), ALU.subtract).then_inc(s[f"f{L}_al"], 1)

            def accumulate(n, g, e, k):
                b = 4 + 2 * (k % 2)
                dve.wait_ge(s[f"f{L}_dn"], n + 1)
                wait(dve, s[f"f{L}_acc"], n)
                for t in range(GT):
                    hj = h[:, ds(g * GT + t, 1), :].squeeze(1)
                    ins = V.scalar_tensor_tensor(out=hj, in0=PS[:, b + t // 2, (t % 2) * D:(t % 2) * D + D],
                                                 scalar=cmb[:, ds(g * GT + t, 1), e:e + 1].squeeze(1), in1=hj, op0=ALU.mult, op1=ALU.add)
                ins.then_inc(s[f"f{L}_acc"], 1)

            def body(r, first=False):
                for k in range(per):
                    n = r * per + k
                    gated(n, k)
                    if not first or k >= 2:
                        m = n - 2
                        kk = (k - 2) % per
                        g = (r * gu + (k - 2) // ne)
                        accumulate(m, g, (k - 2) % ne, kk)
                    low(n, k)
            assert per % 2 == 0
            body(0, True)
            with dve.Fori(1, NG // gu) as r:
                body(r)
            for k in (per, per + 1):
                n = (NG // gu - 1) * per + k
                accumulate(n - 2, NG - 1, (k - 2) % ne, k - 2)
            dve.wait_ge(s[f"f{L}_acc"], NG * ne)

        def all_stats(n, c):
            own.loop(0, NT, 1, lambda j: own(V.bn_stats(stats[:, ds(j, 1), :].squeeze(1), h[:, ds(j, 1), :].squeeze(1))))
            own.settle()
            moments()
            dve.sem_inc(s[f"st_ready{n}"], 1)

        prep("c", 1, xnc)
        routing(0)
        experts(0, 2)
        all_stats(2, "e")
        prep("e", 2, xn1)

        def turn(it, pr, sp_, st):
            done = 0
            for U in range(NU):
                if pr and U in PR_U:
                    m = PR_U.index(U)
                    dve.wait_ge(s["e_pr"], 3 * it + m + 1)
                    wait(dve, s["e_split"], 2 * it)
                    if m == 2:
                        wait(dve, s["e_vt"], it)
                    if m == 2:
                        ins = V.tensor_scalar(qf[:, m], PS[:, 7, 0:POS], bq1[:, m:m + 1], None, ALU.add)
                    else:
                        ins = V.tensor_scalar(qf[:, m], PS[:, 7, 0:POS], bq1[:, m:m + 1], 0.25, ALU.add, ALU.mult)
                    ins.then_inc(s["e_prev"], 1)
                if sp_:
                    i = it - 1
                    for c in range(done, S_UPTO[U]):
                        dve.wait_ge(s["e_s"], NS * i + c + 1)
                        if c == 0:
                            wait(dve, s["e_mT"], i)
                        V.tensor_reduce(MX[:, c:c + 1], PS[:, 4 + c % 2, 0:POS], AX_X, ALU.max).then_inc(s["e_mx"], 1)
                    done = S_UPTO[U]
                    if U == MT_U:
                        dve.wait_ge(s["e_mT"], i + 1)
                        wait(dve, s["e_mout"], 32 * i)
                        own(V.tensor_copy(Mh[:, :], PS[0:NS, 7, 0:P]))
                        own.settle()
                        V.tensor_tensor(Ml[:, :], PS[0:NS, 7, 0:P], Mh[:, :].bitcast(F32), ALU.subtract).then_inc(s["e_msplit"], 1)
                if st and U in SB_AT:
                    y_rec(it - 2, SB_AT.index(U))
            if st:
                y_rec(it - 2, NGQ - 1)

        def y_rec(i, g):
            dve.wait_ge(s["e_sb"], NGQ * i + g + 1)
            wait(dve, s["e_y"], NGQ * i + g)
            V.reciprocal(yrec[:, :], PS[:, 7, 0:POS]).then_inc(s["e_rec"], 1)

        dve.wait_ge(s["e_kv_const"], 4)
        turn(0, True, False, False)
        turn(1, True, True, False)
        turn(2, True, True, True)
        turn(3, True, True, True)
        own.loop(2, 4, 2, lambda r: [turn(2 * r + x, True, True, True) for x in range(2)])
        turn(8, False, True, True)
        turn(9, False, False, True)
        dve.wait_ge(s["e_bo"], NT)
        for j in range(NT):
            dve.wait_ge(s["g_wo"], j + 1)
            V.tensor_tensor(h[:, j, :], PS[:, j % 4, 0:D], h[:, j, :], ALU.add).then_inc(s["g_res"], 1)
        dve.wait_ge(s["g_res"], NT)
        all_stats(3, "p")
        prep("p", 3, xnc)
        routing(1)
        experts(1, 3)

    @block.tensor
    def _(pe):
        M = nc.tensor.matmul

        def split3(out_, pairs, start=True, stop=True):
            n = len(pairs)
            for c, (wh, wl, xh, xl) in enumerate(pairs):
                M(out_, wh, xh, start=(start and c == 0), stop=False)
                M(out_, wl, xh, start=False, stop=False)
                ins = M(out_, wh, xl, start=False, stop=(stop and c == n - 1))
            return ins

        pe.wait_ge(s["dots_ready"], 1)
        pe.wait_ge(s["d_const"], 16 * 5)
        M(PS[:, 0, 0:10], same_img[:, :], lg[:, :], start=True, stop=True).then_inc(s["dots_sum"], 1)

        def transposes(i):
            pe.wait_ge(s["b_xn"], i + 1)
            wait(pe, s["b_x"], i)
            for t in range(GT):
                for k in range(KC):
                    c = (t % 2) * D + k * P
                    ins = nc.tensor.transpose(PS[:, 4 + t // 2, c:c + P], xn[:, t, k * P:k * P + P], ident[:, :])
            ins.then_inc(s["b_T"], 1)

        def l0(i, prev, cur, nxt):
            if cur:
                pe.wait_ge(s["b_x"], i + 1)
                wait(pe, s["b_vev"], i)
                wait(pe, s["b_res"], i - 1)
                for m in range(4):
                    c = (m % 2) * P
                    if m == 2:
                        wait(pe, s["b_res"], i - 1)
                    ins = split3(PS[:, m, 0:GW], [(qkv_h[:, m // 2, k, c:c + P], qkv_l[:, m // 2, k, c:c + P], xwh[:, k], xwl[:, k]) for k in range(KC)])
                ins.then_inc(s["b_qk"], 1)
            if prev:
                pe.wait_ge(s["b_exp"], i)
                for t in range(GT):
                    ins = nc.tensor.transpose(PS[:, 7, t * P:t * P + P], Pm[:, t], ident[:, :])
                ins.then_inc(s["b_pt"], 1)
            if cur:
                pe.wait_ge(s["b_dqk"], i + 1)
                for t in range(GT):
                    ins = split3(PS[:, t // 2, (t % 2) * D:(t % 2) * D + D],
                                 [(xwh[:, k, t * P:t * P + P], xwl[:, k, t * P:t * P + P], qkv_h[:, 2, k], qkv_l[:, 2, k]) for k in range(KC)])
                ins.then_inc(s["b_v"], 1)
            if nxt:
                transposes(i + 1)
            if prev:
                pe.wait_ge(s["b_ptev"], i)
                for t in range(GT):
                    ins = M(PS[:, 2 + t // 2, (t % 2) * D:(t % 2) * D + D], PT[:, t], v_sb[:, t], start=True, stop=True)
                ins.then_inc(s["b_av"], 1)
            if cur:
                pe.wait_ge(s["b_qs"], i + 1)
                wait(pe, s["b_dm"], i)
                for t in range(GT):
                    o_ = PS[:, 6, t * P:t * P + P]
                    c = slice(t * P, t * P + P)
                    M(o_, ones[:, :], ks[:, c], start=True, stop=False)
                    M(o_, qs[:, c], ones[:, :], start=False, stop=False)
                    M(o_, qT[:, 0, c], km2[:, 0, c], start=False, stop=False)
                    ins = M(o_, qT[:, 1, c], km2[:, 1, c], start=False, stop=True)
                ins.then_inc(s["b_d2"], 1)

        pe.wait_ge(s["qkv_split"], 1)
        pe.wait_ge(s["const_pool"], 3)
        transposes(0)
        l0(0, False, True, True)
        l0(1, True, True, True)
        with pe.Fori(2, NG - 1) as i:
            l0(i, True, True, True)
        l0(NG - 1, True, True, False)
        l0(NG, True, False, False)

        def prep(c, buf):
            def one(j, u):
                pe.wait_ge(s[f"{c}_xn"], j + 1)
                wait(pe, s[f"{c}_lo"], j - 1)
                for k in range(KC):
                    ins = nc.tensor.transpose(PS[:, u, k * P:k * P + P], buf[:, u, k * P:k * P + P], ident[:, :])
                ins.then_inc(s[f"{c}_T"], 1)
            one(0, 0)
            one(1, 1)
            with pe.Fori(1, NT // 2) as r:
                one(2 * r, 0)
                one(2 * r + 1, 1)

        def logits(L, c):
            pe.wait_ge(s[f"{c}_lo"], NT)
            pe.wait_ge(s[f"{c}_hi"], NT)
            pe.wait_ge(s["rw_split0"], 2)

            def one(g, b):
                wait(pe, s[f"f{L}_lgT"], g - 1)
                split3(PS[0:NE, 2 + b, 0:GW], [(rwh[L][:, k], rwl[L][:, k], xTh[:, k, ds(g * GW, GW)], xTl[:, k, ds(g * GW, GW)]) for k in range(KC)])\
                    .then_inc(s[f"f{L}_lg"], 1)
            one(0, 0)
            one(1, 1)
            with pe.Fori(1, NG // 2) as r:
                one(2 * r, 0)
                one(2 * r + 1, 1)
            pe.wait_ge(s[f"f{L}_lgT"], NG)
            for j in range(NT):
                ins = nc.tensor.transpose(PS[:, 4, j * NE:j * NE + NE], lgT[:, j * P:j * P + P], ident[0:NE, 0:NE])
            ins.then_inc(s[f"f{L}_lgt"], 1)
            if L == 1:
                pe.wait_ge(s["f1_tot"], 1)
                M(PS[:, 5, 0:2 * NE], ones[:, :], tot[:, :], start=True, stop=True).then_inc(s["f1_sum"], 1)

        def experts(L, gu):
            ne = 9 + L
            per = gu * ne
            Gh, Gl = w_part(W_h[L], L, 0), w_part(W_l[L], L, 0)
            Uh, Ul = w_part(W_h[L], L, 1), w_part(W_l[L], L, 1)
            Dh, Dl = w_part(W_h[L], L, 2), w_part(W_l[L], L, 2)

            def gate_up(n, g, e, k):
                b = k % 2
                wait(pe, s[f"f{L}_mul"], n - 1)
                xs = [(xTh[:, c, ds(g * GW, GW)], xTl[:, c, ds(g * GW, GW)]) for c in range(KC)]
                split3(PS[:, b, 0:GW], [(Gh[:, e, c], Gl[:, e, c], *xs[c]) for c in range(KC)])
                split3(PS[:, 2 + b, 0:GW], [(Uh[:, e, c], Ul[:, e, c], *xs[c]) for c in range(KC)]).then_inc(s[f"f{L}_gu"], 1)

            def down(n, e, k):
                b = k % 2
                pe.wait_ge(s[f"f{L}_al"], n + 1)
                wait(pe, s[f"f{L}_acc"], n - 1)
                for t in range(GT):
                    c = slice(t * P, t * P + P)
                    ins = split3(PS[:, 4 + 2 * b + t // 2, (t % 2) * D:(t % 2) * D + D], [(ah[:, b, c], al[:, b, c], Dh[:, e], Dl[:, e])])
                ins.then_inc(s[f"f{L}_dn"], 1)

            def body(r, first=False):
                for k in range(per):
                    n = r * per + k
                    gate_up(n, r * gu + k // ne, k % ne, k)
                    if not first or k >= 1:
                        down(n - 1, (k - 1) % ne, (k - 1) % per)

            body(0, True)
            with pe.Fori(1, NG // gu) as r:
                body(r)
            down(NG * ne - 1, ne - 1, per - 1)

        prep("c", xnc)
        logits(0, "c")
        pe.wait_ge(s["w_split0"], NG)
        experts(0, 2)
        prep("e", xn1)

        def project(i, m):
            wait_misc()
            split3(PS[:, 7, 0:POS].rearrange("p (j c) -> p j c", j=NT),
                   [(a1h[:, k, m * P:m * P + P], a1l[:, k, m * P:m * P + P], img(xTh[:, k, :], i), img(xTl[:, k, :], i)) for k in range(KC)]).then_inc(s["e_pr"], 1)
            last[0] = ("e_prev", 3 * i + m + 1)

        last = [None]

        def wait_misc():
            if last[0] is not None:
                wait(pe, s[last[0][0]], last[0][1])

        def turn(it, p, pr, sp_, st):
            q = 1 - p
            done = 0
            av = 0
            for U in range(NU):
                if sp_ and U == VT_U:
                    pe.wait_ge(s["e_prev"], 3 * it)
                    wait_misc()
                    for kt in range(NKT):
                        ins = nc.tensor.transpose(PS[0:KT, 7, kt * P:kt * P + P], qf[:, 2, kt * KT:kt * KT + KT], ident[:, :])
                    ins.then_inc(s["e_vt"], 1)
                    last[0] = ("e_va", it)
                if pr and U in PR_U:
                    project(it, PR_U.index(U))
                if st:
                    i = it - 2
                    if U == 0:
                        pe.wait_ge(s["e_min"], 16 * (i + 1))
                    wait(pe, s["e_exp"], i * NU + U - 1)
                    for n in (2 * U, 2 * U + 1):
                        g, kt, cc = n // 9, n % 9 // 3, n % 3
                        ins = M(PS[0:KT, n % 4, 0:CW], KS[p][:, g * POS + kt * KT:g * POS + kt * KT + KT],
                                QS[p][:, g * HQ + cc * CW:g * HQ + cc * CW + CW], start=True, stop=True)
                    ins.then_inc(s["e_st"], 1)
                if sp_:
                    i = it - 1
                    for c in range(done, S_UPTO[U]):
                        if c % (NS // 2) == 0:
                            pe.wait_ge(s[f"e_in{c // (NS // 2)}"], 16 * 6 * (i + 1))
                        wait(pe, s["e_mx"], NS * i + c - 1)
                        M(PS[:, 4 + c % 2, 0:POS], QS[q][0:STK, c * P:c * P + P], KS[q][0:STK, c // 9 * POS:c // 9 * POS + POS],
                          start=True, stop=True).then_inc(s["e_s"], 1)
                    done = S_UPTO[U]
                    if U == MT_U:
                        pe.wait_ge(s["e_mx"], NS * (i + 1))
                        wait_misc()
                        nc.tensor.transpose(PS[:, 7, 0:P], MX[:, :], ident[:, :]).then_inc(s["e_mT"], 1)
                        last[0] = ("e_msplit", i + 1)
                if st:
                    while av < NAV and (3 * av + 2) // 2 + 2 <= U:
                        values(it - 2, av, p)
                        av += 1
                    if U in SB_AT:
                        spread(it - 2, SB_AT.index(U))
            if st:
                while av < NAV:
                    values(it - 2, av, p)
                    av += 1
                spread(it - 2, NGQ - 1)

        def values(i, m, p):
            g, kt = m // NKT, m % NKT
            pe.wait_ge(s["e_exp"], i * NU + (3 * m + 2) // 2 + 1)
            if m == 0:
                pe.wait_ge(s["e_va"], i + 1)
            if kt == 0:
                wait(pe, s["e_yr"], NGQ * i + g)
            c0 = (3 * m) % RING
            for hh in range(HPG):
                ins = M(PS[32 * hh:32 * hh + 32, 6, 0:POS], VA[p][:, kt, g, :],
                        PR[:, c0:c0 + 3, :].rearrange("p c w -> p (c w)")[:, hh * POS:hh * POS + POS],
                        start=(kt == 0), stop=(kt == NKT - 1), tile_position=(0, 32 * hh))
            ins.then_inc(s["e_avt"], 1)

        def spread(i, g):
            pe.wait_ge(s["e_yr"], NGQ * i + g + 1)
            wait_misc()
            M(PS[:, 7, 0:POS], sel16[:, :], yr[:, :], start=True, stop=True).then_inc(s["e_sb"], 1)
            last[0] = ("e_rec", NGQ * i + g + 1)

        pe.wait_ge(s["e_a1"], 1)
        pe.wait_ge(s["e_kv_const"], 4)
        pe.wait_ge(s["d_wo"], 48)
        pe.wait_ge(s["e_lo"], NT)
        pe.wait_ge(s["e_hi"], NT)
        turn(0, 0, True, False, False)
        turn(1, 1, True, True, False)
        turn(2, 0, True, True, True)
        turn(3, 1, True, True, True)
        with pe.Fori(2, 4) as r:
            last[0] = ("e_rec", NGQ * (2 * r - 2))
            turn(2 * r, 0, True, True, True)
            turn(2 * r + 1, 1, True, True, True)
        last[0] = ("e_rec", NGQ * 6)
        turn(8, 0, False, True, True)
        turn(9, 1, False, False, True)
        pe.wait_ge(s["e_y"], NGQ * IMGS)
        for j in range(NT):
            wait(pe, s["g_res"], j - 3)
            for g in range(NGQ):
                ins = M(PS[:, j % 4, 0:D], yT[:, g, j * P:j * P + P], wo[:, g, :], start=(g == 0), stop=(g == NGQ - 1))
            ins.then_inc(s["g_wo"], 1)
        prep("p", xnc)
        logits(1, "p")
        pe.wait_ge(s["w_split1"], NG)
        experts(1, 3)

    ctx.close()


PR_U = [1, 3, 5]
VT_U = 0
S_UPTO = [min(NS, (NS * (U + 1) + 13) // 14) for U in range(NU)]
MT_U = 14
YR_AT = [7, 12, 16]
SB_AT = [8, 13, 17]


def kernel(x, txt, L0_tok_Wa, L0_tok_ba, L0_tok_Wd1, L0_tok_bd1, L0_tok_Wd2, L0_tok_bd2, L0_tok_Wd3, L0_tok_bd3,
           L0_attn_Wq, L0_attn_bq, L0_attn_Wk, L0_attn_bk, L0_attn_Wv, L0_attn_bv,
           L0_ffn_router_weight, L0_ffn_correction_bias, L0_ffn_w_gate, L0_ffn_w_up, L0_ffn_w_down,
           L0_ffn_sw_gate, L0_ffn_sw_up, L0_ffn_sw_down,
           L1_attn_Wq, L1_attn_bq, L1_attn_Wk, L1_attn_bk, L1_attn_Wv, L1_attn_bv, L1_attn_Wo, L1_attn_bo,
           L1_ffn_gate_w, L1_ffn_lb_bias, L1_ffn_expert_gate_w, L1_ffn_expert_up_w, L1_ffn_expert_down_w,
           L1_ffn_shared_gate_w, L1_ffn_shared_up_w, L1_ffn_shared_down_w):
    import numpy as np
    import concourse.bacc as bacc
    from concourse.bass_utils import run_bass_kernel_spmd

    f = lambda a: np.asarray(a)
    arr = {}
    arr["x"] = f(x).reshape(P, ROWS, SIDE)
    arr["txt"] = f(txt).reshape(IMGS, TXT_T, RG, D).transpose(0, 2, 1, 3).reshape(P, TXT_T, D)
    for n, w in enumerate((L0_tok_Wd3, L0_tok_Wd2, L0_tok_Wd1)):
        r, c = ROWS >> (n + 1), SIDE >> (n + 1)
        arr[f"wd{n}"] = f(w).reshape(3, RG, r, c, 3).transpose(1, 4, 0, 2, 3).reshape(RG, 3, 3 * r * c)
    arr["wa"] = f(L0_tok_Wa).reshape(RG, (ROWS // 8) * (SIDE // 8))
    arr["lbias"] = np.concatenate([f(L0_tok_bd1), f(L0_tok_bd2), f(L0_tok_bd3), f(L0_tok_ba)])[None]
    p = np.arange(P)
    consts = np.zeros((P, 4, P), np.float32)
    consts[:, 0] = np.eye(P)
    consts[:, 1] = p[:, None] // RG == p[None, :] // RG
    consts[:, 2] = np.where(p[:, None] % RG == p[None, :] % RG, 0.0, BIG)
    consts[:, 3] = p[:, None] == p[None, :] // 32 * 32 + HD
    arr["consts"] = consts
    arr["lt"] = (np.arange(NE)[None, :] < np.arange(NE)[:, None]).astype(np.float32).reshape(1, NE * NE)

    def rows_in(w):
        return w.reshape(KC, P, w.shape[-1]).transpose(1, 0, 2)

    arr["qkv0"] = np.stack([rows_in(f(w).T) for w in (L0_attn_Wq, L0_attn_Wk, L0_attn_Wv)], 1)
    arr["bqk0"] = np.stack([f(L0_attn_bq)[:P], f(L0_attn_bq)[P:], f(L0_attn_bk)[:P], f(L0_attn_bk)[P:]], 1)
    arr["bv0"] = f(L0_attn_bv)[None]
    arr["cb0"] = f(L0_ffn_correction_bias)[None]
    arr["lb1"] = f(L1_ffn_lb_bias)[None]
    arr["bo1"] = f(L1_attn_bo)[None]
    arr["rw0"] = rows_in(f(L0_ffn_router_weight).T)
    arr["rw1"] = rows_in(f(L1_ffn_gate_w).T)

    def ffn(gate, up, down):
        ge = lambda w: w.reshape(w.shape[0], KC, P, P).transpose(2, 0, 1, 3).reshape(P, -1)
        return np.concatenate([ge(gate), ge(up), down.transpose(1, 0, 2).reshape(P, -1)], 1)

    arr["w0"] = ffn(np.concatenate([f(L0_ffn_w_gate), f(L0_ffn_sw_gate)[None]]),
                    np.concatenate([f(L0_ffn_w_up), f(L0_ffn_sw_up)[None]]),
                    np.concatenate([f(L0_ffn_w_down), f(L0_ffn_sw_down)[None]]))
    two = lambda w: w.reshape(2, P, D)
    arr["w1"] = ffn(np.concatenate([f(L1_ffn_expert_gate_w), two(f(L1_ffn_shared_gate_w))]).transpose(0, 2, 1),
                    np.concatenate([f(L1_ffn_expert_up_w), two(f(L1_ffn_shared_up_w))]).transpose(0, 2, 1),
                    np.concatenate([f(L1_ffn_expert_down_w), f(L1_ffn_shared_down_w).reshape(D, 2, P).transpose(1, 0, 2)]).transpose(0, 2, 1))
    arr["a1"] = rows_in(np.concatenate([f(L1_attn_Wq), f(L1_attn_Wk), f(L1_attn_Wv)]).T)
    arr["bq1"] = np.stack([f(L1_attn_bq)[:P], f(L1_attn_bq)[P:], np.concatenate([f(L1_attn_bk), f(L1_attn_bv)])], 1)
    wo = np.zeros((HPG, 32, NGQ, D), np.float32)
    wo[:, 0:HD] = f(L1_attn_Wo).T.reshape(NGQ, HPG, HD, D).transpose(1, 2, 0, 3)
    arr["wo1"] = wo.reshape(P, NGQ, D)

    nc = bacc.Bacc("TRN2", target_bir_lowering=False, num_devices=1)
    ins, A = {}, {}
    for name, a in arr.items():
        a = np.ascontiguousarray(a)
        ins["in_" + name] = a
        A[name] = nc.dram_tensor("in_" + name, a.shape, mybir.dt.from_np(a.dtype), kind="ExternalInput").ap()
    out = nc.dram_tensor("out_tokens", (P, NT, D), F32, kind="ExternalOutput").ap()
    build(nc, A, out)
    got = run_bass_kernel_spmd(nc, [ins], core_ids=[0]).results[0]["out_tokens"]
    y = np.asarray(got).reshape(IMGS, RG, NT, D)
    image = y[:, :, :ROWS].reshape(IMGS, SIDE, D)
    text = y[:, :, ROWS:].transpose(0, 2, 1, 3).reshape(IMGS, TXT_T * RG, D)
    return np.concatenate([image, text], 1)
```

```python
from contextlib import ExitStack

import concourse.bass as bass
from concourse import mybir

ALU = mybir.AluOpType
ACT = mybir.ActivationFunctionType
AX_X = mybir.AxisListType.X
F32 = mybir.dt.float32
F32R = mybir.dt.float32r
ds = bass.ds

P = 128
IMGS = 8
RG = P // IMGS
SIDE = 256
D = 256
KC = D // P
ROWS = SIDE // RG
TXT_T = 2
NT = ROWS + TXT_T
TOK = NT * P
POS = TOK // IMGS
GT = 3
NG = NT // GT
GW = GT * P
NE = 8
LN_EPS = 1e-5
BIG = 3.0e38
NGQ, HPG, HD = 4, 4, 16
HQ = HPG * POS
KT = 96
NKT = POS // KT
CW = 384
NCH = NGQ * NKT * (HQ // CW)
NU = NCH // 2
RING = 12
NS = NGQ * HQ // P
MROW = 96
NAV = NGQ * NKT
WCOLS = {0: (9 * KC * P, 9 * KC * P, 9 * D), 1: (10 * KC * P, 10 * KC * P, 10 * D)}


def wait(eng, sem, value):
    if isinstance(value, int) and value <= 0:
        return
    eng.wait_ge(sem, value)


class Own:

    def __init__(self, eng, sem):
        self.eng, self.sem, self.n, self.base = eng, sem, 0, 0

    def __call__(self, ins):
        ins.then_inc(self.sem, 1)
        self.n += 1

    def settle(self):
        self.eng.wait_ge(self.sem, self.base + self.n)

    def loop(self, lo, hi, per, body):
        start = self.base + self.n
        with self.eng.Fori(lo, hi) as i:
            self.base, self.n = start + (i - lo) * per, 0
            body(i)
            assert self.n == per, (self.n, per)
        self.base, self.n = start + (hi - lo) * per, 0


def build(nc, A, out):
    ctx = ExitStack()
    base0 = 16512
    end = 229344
    top = [base0]

    def at(name, shape, dt, off):
        size = 4
        for n in shape[1:]:
            size *= n
        assert off % 32 == 0 and off + size <= end, (name, off, size, end)
        return nc.alloc_sbuf_tensor_at(name, shape, dt, offset=off)

    def keep(name, shape, dt=F32):
        size = 4
        for n in shape[1:]:
            size *= n
        t = at(name, shape, dt, top[0])
        top[0] += (size + 31) // 32 * 32
        return t

    h = keep("h", [P, NT, D])
    xTh = keep("xTh", [P, KC, TOK], F32R)
    xTl = keep("xTl", [P, KC, TOK], F32R)
    ident = keep("ident", [P, P])
    same_img = keep("same_img", [P, P])
    far_mask = keep("far_mask", [P, P])
    ones = keep("ones", [P, P])
    gather = keep("gather", [P, NGQ, NGQ * HPG])
    spread = keep("spread", [NGQ * HPG, NGQ, P])
    lt = keep("lt", [P, NE * NE])
    stats = keep("stats", [P, NT, 6])
    mv = keep("mv", [P, NT, 2])
    mt = keep("mt", [P, 4, NT])
    rstd = keep("rstd", [P, NT])
    eps = keep("eps", [P, 1])
    bqk0 = keep("bqk0", [P, 4])
    bv0 = keep("bv0", [P, D])
    bq1 = keep("bq1", [P, 3])
    bo1 = keep("bo1", [P, D])
    cb0 = keep("cb0", [P, NE])
    lb1 = keep("lb1", [P, NE])
    rw = [keep(f"rw{x}", [P, KC, NE]) for x in range(2)]
    rwh = [keep(f"rwh{x}", [P, KC, NE], F32R) for x in range(2)]
    rwl = [keep(f"rwl{x}", [P, KC, NE], F32R) for x in range(2)]
    cmb = keep("cmb", [P, NT, 10])
    R1 = top[0]

    o = [R1]

    def seq(name, shape, dt=F32, cur=o):
        size = 4
        for n in shape[1:]:
            size *= n
        t = at(name, shape, dt, cur[0])
        cur[0] += (size + 31) // 32 * 32
        return t

    NLV = 3
    rows = [ROWS >> (n + 1) for n in range(NLV)]
    cols = [SIDE >> (n + 1) for n in range(NLV)]
    x_in = seq("x_in", [P, ROWS, SIDE])
    lo = [seq(f"lo{n}", [P, 2 * rows[n], cols[n]]) for n in range(NLV)]
    hi = [seq(f"hi{n}", [P, 2 * rows[n], cols[n]]) for n in range(NLV)]
    app = [seq(f"app{n}", [P, rows[n], cols[n]]) for n in range(NLV)]
    det = [seq(f"det{n}", [P, 3, rows[n], cols[n]]) for n in range(NLV)]
    dsc = [seq(f"dsc{n}", [P, rows[n], cols[n]]) for n in range(NLV)]
    sizes = [3 * rows[n] * cols[n] for n in range(NLV)]
    wd = [seq(f"wd{n}", [P, 3, sizes[n]]) for n in range(NLV)]
    wa = seq("wa", [P, rows[2] * cols[2]])
    junk = seq("junk", [P, sizes[0]])
    dots = seq("dots", [P, 10])
    lg = seq("lg", [P, 10])
    lbias = seq("lbias", [P, 10])
    wmx = seq("wmx", [P, NLV])
    wex = seq("wex", [P, 10])
    wsm = seq("wsm", [P, 4])
    wts = seq("wts", [P, 10])

    wb = [base0 + NT * D * 4]
    qkv_raw = seq("qkv_raw", [P, 3, KC, D], cur=wb)
    qkv_h = seq("qkv_h", [P, 3, KC, D], F32R, cur=wb)
    qkv_l = seq("qkv_l", [P, 3, KC, D], F32R, cur=wb)
    assert wb[0] <= base0 + NT * D * 4 + 2 * KC * TOK * 4
    FW = 3 * 10 * D * 4
    wk = [R1 + 3 * FW]
    xwh = seq("xwh", [P, KC, GW], F32R, cur=wk)
    xwl = seq("xwl", [P, KC, GW], F32R, cur=wk)
    xn = seq("xn", [P, GT, D], cur=wk)
    qT = seq("qT", [P, KC, GW], cur=wk)
    km2 = seq("km2", [P, KC, GW], cur=wk)
    qsq = seq("qsq", [P, KC, GW], cur=wk)
    ksq = seq("ksq", [P, KC, GW], cur=wk)
    qs = seq("qs", [P, GW], cur=wk)
    ks = seq("ks", [P, GW], cur=wk)
    v_sb = seq("v_sb", [P, GT, D], cur=wk)
    dm = seq("dm", [P, GT, P], cur=wk)
    Pm = seq("Pm", [P, GT, P], cur=wk)
    PT = seq("PT", [P, GT, P], cur=wk)
    mn = seq("mn", [P, GT], cur=wk)
    hb = seq("hb", [P, GT], cur=wk)
    rs = seq("rs", [P, GT], cur=wk)
    ri = seq("ri", [P, GT], cur=wk)

    W_raw, W_h, W_l = [], [], []
    for L in range(2):
        n = sum(WCOLS[L])
        W_h.append(at(f"W{L}h", [P, n], F32R, R1))
        W_l.append(at(f"W{L}l", [P, n], F32R, R1 + FW))
        W_raw.append(at(f"W{L}raw", [P, n], F32, R1 + 2 * FW))

    def w_part(t, L, part):
        ne = 9 + L
        a = sum(WCOLS[L][:part])
        v = t[:, a:a + WCOLS[L][part]]
        return v.rearrange("p (e k i) -> p e k i", e=ne, k=KC) if part < 2 else v.rearrange("p (e d) -> p e d", e=ne)

    fk = [R1 + 3 * FW]
    xnc = seq("xnc", [P, 2, D], cur=fk)
    lgT = seq("lgT", [NE, TOK], cur=fk)
    sc = seq("sc", [P, NT, NE], cur=fk)
    sv = seq("sv", [P, NT, NE], cur=fk)
    ra = seq("ra", [P, NT, NE, NE], cur=fk)
    rb_ = seq("rb_", [P, NT, NE, NE], cur=fk)
    t1 = seq("t1", [P, NT, NE], cur=fk)
    t2 = seq("t2", [P, NT, NE], cur=fk)
    t3 = seq("t3", [P, NT, NE], cur=fk)
    tot = seq("tot", [P, 2 * NE], cur=fk)
    hk = [fk[0]]
    sg = seq("sg", [P, 2, GW], cur=hk)
    aa = seq("aa", [P, 2, GW], cur=hk)
    ah = seq("ah", [P, 2, GW], F32R, cur=hk)
    al = seq("al", [P, 2, GW], F32R, cur=hk)

    k1 = [R1]
    QS = [seq(f"QS{p}", [P, NGQ * HQ], F32R, cur=k1) for p in range(2)]
    KS = [seq(f"KS{p}", [P, NGQ * POS], F32R, cur=k1) for p in range(2)]
    PR = seq("PR", [P, RING, CW], cur=k1)
    VA = [seq(f"VA{p}", [P, NKT, NGQ, 32], cur=k1) for p in range(2)]
    qf = [seq(f"qf{p}", [P, 3, POS], cur=k1) for p in range(2)]
    qh = seq("qh", [P, 3, POS], F32R, cur=k1)
    ql = seq("ql", [P, 3, POS], F32R, cur=k1)
    MX = seq("MX", [P, P], cur=k1)
    Mh = seq("Mh", [NS, P], F32R, cur=k1)
    Ml = seq("Ml", [NS, P], F32R, cur=k1)
    neg1 = at("neg1", [2, NGQ * POS], F32, k1[0])
    yr = [seq(f"yr{p}", [P, NGQ, POS], cur=k1) for p in range(2)]
    rec = seq("rec", [NGQ * HPG, POS], cur=k1)
    yT = seq("yT", [P, NGQ, TOK], cur=k1)
    wo = seq("wo", [P, NGQ, D], cur=k1)
    a1raw = seq("a1raw", [P, KC, 3 * P], cur=k1)
    a1h = seq("a1h", [P, KC, 3 * P], F32R, cur=k1)
    a1l = seq("a1l", [P, KC, 3 * P], F32R, cur=k1)
    xn1 = seq("xn1", [P, 2, D], cur=k1)

    PS = ctx.enter_context(nc.psum_tensor("PS", [P, 8, 512], F32))
    scrH = nc.dram_tensor("scrH", (IMGS, P, 3, POS), F32, kind="Internal").ap()
    scrL = nc.dram_tensor("scrL", (IMGS, P, 3, POS), F32, kind="Internal").ap()
    scrM = nc.dram_tensor("scrM", (IMGS, 2, NS, P), F32, kind="Internal").ap()

    S = {}

    def sem(name):
        if name not in S:
            S[name] = ctx.enter_context(nc.semaphore(name))
        return S[name]

    names = """d_x d_txt d_const d_wd d_bias d_qkv d_small d_w0 d_w1 d_a1 d_wo d_out
        dve_own act_own pool_own
        pool_hi dots_ready dots_sum wex_in wex_ready wts_ready dsc_ready img_done
        st_ready0 st_ready1 st_ready2 st_ready3 std_ready0 std_ready1 std_ready2 std_ready3
        rstd_ready0 rstd_ready1 rstd_ready2 rstd_ready3
        const_pool qkv_hi qkv_split rw_split0 rw_split1
        b_xn b_T b_hi b_x b_qk b_dqk b_aqk b_qs b_hb b_v b_vev b_d2 b_dm b_exp b_pt b_ptev b_av b_res
        w_hi0 w_split0 w_hi1 w_split1
        c_scan
        e_kv_const e_a1h e_a1 e_bo
        e_pr e_prev e_split e_out e_in0 e_in1 e_vt e_va e_s e_mx e_mT e_msplit e_mout e_min
        e_st e_exp e_avt e_yr e_sum e_rec e_sb e_y e_hi3
        g_wo g_res""".split()
    for n in names:
        sem(n)
    for c in "cep":
        for n in ("xn", "T", "hi", "lo"):
            sem(f"{c}_{n}")
    for L in range(2):
        for n in ("lg", "lgT", "lgt", "sig", "lraw", "tot", "sum", "cmb", "gu", "silu", "mul", "ah", "al", "dn", "acc"):
            sem(f"f{L}_{n}")
    assert len(S) < 200, len(S)
    s = S
    block = ctx.enter_context(nc.Block())

    def img(t, i):
        return t.rearrange("p (j c) -> p j c", j=NT)[:, :, ds(i * RG, RG)]

    @block.sync
    def _(sp):
        for n in range(2):
            sp.dma_start(x_in[:, n * 8:n * 8 + 8, :], A["x"][:, n * 8:n * 8 + 8, :]).then_inc(s["d_x"], 16)
        sp.dma_start(h[:, ROWS:NT, :], A["txt"]).then_inc(s["d_txt"], 16)
        for n, t in enumerate((ident, same_img, far_mask)):
            sp.dma_start(t[:, :], A["consts"][:, n, :]).then_inc(s["d_const"], 16)
        sp.dma_start(gather[:, :, :], A["gather"]).then_inc(s["d_const"], 16)
        sp.dma_start(spread[:, :, :], A["spread"]).then_inc(s["d_const"], 16)
        sp.dma_start(lt[:, :], A["lt"].broadcast_to([P, NE * NE])).then_inc(s["d_const"], 16)
        sp.dma_start(lbias[:, :], A["lbias"].broadcast_to([P, 10])).then_inc(s["d_bias"], 16)
        sp.dma_start(qkv_raw[:, :, :, :], A["qkv0"]).then_inc(s["d_qkv"], 16)
        sp.dma_start(bqk0[:, :], A["bqk0"]).then_inc(s["d_small"], 16)
        sp.dma_start(bv0[:, :], A["bv0"].broadcast_to([P, D])).then_inc(s["d_small"], 16)
        sp.dma_start(bq1[:, :], A["bq1"]).then_inc(s["d_small"], 16)
        sp.dma_start(bo1[:, :], A["bo1"].broadcast_to([P, D])).then_inc(s["d_small"], 16)
        sp.dma_start(cb0[:, :], A["cb0"].broadcast_to([P, NE])).then_inc(s["d_small"], 16)
        sp.dma_start(lb1[:, :], A["lb1"].broadcast_to([P, NE])).then_inc(s["d_small"], 16)
        for L in range(2):
            sp.dma_start(rw[L][:, :, :], A[f"rw{L}"]).then_inc(s["d_small"], 16)
        sp.wait_ge(s["img_done"], 1)
        sp.dma_start(W_raw[0][:, :], A["w0"]).then_inc(s["d_w0"], 16)
        sp.wait_ge(s["f0_acc"], NG * 9)
        sp.dma_start(a1raw[:, :, :], A["a1"]).then_inc(s["d_a1"], 16)
        sp.dma_start(wo[:, :, :], A["wo1"]).then_inc(s["d_wo"], 16)
        sp.wait_ge(s["e_kv_const"], 4)
        for p in range(2):
            sp.dma_start(KS[p][MROW:MROW + 2, :].bitcast(F32), neg1[:, :]).then_inc(s["d_wo"], 16)

        def stack_out(i):
            sp.wait_ge(s["e_split"], 3 * (i + 1))
            sp.dma_start(scrH[ds(i, 1)].rearrange("o p m q -> (o p) m q"), qh[:, :, :].bitcast(F32)).then_inc(s["e_out"], 16)
            sp.dma_start(scrL[ds(i, 1)].rearrange("o p m q -> (o p) m q"), ql[:, :, :].bitcast(F32)).then_inc(s["e_out"], 16)

        def stack_in(i, p, m):
            if m == 0:
                sp.wait_ge(s["e_out"], 32 * (i + 1))
            if not (isinstance(i, int) and i < 2):
                sp.wait_ge(s["e_st"], (i - 2) * NU + NU // 2 * (m + 1))
            for n, src in enumerate((scrH, scrH, scrL)):
                sp.dma_start(QS[p][n * HD:n * HD + HD, m * 8 * POS:(m + 1) * 8 * POS].bitcast(F32).rearrange("d (h q) -> d h q", h=8),
                             src[ds(i, 1), :, m, :].rearrange("o (h d) q -> d (o h) q", d=HD)).then_inc(s[f"e_in{m}"], 16)
            for n, src in enumerate((scrH, scrL, scrH)):
                sp.dma_start(KS[p][n * HD:n * HD + HD, m * 2 * POS:(m + 1) * 2 * POS].bitcast(F32).rearrange("d (g q) -> d g q", g=2),
                             src[ds(i, 1), m * 2 * HD:(m + 1) * 2 * HD, 2, :].rearrange("o (g d) q -> d (o g) q", d=HD)).then_inc(s[f"e_in{m}"], 16)

        def max_rows(i, p):
            sp.wait_ge(s["e_msplit"], i + 1)
            for n, src in enumerate((Mh, Ml)):
                sp.dma_start(scrM[ds(i, 1), n].rearrange("o c r -> (o c) r"), src[:, :].bitcast(F32)).then_inc(s["e_mout"], 16)
            sp.wait_ge(s["e_mout"], 32 * (i + 1))
            sp.dma_start(QS[p][MROW:MROW + 2, :].bitcast(F32), scrM[ds(i, 1)].rearrange("o n c r -> (o n) (c r)")).then_inc(s["e_min"], 16)

        def turn(it, p, pr, sp_, st):
            if pr:
                stack_out(it)
                stack_in(it, p, 0)
            if sp_:
                max_rows(it - 1, 1 - p)
            if pr:
                stack_in(it, p, 1)

        turn(0, 0, True, False, False)
        turn(1, 1, True, True, False)
        turn(2, 0, True, True, True)
        turn(3, 1, True, True, True)
        with sp.Fori(2, 4) as r:
            turn(2 * r, 0, True, True, True)
            turn(2 * r + 1, 1, True, True, True)
        turn(8, 0, False, True, True)
        sp.wait_ge(s["g_wo"], NT)
        sp.dma_start(W_raw[1][:, :], A["w1"]).then_inc(s["d_w1"], 16)
        with sp.Fori(0, NG) as g:
            sp.wait_ge(s["f1_acc"], 10 * (g + 1))
            sp.dma_start(out[:, ds(g * GT, GT), :], h[:, ds(g * GT, GT), :]).then_inc(s["d_out"], 16)
        sp.wait_ge(s["d_out"], 16 * NG)

    @block.gpsimd
    def _(pool):
        own = Own(pool, s["pool_own"])
        nc.gpsimd.memset(ones[:, :], 1.0).then_inc(s["const_pool"], 1)
        nc.gpsimd.memset(eps[:, :], LN_EPS).then_inc(s["const_pool"], 1)
        nc.gpsimd.memset(cmb[:, :, :], 1.0).then_inc(s["const_pool"], 1)
        pool.wait_ge(s["d_x"], 32)
        xv = x_in[:, :, :].rearrange("p r (c t) -> p r c t", t=2)
        own(nc.gpsimd.tensor_tensor(hi[0][:, :, :], xv[:, :, :, 0], xv[:, :, :, 1], ALU.subtract))
        own.settle()
        hv = hi[0][:, :, :].rearrange("p (r t) c -> p r t c", t=2)
        nc.gpsimd.tensor_tensor(det[0][:, 1], hv[:, :, 0, :], hv[:, :, 1, :], ALU.add)
        nc.gpsimd.tensor_tensor(det[0][:, 2], hv[:, :, 0, :], hv[:, :, 1, :], ALU.subtract).then_inc(s["pool_hi"], 1)
        pool.wait_ge(s["qkv_hi"], 1)
        nc.gpsimd.tensor_tensor(qkv_l[:, :, :, :], qkv_raw[:, :, :, :], qkv_h[:, :, :, :].bitcast(F32), ALU.subtract).then_inc(s["qkv_split"], 1)
        pool.wait_ge(s["d_small"], 16 * 8)
        pool.wait_ge(s["qkv_hi"], 2)
        for L in range(2):
            nc.gpsimd.tensor_tensor(rwl[L][:, :, :], rw[L][:, :, :], rwh[L][:, :, :].bitcast(F32), ALU.subtract).then_inc(s["rw_split0"], 1)

        n0 = sum(WCOLS[0]) // NG

        def l0(i):
            pool.wait_ge(s["b_xn"], i + 1)
            for t in range(GT):
                nc.gpsimd.tensor_tensor(h[:, ds(i * GT + t, 1), :].squeeze(1), h[:, ds(i * GT + t, 1), :].squeeze(1), bv0[:, :], ALU.add).then_inc(s["b_hb"], 1)
            pool.wait_ge(s["b_aqk"], i + 1)
            wait(pool, s["b_d2"], i)
            nc.gpsimd.tensor_tensor(qs[:, :], qsq[:, 0], qsq[:, 1], ALU.add)
            nc.gpsimd.tensor_tensor(ks[:, :], ksq[:, 0], ksq[:, 1], ALU.add).then_inc(s["b_qs"], 1)
            pool.wait_ge(s["w_hi0"], i + 1)
            nc.gpsimd.tensor_tensor(W_l[0][:, ds(i * n0, n0)], W_raw[0][:, ds(i * n0, n0)], W_h[0][:, ds(i * n0, n0)].bitcast(F32), ALU.subtract).then_inc(s["w_split0"], 1)

        l0(0)
        with pool.Fori(1, NG) as i:
            l0(i)

        pool.wait_ge(s["f0_acc"], NG * 9)
        nc.gpsimd.memset(neg1[:, :], -1.0).then_inc(s["e_kv_const"], 1)
        nc.gpsimd.memset(MX[:, :], 0.0).then_inc(s["e_kv_const"], 1)
        for p in range(2):
            own(nc.gpsimd.memset(QS[p][:, :].bitcast(F32), 0.0))
            own(nc.gpsimd.memset(KS[p][:, :].bitcast(F32), 0.0))
            own(nc.gpsimd.memset(VA[p][:, :, :, :], 0.0))
        own.settle()
        own(nc.gpsimd.memset(PR[96:P, :, :], 0.0))
        own.settle()
        for p in range(2):
            nc.gpsimd.memset(VA[p][0:KT, :, :, HD:HD + 1], 1.0).then_inc(s["e_kv_const"], 1)
        pool.wait_ge(s["e_a1h"], 1)
        nc.gpsimd.tensor_tensor(a1l[:, :, :], a1raw[:, :, :], a1h[:, :, :].bitcast(F32), ALU.subtract).then_inc(s["e_a1"], 1)
        pool.wait_ge(s["e_xn"], NT)
        with pool.Fori(0, NT) as j:
            nc.gpsimd.tensor_tensor(h[:, ds(j, 1), :].squeeze(1), h[:, ds(j, 1), :].squeeze(1), bo1[:, :], ALU.add).then_inc(s["e_bo"], 1)

        def low_halves(it, p):
            for m in range(3):
                pool.wait_ge(s["e_hi3"], 3 * it + m + 1)
                if m == 0:
                    wait(pool, s["e_out"], 32 * it)
                nc.gpsimd.tensor_tensor(ql[:, m], qf[p][:, m], qh[:, m].bitcast(F32), ALU.subtract).then_inc(s["e_split"], 1)

        low_halves(0, 0)
        low_halves(1, 1)
        with pool.Fori(1, IMGS // 2) as r:
            low_halves(2 * r, 0)
            low_halves(2 * r + 1, 1)
        n1 = sum(WCOLS[1]) // NG
        with pool.Fori(0, NG) as i:
            pool.wait_ge(s["w_hi1"], i + 1)
            nc.gpsimd.tensor_tensor(W_l[1][:, ds(i * n1, n1)], W_raw[1][:, ds(i * n1, n1)], W_h[1][:, ds(i * n1, n1)].bitcast(F32), ALU.subtract).then_inc(s["w_split1"], 1)

    @block.scalar
    def _(act):
        A_ = nc.scalar.activation
        for n in (2, 1, 0):
            for b in range(IMGS):
                act.dma_start(wd[n][b * RG:b * RG + RG, :, :], A[f"wd{n}"]).then_inc(s["d_wd"], 16)
        for b in range(IMGS):
            act.dma_start(wa[b * RG:b * RG + RG, :], A["wa"]).then_inc(s["d_wd"], 16)
        act.wait_ge(s["d_qkv"], 16)
        A_(qkv_h[:, :, :, :], qkv_raw[:, :, :, :], ACT.Copy).then_inc(s["qkv_hi"], 1)
        act.wait_ge(s["d_small"], 16 * 8)
        A_(rwh[0][:, :, :], rw[0][:, :, :], ACT.Copy)
        A_(rwh[1][:, :, :], rw[1][:, :, :], ACT.Copy).then_inc(s["qkv_hi"], 1)
        act.wait_ge(s["wex_in"], 1)
        A_(wex[:, 0:9], wex[:, 0:9], ACT.Exp)
        A_(wex[:, 9:10], lg[:, 9:10], ACT.Exp, scale=-1.0).then_inc(s["wex_ready"], 1)
        act.wait_ge(s["wts_ready"], 1)
        for n in (2, 1, 0):
            c = 3 * (2 - n) + 2
            A_(dsc[n][:, :, :], det[n][:, 2], ACT.Copy, scale=wts[:, c:c + 1]).then_inc(s["dsc_ready"], 1)

        def std(n):
            act.wait_ge(s[f"st_ready{n}"], 1)
            A_(rstd[:, :], mv[:, :, 1], ACT.Sqrt, bias=eps[:, 0:1]).then_inc(s[f"std_ready{n}"], 1)

        act.wait_ge(s["const_pool"], 3)
        std(0)
        n0 = sum(WCOLS[0]) // NG

        def ln_hi(i):
            act.wait_ge(s["b_T"], i + 1)
            wait(act, s["b_v"], i)
            A_(xwh[:, :, 0:2 * P].rearrange("p k (t c) -> p t k c", t=2), PS[:, 4, :].rearrange("p (t k c) -> p t k c", t=2, k=KC), ACT.Copy)
            A_(xwh[:, :, 2 * P:], PS[:, 5, 0:D].rearrange("p (k c) -> p k c", k=KC), ACT.Copy).then_inc(s["b_hi"], 1)

        def l0(i, prev, cur, nxt):
            if cur:
                act.wait_ge(s["b_dqk"], i + 1)
                wait(act, s["b_qs"], i)
                A_(qsq[:, :, :], qT[:, :, :], ACT.Square)
                A_(ksq[:, :, :], km2[:, :, :], ACT.Square, scale=0.5).then_inc(s["b_aqk"], 1)
            if prev:
                act.wait_ge(s["b_pt"], i)
                wait(act, s["b_av"], i - 1)
                A_(PT[:, :, :], PS[:, 7, 0:GW].rearrange("p (t c) -> p t c", t=GT), ACT.Copy).then_inc(s["b_ptev"], 1)
            if nxt:
                ln_hi(i + 1)
            if cur:
                act.wait_ge(s["b_v"], i + 1)
                wait(act, s["b_av"], i)
                A_(v_sb[:, 0:2, :], PS[:, 0, :].rearrange("p (t c) -> p t c", t=2), ACT.Copy)
                A_(v_sb[:, 2, :], PS[:, 1, 0:D], ACT.Copy).then_inc(s["b_vev"], 1)
                act.wait_ge(s["b_dm"], i + 1)
                wait(act, s["b_pt"], i)
                wait(act, s["b_res"], i)
                for t in range(GT):
                    ins = A_(Pm[:, t], dm[:, t], ACT.Exp, bias=hb[:, t:t + 1], scale=-0.5, accum_out=rs[:, t:t + 1])
                ins.then_inc(s["b_exp"], 1)
                if isinstance(i, int) and i == 0:
                    act.wait_ge(s["d_w0"], 16)
                A_(W_h[0][:, ds(i * n0, n0)], W_raw[0][:, ds(i * n0, n0)], ACT.Copy).then_inc(s["w_hi0"], 1)

        ln_hi(0)
        l0(0, False, True, True)
        with act.Fori(1, NG - 1) as i:
            l0(i, True, True, True)
        l0(NG - 1, True, True, False)
        l0(NG, True, False, False)

        def prep(c):
            def two(j):
                for u in range(2):
                    act.wait_ge(s[f"{c}_T"], j + u + 1)
                    A_(xTh[:, :, ds((j + u) * P, P)], PS[:, u, 0:D].rearrange("p (k c) -> p k c", k=KC), ACT.Copy).then_inc(s[f"{c}_hi"], 1)
            with act.Fori(0, NT // 2) as jj:
                two(jj * 2)

        def logits(L):
            def one(g, b):
                act.wait_ge(s[f"f{L}_lg"], g + 1)
                A_(lgT[:, ds(g * GW, GW)], PS[0:NE, 2 + b, 0:GW], ACT.Copy).then_inc(s[f"f{L}_lgT"], 1)
            with act.Fori(0, NG // 2) as r:
                one(2 * r, 0)
                one(2 * r + 1, 1)
            if L == 0:
                act.wait_ge(s["f0_lgt"], 1)
                A_(sc[:, :, :], PS[:, 4, 0:NT * NE].rearrange("p (j e) -> p j e", e=NE), ACT.Sigmoid).then_inc(s["f0_sig"], 1)
            else:
                act.wait_ge(s["f1_lraw"], 1)
                A_(sc[:, :, :], sc[:, :, :], ACT.Sigmoid).then_inc(s["f1_sig"], 1)

        def experts(L, gu):
            ne = 9 + L
            def body(r):
                for k in range(gu * ne):
                    n = r * (gu * ne) + k
                    b = k % 2
                    act.wait_ge(s[f"f{L}_gu"], n + 1)
                    A_(sg[:, b], PS[:, b, 0:GW], ACT.Silu).then_inc(s[f"f{L}_silu"], 1)
                    act.wait_ge(s[f"f{L}_mul"], n + 1)
                    wait(act, s[f"f{L}_dn"], n - 1)
                    A_(ah[:, b], aa[:, b], ACT.Copy).then_inc(s[f"f{L}_ah"], 1)
            turns = NG // gu
            body(0)
            with act.Fori(1, turns) as r:
                body(r)

        std(1)
        prep("c")
        logits(0)
        experts(0, 2)
        std(2)
        act.wait_ge(s["d_a1"], 16)
        A_(a1h[:, :, :], a1raw[:, :, :], ACT.Copy).then_inc(s["e_a1h"], 1)
        prep("e")

        def turn(it, p):
            for U in range(NU):
                if live(it, 2):
                    i = it - 2
                    act.wait_ge(s["e_st"], i * NU + U + 1)
                    old = (2 * U + 1 - RING) // 3
                    wait(act, s["e_avt"], i * NAV + old + 1)
                    c0 = (2 * U) % RING
                    b = 2 * (U % 2)
                    A_(PR[0:KT, c0:c0 + 2, :], PS[0:KT, b:b + 2, 0:CW], ACT.Exp).then_inc(s["e_exp"], 1)
                if U in PR_U and live(it, 0):
                    m = PR_U.index(U)
                    act.wait_ge(s["e_prev"], 3 * it + m + 1)
                    if m == 0:
                        wait(act, s["e_out"], 32 * it)
                    A_(qh[:, m], qf[p][:, m], ACT.Copy).then_inc(s["e_hi3"], 1)
                if U == VT_U and live(it, 1):
                    act.wait_ge(s["e_vt"], it)
                    wait(act, s["e_avt"], (it - 2) * NAV)
                    for kt in range(NKT):
                        ins = A_(VA[1 - p][0:KT, kt, :, 0:HD], PS[0:KT, 7, kt * P + 64:kt * P + P].rearrange("p (g d) -> p g d", g=NGQ), ACT.Copy)
                    ins.then_inc(s["e_va"], 1)
                for k, g in y_at(U):
                    if live(it, k):
                        y_raw(it - k, g, p ^ (k % 2))

        def y_raw(i, g, p):
            act.wait_ge(s["e_avt"], NAV * i + NKT * (g + 1))
            wait(act, s["e_y"], NGQ * (i - 2) + g + 1)
            A_(yr[p][:, g], PS[:, 6, 0:POS], ACT.Copy).then_inc(s["e_yr"], 1)

        act.wait_ge(s["e_kv_const"], 4)
        for it in range(4):
            turn(it, it % 2)
        with act.Fori(2, 4) as r:
            turn(2 * r, 0)
            turn(2 * r + 1, 1)
        for it in range(8, 11):
            turn(it, it % 2)
        n1 = sum(WCOLS[1]) // NG
        act.wait_ge(s["d_w1"], 16)
        with act.Fori(0, NG) as i:
            A_(W_h[1][:, ds(i * n1, n1)], W_raw[1][:, ds(i * n1, n1)], ACT.Copy).then_inc(s["w_hi1"], 1)
        std(3)
        prep("p")
        logits(1)
        experts(1, 3)

    @block.vector
    def _(dve):
        V = nc.vector
        own = Own(dve, s["dve_own"])

        def moments():
            me, mo = stats[:, :, 1], stats[:, :, 4]
            own(V.tensor_tensor(mt[:, 0], me, mo, ALU.add))
            own(V.tensor_tensor(mt[:, 1], me, mo, ALU.subtract))
            own(V.tensor_tensor(mt[:, 2], stats[:, :, 2], stats[:, :, 5], ALU.add))
            own.settle()
            own(V.tensor_scalar(mv[:, :, 0], mt[:, 0], 0.5, None, ALU.mult))
            own(V.tensor_tensor(mt[:, 3], mt[:, 1], mt[:, 1], ALU.mult))
            own.settle()
            own(V.tensor_scalar(mt[:, 0], mt[:, 3], 0.25, None, ALU.mult))
            own.settle()
            own(V.scalar_tensor_tensor(out=mv[:, :, 1], in0=mt[:, 2], scalar=1.0 / D, in1=mt[:, 0], op0=ALU.mult, op1=ALU.add))
            own.settle()

        dve.wait_ge(s["d_x"], 32)
        src = x_in[:, :, :]
        for n in range(NLV):
            sv4 = src.rearrange("p r (c t) -> p r c t", t=2)
            own(V.tensor_tensor(lo[n][:, :, :], sv4[:, :, :, 0], sv4[:, :, :, 1], ALU.add))
            if n:
                own(V.tensor_tensor(hi[n][:, :, :], sv4[:, :, :, 0], sv4[:, :, :, 1], ALU.subtract))
            own.settle()
            lv = lo[n][:, :, :].rearrange("p (r t) c -> p r t c", t=2)
            hv = hi[n][:, :, :].rearrange("p (r t) c -> p r t c", t=2)
            own(V.tensor_tensor(app[n][:, :, :], lv[:, :, 0, :], lv[:, :, 1, :], ALU.add))
            own(V.tensor_tensor(det[n][:, 0], lv[:, :, 0, :], lv[:, :, 1, :], ALU.subtract))
            if n:
                own(V.tensor_tensor(det[n][:, 1], hv[:, :, 0, :], hv[:, :, 1, :], ALU.add))
                own(V.tensor_tensor(det[n][:, 2], hv[:, :, 0, :], hv[:, :, 1, :], ALU.subtract))
            own.settle()
            src = app[n][:, :, :]
        dve.wait_ge(s["pool_hi"], 1)
        dve.wait_ge(s["d_wd"], 16 * 4 * IMGS)
        own(V.tensor_tensor_reduce(junk[:, 0:rows[2] * cols[2]], app[2][:, :, :].rearrange("p r c -> p (r c)"), wa[:, :], 1.0, 0.0, ALU.mult, ALU.add, dots[:, 9:10]))
        for n in (2, 1, 0):
            for k in range(3):
                own.settle()
                own(V.tensor_tensor_reduce(junk[:, 0:sizes[n]], det[n][:, :, :, :].rearrange("p b r c -> p (b r c)"), wd[n][:, k, :], 1.0, 0.0,
                                           ALU.mult, ALU.add, dots[:, 3 * (2 - n) + k:3 * (2 - n) + k + 1]))
        own.settle()
        V.tensor_copy(lg[:, :], dots[:, :]).then_inc(s["dots_ready"], 1)
        dve.wait_ge(s["dots_sum"], 1)
        dve.wait_ge(s["d_bias"], 16)
        for n, (a, b, f) in enumerate(((0, 3, 0.125), (3, 6, 0.25), (6, 9, 0.5), (9, 10, 0.125))):
            own(V.scalar_tensor_tensor(out=lg[:, a:b], in0=PS[:, 0, a:b], scalar=f, in1=lbias[:, a:b], op0=ALU.mult, op1=ALU.add))
        own.settle()
        l3 = lg[:, 0:9].rearrange("p (n k) -> p n k", n=3)
        e3 = wex[:, 0:9].rearrange("p (n k) -> p n k", n=3)
        own(V.tensor_reduce(wmx[:, :], l3, AX_X, ALU.max))
        own.settle()
        V.tensor_tensor(e3, l3, wmx[:, :].unsqueeze(2).broadcast_to([P, 3, 3]), ALU.subtract).then_inc(s["wex_in"], 1)
        dve.wait_ge(s["wex_ready"], 1)
        own(V.tensor_reduce(wsm[:, 0:3], e3, AX_X, ALU.add))
        own(V.tensor_scalar(wsm[:, 3:4], wex[:, 9:10], 1.0, None, ALU.add))
        own.settle()
        own(V.reciprocal(wsm[:, :], wsm[:, :]))
        own.settle()
        for n, f in enumerate((1 / 64, 1 / 16, 1 / 4)):
            own(V.tensor_scalar(wts[:, 3 * n:3 * n + 3], wex[:, 3 * n:3 * n + 3], wsm[:, n:n + 1], f, ALU.mult, ALU.mult))
        own(V.tensor_scalar(wts[:, 9:10], wsm[:, 3:4], 1 / 64, None, ALU.mult))
        own.settle()
        V.tensor_scalar(app[2][:, :, :], app[2][:, :, :], wts[:, 9:10], None, ALU.mult).then_inc(s["wts_ready"], 1)
        dve.wait_ge(s["wts_ready"], 1)
        for n in (2, 1, 0):
            c = 3 * (2 - n)
            u = app[n][:, :, :]
            lv = lo[n][:, :, :].rearrange("p (r t) c -> p r t c", t=2)
            hv = hi[n][:, :, :].rearrange("p (r t) c -> p r t c", t=2)
            own(V.scalar_tensor_tensor(out=lv[:, :, 0, :], in0=det[n][:, 0], scalar=wts[:, c:c + 1], in1=u, op0=ALU.mult, op1=ALU.add))
            own(V.scalar_tensor_tensor(out=lv[:, :, 1, :], in0=det[n][:, 0], scalar=wts[:, c:c + 1], in1=u, op0=ALU.mult, op1=ALU.subtract, reverse1=True))
            dve.wait_ge(s["dsc_ready"], 3 - n)
            own(V.scalar_tensor_tensor(out=hv[:, :, 0, :], in0=det[n][:, 1], scalar=wts[:, c + 1:c + 2], in1=dsc[n][:, :, :], op0=ALU.mult, op1=ALU.add))
            own(V.scalar_tensor_tensor(out=hv[:, :, 1, :], in0=det[n][:, 1], scalar=wts[:, c + 1:c + 2], in1=dsc[n][:, :, :], op0=ALU.mult, op1=ALU.subtract))
            own.settle()
            dst = app[n - 1][:, :, :] if n else h[:, 0:ROWS, :]
            dv = dst.rearrange("p r (c t) -> p r c t", t=2)
            own(V.tensor_tensor(dv[:, :, :, 0], lo[n][:, :, :], hi[n][:, :, :], ALU.add))
            own(V.tensor_tensor(dv[:, :, :, 1], lo[n][:, :, :], hi[n][:, :, :], ALU.subtract))
            own.settle()
        dve.sem_inc(s["img_done"], 1)
        dve.wait_ge(s["d_txt"], 16)
        with dve.Fori(0, NT) as j:
            V.bn_stats(stats[:, ds(j, 1), :].squeeze(1), h[:, ds(j, 1), :].squeeze(1)).then_inc(s["c_scan"], 1)
        dve.wait_ge(s["c_scan"], NT)
        moments()
        dve.sem_inc(s["st_ready0"], 1)

        def rstd_(n):
            dve.wait_ge(s[f"std_ready{n}"], 1)
            V.reciprocal(rstd[:, :], rstd[:, :]).then_inc(s[f"rstd_ready{n}"], 1)
            dve.wait_ge(s[f"rstd_ready{n}"], 1)

        def normalise(dst, j):
            return V.tensor_scalar(dst, h[:, ds(j, 1), :].squeeze(1), mv[:, ds(j, 1), 0:1].squeeze(1),
                                   rstd[:, ds(j, 1)], ALU.subtract, ALU.mult)

        def xn_group(i):
            wait(dve, s["b_T"], i)
            for t in range(GT):
                ins = normalise(xn[:, t], i * GT + t)
            ins.then_inc(s["b_xn"], 1)

        def ln_lo(i):
            dve.wait_ge(s["b_hi"], i + 1)
            V.tensor_tensor(xwl[:, :, 0:2 * P].rearrange("p k (t c) -> p t k c", t=2), PS[:, 4, :].rearrange("p (t k c) -> p t k c", t=2, k=KC),
                            xwh[:, :, 0:2 * P].rearrange("p k (t c) -> p t k c", t=2).bitcast(F32), ALU.subtract)
            V.tensor_tensor(xwl[:, :, 2 * P:], PS[:, 5, 0:D].rearrange("p (k c) -> p k c", k=KC),
                            xwh[:, :, 2 * P:].bitcast(F32), ALU.subtract).then_inc(s["b_x"], 1)

        def l0(i, prev, cur, nxt):
            if nxt:
                xn_group(i + 1)
            if cur:
                dve.wait_ge(s["b_qk"], i + 1)
                wait(dve, s["b_d2"], i)
                for m in range(2):
                    V.tensor_scalar(qT[:, m], PS[:, m, 0:GW], bqk0[:, m:m + 1], None, ALU.add)
                for m in range(2):
                    ins = V.tensor_scalar(km2[:, m], PS[:, 2 + m, 0:GW], bqk0[:, 2 + m:3 + m], -2.0, ALU.add, ALU.mult)
                ins.then_inc(s["b_dqk"], 1)
            if nxt:
                ln_lo(i + 1)
            if prev:
                dve.wait_ge(s["b_exp"], i)
                own(V.reciprocal(ri[:, :], rs[:, :]))
                own.settle()
                dve.wait_ge(s["b_av"], i)
                dve.wait_ge(s["b_hb"], GT * i)
                for t in range(GT):
                    j = (i - 1) * GT + t
                    hj = h[:, ds(j, 1), :].squeeze(1)
                    own(V.scalar_tensor_tensor(out=hj, in0=PS[:, 2 + t // 2, (t % 2) * D:(t % 2) * D + D], scalar=ri[:, t:t + 1], in1=hj, op0=ALU.mult, op1=ALU.add))
                own.settle()
                dve.sem_inc(s["b_res"], 1)
                for t in range(GT):
                    j = (i - 1) * GT + t
                    own(V.bn_stats(stats[:, ds(j, 1), :].squeeze(1), h[:, ds(j, 1), :].squeeze(1)))
            if cur:
                dve.wait_ge(s["b_d2"], i + 1)
                wait(dve, s["b_exp"], i)
                for t in range(GT):
                    own(V.scalar_tensor_tensor(out=dm[:, t], in0=PS[:, 6, t * P:t * P + P], scalar=0.0, in1=far_mask[:, :], op0=ALU.max, op1=ALU.add))
                own.settle()
                own(V.tensor_reduce(mn[:, :], dm[:, :, :], AX_X, ALU.min))
                own.settle()
                V.tensor_scalar(hb[:, :], mn[:, :], 0.5, None, ALU.mult).then_inc(s["b_dm"], 1)

        rstd_(0)
        dve.wait_ge(s["d_small"], 16 * 8)
        dve.wait_ge(s["d_const"], 16 * 6)
        xn_group(0)
        ln_lo(0)
        l0(0, False, True, True)
        own.loop(1, NG - 1, 1 + 3 * GT + 1, lambda i: l0(i, True, True, True))
        l0(NG - 1, True, True, False)
        l0(NG, True, False, False)
        own.settle()
        moments()
        dve.sem_inc(s["st_ready1"], 1)

        def prep(c, n, buf):
            rstd_(n)
            def xn_(j, u):
                normalise(buf[:, u], j).then_inc(s[f"{c}_xn"], 1)

            def lo_(j, u):
                dve.wait_ge(s[f"{c}_hi"], j + 1)
                V.tensor_tensor(xTl[:, :, ds(j * P, P)], PS[:, u, 0:D].rearrange("p (k c) -> p k c", k=KC),
                                xTh[:, :, ds(j * P, P)].bitcast(F32), ALU.subtract).then_inc(s[f"{c}_lo"], 1)

            xn_(0, 0)
            xn_(1, 1)
            with dve.Fori(0, NT // 2 - 1) as r:
                for u in range(2):
                    lo_(2 * r + u, u)
                    xn_(2 * r + u + 2, u)
            lo_(NT - 2, 0)
            lo_(NT - 1, 1)

        def routing(L):
            s8 = [P, NT, NE, NE]
            if L == 0:
                dve.wait_ge(s["f0_sig"], 1)
                own(V.tensor_tensor(sv[:, :, :], sc[:, :, :], cb0[:, :].unsqueeze(1).broadcast_to([P, NT, NE]), ALU.add))
                own.settle()
                pr = sv[:, :, :].rearrange("p j (q t) -> p j q t", t=2)
                hiP, loP = t1[:, :, 0:4], t2[:, :, 0:4]
                own(V.tensor_tensor(hiP, pr[:, :, :, 0], pr[:, :, :, 1], ALU.max))
                own(V.tensor_tensor(loP, pr[:, :, :, 0], pr[:, :, :, 1], ALU.min))
                own.settle()
                hp = hiP.rearrange("p j (g t) -> p j g t", t=2)
                lp = loP.rearrange("p j (g t) -> p j g t", t=2)
                own(V.tensor_tensor(t3[:, :, 0:2], hp[:, :, :, 0], hp[:, :, :, 1], ALU.max))
                own(V.tensor_tensor(t3[:, :, 2:4], hp[:, :, :, 0], hp[:, :, :, 1], ALU.min))
                own(V.tensor_tensor(t3[:, :, 4:6], lp[:, :, :, 0], lp[:, :, :, 1], ALU.max))
                own.settle()
                own(V.tensor_tensor(t3[:, :, 6:8], t3[:, :, 2:4], t3[:, :, 4:6], ALU.max))
                own.settle()
                own(V.tensor_tensor(t1[:, :, 4:6], t3[:, :, 0:2], t3[:, :, 6:8], ALU.add))
                own.settle()
                own(V.tensor_tensor(t2[:, :, 4:5], t1[:, :, 4:5], t1[:, :, 5:6], ALU.is_ge))
                own(V.tensor_tensor(t2[:, :, 5:6], t1[:, :, 4:5], t1[:, :, 5:6], ALU.is_lt))
                own.settle()
                own(V.tensor_tensor(sv[:, :, :].rearrange("p j (g q) -> p j g q", g=2), sv[:, :, :].rearrange("p j (g q) -> p j g q", g=2),
                                    t2[:, :, 4:6].unsqueeze(3).broadcast_to([P, NT, 2, 4]), ALU.mult))
                own.settle()
                key = sv
            else:
                dve.wait_ge(s["f1_lgt"], 1)
                V.tensor_tensor(sc[:, :, :], PS[:, 4, 0:NT * NE].rearrange("p (j e) -> p j e", e=NE),
                                lb1[:, :].unsqueeze(1).broadcast_to([P, NT, NE]), ALU.add).then_inc(s["f1_lraw"], 1)
                dve.wait_ge(s["f1_sig"], 1)
                key = sc
            vf = key[:, :, :].unsqueeze(2).broadcast_to(s8)
            ve = key[:, :, :].unsqueeze(3).broadcast_to(s8)
            own(V.tensor_tensor(ra[:, :, :, :], vf, ve, ALU.is_equal))
            own(V.tensor_tensor(rb_[:, :, :, :], vf, ve, ALU.is_gt))
            own.settle()
            own(V.tensor_tensor(ra[:, :, :, :].rearrange("p j e f -> p j (e f)"), ra[:, :, :, :].rearrange("p j e f -> p j (e f)"),
                                lt[:, :].unsqueeze(1).broadcast_to([P, NT, NE * NE]), ALU.mult))
            own.settle()
            own(V.tensor_tensor(ra[:, :, :, :], ra[:, :, :, :], rb_[:, :, :, :], ALU.add))
            own.settle()
            own(V.tensor_reduce(t1[:, :, :], ra[:, :, :, :], AX_X, ALU.add))
            own.settle()
            own(V.tensor_scalar(t2[:, :, :], t1[:, :, :], 1.5, None, ALU.is_lt))
            own.settle()
            own(V.tensor_tensor(t3[:, :, :], t2[:, :, :], sc[:, :, :], ALU.mult))
            own.settle()
            own(V.tensor_reduce(t1[:, :, 0:1].squeeze(2), t3[:, :, :], AX_X, ALU.add))
            own.settle()
            own(V.tensor_scalar(t1[:, :, 1:2].squeeze(2), t1[:, :, 0:1].squeeze(2), (1e-20, 1e-8)[L], None, ALU.add))
            own.settle()
            own(V.reciprocal(t1[:, :, 2:3].squeeze(2), t1[:, :, 1:2].squeeze(2)))
            own.settle()
            rcp = t1[:, :, 2:3].broadcast_to([P, NT, NE])
            if L == 0:
                own(V.tensor_tensor(cmb[:, :, 0:NE], t3[:, :, :], rcp, ALU.mult))
                own.settle()
                return
            own(V.tensor_tensor(sv[:, :, :], t3[:, :, :], rcp, ALU.mult))
            own.settle()
            own(V.tensor_reduce(tot[:, 0:NE], t2[:, :, :].rearrange("p j e -> p e j"), AX_X, ALU.add))
            own(V.tensor_reduce(tot[:, NE:2 * NE], sv[:, :, :].rearrange("p j e -> p e j"), AX_X, ALU.add))
            own.settle()
            dve.sem_inc(s["f1_tot"], 1)
            dve.wait_ge(s["f1_sum"], 1)
            own(V.tensor_scalar(t1[:, 0, :], PS[:, 5, 0:NE], 1.0, None, ALU.max))
            own.settle()
            own(V.reciprocal(t1[:, 1, :], t1[:, 0, :]))
            own.settle()
            own(V.tensor_tensor(t1[:, 2, :], PS[:, 5, NE:2 * NE], t1[:, 1, :], ALU.mult))
            own.settle()
            own(V.tensor_tensor(cmb[:, :, 0:NE], t2[:, :, :], t1[:, 2:3, :].broadcast_to([P, NT, NE]), ALU.mult))
            own.settle()

        def experts(L, gu):
            ne = 9 + L
            per = gu * ne

            def gated(n, k):
                b = k % 2
                dve.wait_ge(s[f"f{L}_silu"], n + 1)
                wait(dve, s[f"f{L}_ah"], n - 1)
                V.tensor_tensor(aa[:, b], sg[:, b], PS[:, 2 + b, 0:GW], ALU.mult).then_inc(s[f"f{L}_mul"], 1)

            def low(n, k):
                b = k % 2
                dve.wait_ge(s[f"f{L}_ah"], n + 1)
                wait(dve, s[f"f{L}_dn"], n - 1)
                V.tensor_tensor(al[:, b], aa[:, b], ah[:, b].bitcast(F32), ALU.subtract).then_inc(s[f"f{L}_al"], 1)

            def accumulate(n, g, e, k):
                b = 4 + 2 * (k % 2)
                dve.wait_ge(s[f"f{L}_dn"], n + 1)
                wait(dve, s[f"f{L}_acc"], n)
                for t in range(GT):
                    hj = h[:, ds(g * GT + t, 1), :].squeeze(1)
                    ins = V.scalar_tensor_tensor(out=hj, in0=PS[:, b + t // 2, (t % 2) * D:(t % 2) * D + D],
                                                 scalar=cmb[:, ds(g * GT + t, 1), e:e + 1].squeeze(1), in1=hj, op0=ALU.mult, op1=ALU.add)
                ins.then_inc(s[f"f{L}_acc"], 1)

            def body(r, first=False):
                for k in range(per):
                    n = r * per + k
                    gated(n, k)
                    if not first or k >= 2:
                        m = n - 2
                        kk = (k - 2) % per
                        g = (r * gu + (k - 2) // ne)
                        accumulate(m, g, (k - 2) % ne, kk)
                    low(n, k)
            assert per % 2 == 0
            body(0, True)
            with dve.Fori(1, NG // gu) as r:
                body(r)
            for k in (per, per + 1):
                n = (NG // gu - 1) * per + k
                accumulate(n - 2, NG - 1, (k - 2) % ne, k - 2)
            dve.wait_ge(s[f"f{L}_acc"], NG * ne)

        def all_stats(n, c):
            own.loop(0, NT, 1, lambda j: own(V.bn_stats(stats[:, ds(j, 1), :].squeeze(1), h[:, ds(j, 1), :].squeeze(1))))
            own.settle()
            moments()
            dve.sem_inc(s[f"st_ready{n}"], 1)

        prep("c", 1, xnc)
        routing(0)
        experts(0, 2)
        all_stats(2, "e")
        prep("e", 2, xn1)

        def turn(it, p):
            for U in range(NU):
                if U in PR_U and live(it, 0):
                    m = PR_U.index(U)
                    dve.wait_ge(s["e_pr"], 3 * it + m + 1)
                    wait(dve, s["e_split"], 3 * (it - 1))
                    if m == 2:
                        wait(dve, s["e_vt"], it - 1)
                    V.tensor_scalar(qf[p][:, m], PS[:, 7, 0:POS], bq1[:, m:m + 1], (0.25, 0.25, 1.0)[m], ALU.add, ALU.mult).then_inc(s["e_prev"], 1)
                for k, c in s_at(U):
                    if live(it, k):
                        i = it - k
                        dve.wait_ge(s["e_s"], NS * i + c + 1)
                        if c == 0:
                            wait(dve, s["e_mT"], i)
                        V.tensor_reduce(MX[:, c:c + 1], PS[:, 4 + c % 2, 0:POS], AX_X, ALU.max).then_inc(s["e_mx"], 1)
                if U == MT_U and live(it, 1):
                    i = it - 1
                    dve.wait_ge(s["e_mT"], i + 1)
                    wait(dve, s["e_mout"], 32 * i)
                    own(V.tensor_copy(Mh[:, :], PS[0:NS, 7, 0:P]))
                    own.settle()
                    V.tensor_tensor(Ml[:, :], PS[0:NS, 7, 0:P], Mh[:, :].bitcast(F32), ALU.subtract).then_inc(s["e_msplit"], 1)
                if live(it, 3):
                    i = it - 3
                    if U == SUM_U:
                        dve.wait_ge(s["e_sum"], i + 1)
                        V.reciprocal(rec[:, :], PS[0:NGQ * HPG, 7, 0:POS]).then_inc(s["e_rec"], 1)
                    if U in SB_U:
                        g = SB_U.index(U)
                        dve.wait_ge(s["e_sb"], NGQ * i + g + 1)
                        V.tensor_tensor(img(yT[:, g, :], i), yr[1 - p][:, g].rearrange("p (j c) -> p j c", j=NT),
                                        PS[:, 7, 0:POS].rearrange("p (j c) -> p j c", j=NT), ALU.mult).then_inc(s["e_y"], 1)

        dve.wait_ge(s["e_kv_const"], 4)
        for it in range(4):
            turn(it, it % 2)
        own.loop(2, 4, 2, lambda r: (turn(2 * r, 0), turn(2 * r + 1, 1)))
        for it in range(8, 11):
            turn(it, it % 2)
        dve.wait_ge(s["e_bo"], NT)
        for j in range(NT):
            dve.wait_ge(s["g_wo"], j + 1)
            V.tensor_tensor(h[:, j, :], PS[:, j % 4, 0:D], h[:, j, :], ALU.add).then_inc(s["g_res"], 1)
        dve.wait_ge(s["g_res"], NT)
        all_stats(3, "p")
        prep("p", 3, xnc)
        routing(1)
        experts(1, 3)

    @block.tensor
    def _(pe):
        M = nc.tensor.matmul

        def split3(out_, pairs, start=True, stop=True):
            n = len(pairs)
            for c, (wh, wl, xh, xl) in enumerate(pairs):
                M(out_, wh, xh, start=(start and c == 0), stop=False)
                M(out_, wl, xh, start=False, stop=False)
                ins = M(out_, wh, xl, start=False, stop=(stop and c == n - 1))
            return ins

        pe.wait_ge(s["dots_ready"], 1)
        pe.wait_ge(s["d_const"], 16 * 6)
        M(PS[:, 0, 0:10], same_img[:, :], lg[:, :], start=True, stop=True).then_inc(s["dots_sum"], 1)

        def transposes(i):
            pe.wait_ge(s["b_xn"], i + 1)
            wait(pe, s["b_x"], i)
            for t in range(GT):
                for k in range(KC):
                    c = (t % 2) * D + k * P
                    ins = nc.tensor.transpose(PS[:, 4 + t // 2, c:c + P], xn[:, t, k * P:k * P + P], ident[:, :])
            ins.then_inc(s["b_T"], 1)

        def l0(i, prev, cur, nxt):
            if cur:
                pe.wait_ge(s["b_x"], i + 1)
                wait(pe, s["b_vev"], i)
                wait(pe, s["b_res"], i - 1)
                for m in range(4):
                    c = (m % 2) * P
                    if m == 2:
                        wait(pe, s["b_res"], i - 1)
                    ins = split3(PS[:, m, 0:GW], [(qkv_h[:, m // 2, k, c:c + P], qkv_l[:, m // 2, k, c:c + P], xwh[:, k], xwl[:, k]) for k in range(KC)])
                ins.then_inc(s["b_qk"], 1)
            if prev:
                pe.wait_ge(s["b_exp"], i)
                for t in range(GT):
                    ins = nc.tensor.transpose(PS[:, 7, t * P:t * P + P], Pm[:, t], ident[:, :])
                ins.then_inc(s["b_pt"], 1)
            if cur:
                pe.wait_ge(s["b_dqk"], i + 1)
                for t in range(GT):
                    ins = split3(PS[:, t // 2, (t % 2) * D:(t % 2) * D + D],
                                 [(xwh[:, k, t * P:t * P + P], xwl[:, k, t * P:t * P + P], qkv_h[:, 2, k], qkv_l[:, 2, k]) for k in range(KC)])
                ins.then_inc(s["b_v"], 1)
            if nxt:
                transposes(i + 1)
            if prev:
                pe.wait_ge(s["b_ptev"], i)
                for t in range(GT):
                    ins = M(PS[:, 2 + t // 2, (t % 2) * D:(t % 2) * D + D], PT[:, t], v_sb[:, t], start=True, stop=True)
                ins.then_inc(s["b_av"], 1)
            if cur:
                pe.wait_ge(s["b_qs"], i + 1)
                wait(pe, s["b_dm"], i)
                for t in range(GT):
                    o_ = PS[:, 6, t * P:t * P + P]
                    c = slice(t * P, t * P + P)
                    M(o_, ones[:, :], ks[:, c], start=True, stop=False)
                    M(o_, qs[:, c], ones[:, :], start=False, stop=False)
                    M(o_, qT[:, 0, c], km2[:, 0, c], start=False, stop=False)
                    ins = M(o_, qT[:, 1, c], km2[:, 1, c], start=False, stop=True)
                ins.then_inc(s["b_d2"], 1)

        pe.wait_ge(s["qkv_split"], 1)
        pe.wait_ge(s["const_pool"], 3)
        transposes(0)
        l0(0, False, True, True)
        l0(1, True, True, True)
        with pe.Fori(2, NG - 1) as i:
            l0(i, True, True, True)
        l0(NG - 1, True, True, False)
        l0(NG, True, False, False)

        def prep(c, buf):
            def one(j, u):
                pe.wait_ge(s[f"{c}_xn"], j + 1)
                wait(pe, s[f"{c}_lo"], j - 1)
                for k in range(KC):
                    ins = nc.tensor.transpose(PS[:, u, k * P:k * P + P], buf[:, u, k * P:k * P + P], ident[:, :])
                ins.then_inc(s[f"{c}_T"], 1)
            one(0, 0)
            one(1, 1)
            with pe.Fori(1, NT // 2) as r:
                one(2 * r, 0)
                one(2 * r + 1, 1)

        def logits(L, c):
            pe.wait_ge(s[f"{c}_lo"], NT)
            pe.wait_ge(s[f"{c}_hi"], NT)
            pe.wait_ge(s["rw_split0"], 2)

            def one(g, b):
                wait(pe, s[f"f{L}_lgT"], g - 1)
                split3(PS[0:NE, 2 + b, 0:GW], [(rwh[L][:, k], rwl[L][:, k], xTh[:, k, ds(g * GW, GW)], xTl[:, k, ds(g * GW, GW)]) for k in range(KC)])\
                    .then_inc(s[f"f{L}_lg"], 1)
            one(0, 0)
            one(1, 1)
            with pe.Fori(1, NG // 2) as r:
                one(2 * r, 0)
                one(2 * r + 1, 1)
            pe.wait_ge(s[f"f{L}_lgT"], NG)
            for j in range(NT):
                ins = nc.tensor.transpose(PS[:, 4, j * NE:j * NE + NE], lgT[:, j * P:j * P + P], ident[0:NE, 0:NE])
            ins.then_inc(s[f"f{L}_lgt"], 1)
            if L == 1:
                pe.wait_ge(s["f1_tot"], 1)
                M(PS[:, 5, 0:2 * NE], ones[:, :], tot[:, :], start=True, stop=True).then_inc(s["f1_sum"], 1)

        def experts(L, gu):
            ne = 9 + L
            per = gu * ne
            Gh, Gl = w_part(W_h[L], L, 0), w_part(W_l[L], L, 0)
            Uh, Ul = w_part(W_h[L], L, 1), w_part(W_l[L], L, 1)
            Dh, Dl = w_part(W_h[L], L, 2), w_part(W_l[L], L, 2)

            def gate_up(n, g, e, k):
                b = k % 2
                wait(pe, s[f"f{L}_mul"], n - 1)
                xs = [(xTh[:, c, ds(g * GW, GW)], xTl[:, c, ds(g * GW, GW)]) for c in range(KC)]
                split3(PS[:, b, 0:GW], [(Gh[:, e, c], Gl[:, e, c], *xs[c]) for c in range(KC)])
                split3(PS[:, 2 + b, 0:GW], [(Uh[:, e, c], Ul[:, e, c], *xs[c]) for c in range(KC)]).then_inc(s[f"f{L}_gu"], 1)

            def down(n, e, k):
                b = k % 2
                pe.wait_ge(s[f"f{L}_al"], n + 1)
                wait(pe, s[f"f{L}_acc"], n - 1)
                for t in range(GT):
                    c = slice(t * P, t * P + P)
                    ins = split3(PS[:, 4 + 2 * b + t // 2, (t % 2) * D:(t % 2) * D + D], [(ah[:, b, c], al[:, b, c], Dh[:, e], Dl[:, e])])
                ins.then_inc(s[f"f{L}_dn"], 1)

            def body(r, first=False):
                for k in range(per):
                    n = r * per + k
                    gate_up(n, r * gu + k // ne, k % ne, k)
                    if not first or k >= 1:
                        down(n - 1, (k - 1) % ne, (k - 1) % per)

            body(0, True)
            with pe.Fori(1, NG // gu) as r:
                body(r)
            down(NG * ne - 1, ne - 1, per - 1)

        prep("c", xnc)
        logits(0, "c")
        pe.wait_ge(s["w_split0"], NG)
        experts(0, 2)
        prep("e", xn1)

        last = [None]

        def wait_misc():
            if last[0] is not None:
                wait(pe, s[last[0][0]], last[0][1])

        def project(i, m):
            wait_misc()
            split3(PS[:, 7, 0:POS].rearrange("p (j c) -> p j c", j=NT),
                   [(a1h[:, k, m * P:m * P + P], a1l[:, k, m * P:m * P + P], img(xTh[:, k, :], i), img(xTl[:, k, :], i)) for k in range(KC)]).then_inc(s["e_pr"], 1)
            last[0] = ("e_prev", 3 * i + m + 1)

        def turn(it, p):
            for U in range(NU):
                sc_ = [(k, c) for k, c in s_at(U) if live(it, k)]

                def score_max():
                    if not sc_:
                        return
                    k, c = sc_.pop(0)
                    i = it - k
                    q = p ^ (k % 2)
                    if c % (NS // 2) == 0:
                        pe.wait_ge(s[f"e_in{c // (NS // 2)}"], 16 * 6 * (i + 1))
                    wait(pe, s["e_mx"], NS * i + c - 1)
                    M(PS[:, 4 + c % 2, 0:POS], QS[q][0:MROW, c * P:c * P + P], KS[q][0:MROW, c // 9 * POS:c // 9 * POS + POS],
                      start=True, stop=True).then_inc(s["e_s"], 1)

                if live(it, 2):
                    i = it - 2
                    if U == 0:
                        pe.wait_ge(s["e_min"], 16 * (i + 1))
                    wait(pe, s["e_exp"], i * NU + U - 1)
                    for n in (2 * U, 2 * U + 1):
                        g, kt, cc = n // 9, n % 9 // 3, n % 3
                        ins = M(PS[0:KT, n % 4, 0:CW], KS[p][:, g * POS + kt * KT:g * POS + kt * KT + KT],
                                QS[p][:, g * HQ + cc * CW:g * HQ + cc * CW + CW], start=True, stop=True)
                    ins.then_inc(s["e_st"], 1)
                score_max()
                for k, m in av_at(U):
                    if live(it, k):
                        values(it - k, m, p ^ (k % 2))
                if U in PR_U and live(it, 0):
                    project(it, PR_U.index(U))
                if U == VT_U and live(it, 1):
                    pe.wait_ge(s["e_prev"], 3 * it)
                    wait_misc()
                    for kt in range(NKT):
                        ins = nc.tensor.transpose(PS[0:KT, 7, kt * P:kt * P + P], qf[1 - p][:, 2, kt * KT:kt * KT + KT], ident[:, :])
                    ins.then_inc(s["e_vt"], 1)
                    last[0] = ("e_va", it)
                if U == MT_U and live(it, 1):
                    pe.wait_ge(s["e_mx"], NS * it)
                    wait_misc()
                    nc.tensor.transpose(PS[:, 7, 0:P], MX[:, :], ident[:, :]).then_inc(s["e_mT"], 1)
                    last[0] = ("e_msplit", it)
                if live(it, 3):
                    i = it - 3
                    if U == SUM_U:
                        pe.wait_ge(s["e_yr"], NGQ * (i + 1))
                        wait_misc()
                        for g in range(NGQ):
                            ins = M(PS[0:NGQ * HPG, 7, 0:POS], gather[:, g], yr[1 - p][:, g], start=(g == 0), stop=(g == NGQ - 1))
                        ins.then_inc(s["e_sum"], 1)
                        last[0] = ("e_rec", i + 1)
                    if U in SB_U:
                        g = SB_U.index(U)
                        wait_misc()
                        M(PS[:, 7, 0:POS], spread[:, g], rec[:, :], start=True, stop=True).then_inc(s["e_sb"], 1)
                        last[0] = ("e_y", NGQ * i + g + 1)
                score_max()

        def values(i, m, p):
            g, kt = m // NKT, m % NKT
            pe.wait_ge(s["e_exp"], i * NU + (3 * m + 2) // 2 + 1)
            if m == 0:
                pe.wait_ge(s["e_va"], i + 1)
            if kt == 0:
                wait(pe, s["e_yr"], NGQ * i + g)
            c0 = (3 * m) % RING
            for hh in range(HPG):
                ins = M(PS[32 * hh:32 * hh + 32, 6, 0:POS], VA[p][:, kt, g, :],
                        PR[:, c0:c0 + 3, :].rearrange("p c w -> p (c w)")[:, hh * POS:hh * POS + POS],
                        start=(kt == 0), stop=(kt == NKT - 1), tile_position=(0, 32 * hh))
            ins.then_inc(s["e_avt"], 1)

        pe.wait_ge(s["e_a1"], 1)
        pe.wait_ge(s["e_kv_const"], 4)
        pe.wait_ge(s["d_wo"], 48)
        pe.wait_ge(s["e_lo"], NT)
        pe.wait_ge(s["e_hi"], NT)
        for it in range(4):
            turn(it, it % 2)
        with pe.Fori(2, 4) as r:
            last[0] = ("e_msplit", 2 * r - 1)
            turn(2 * r, 0)
            turn(2 * r + 1, 1)
        last[0] = ("e_msplit", 7)
        for it in range(8, 11):
            turn(it, it % 2)
        pe.wait_ge(s["e_y"], NGQ * IMGS)
        for j in range(NT):
            wait(pe, s["g_res"], j - 3)
            for g in range(NGQ):
                ins = M(PS[:, j % 4, 0:D], yT[:, g, j * P:j * P + P], wo[:, g, :], start=(g == 0), stop=(g == NGQ - 1))
            ins.then_inc(s["g_wo"], 1)
        prep("p", xnc)
        logits(1, "p")
        pe.wait_ge(s["w_split1"], NG)
        experts(1, 3)

    ctx.close()


PR_U = [0, 1, 2]
VT_U = 3
MT_U = 13
SUM_U = 5
SB_U = [8, 9, 10, 11]
S_LEAD = 10


def s_at(U):
    c = S_LEAD + 2 * U
    return [(1, c), (1, c + 1)] if c < NS else [(0, c - NS), (0, c - NS + 1)]


def av_at(U):
    at = [(3 * m + 2) // 2 + 2 for m in range(NAV)]
    return [(3, m) for m in range(NAV) if at[m] == U + NU] + [(2, m) for m in range(NAV) if at[m] == U]


def y_at(U):
    return [(k, m // NKT) for k, m in av_at(U) if m % NKT == NKT - 1]


def live(it, back):
    return not isinstance(it, int) or 0 <= it - back < IMGS


def kernel(x, txt, L0_tok_Wa, L0_tok_ba, L0_tok_Wd1, L0_tok_bd1, L0_tok_Wd2, L0_tok_bd2, L0_tok_Wd3, L0_tok_bd3,
           L0_attn_Wq, L0_attn_bq, L0_attn_Wk, L0_attn_bk, L0_attn_Wv, L0_attn_bv,
           L0_ffn_router_weight, L0_ffn_correction_bias, L0_ffn_w_gate, L0_ffn_w_up, L0_ffn_w_down,
           L0_ffn_sw_gate, L0_ffn_sw_up, L0_ffn_sw_down,
           L1_attn_Wq, L1_attn_bq, L1_attn_Wk, L1_attn_bk, L1_attn_Wv, L1_attn_bv, L1_attn_Wo, L1_attn_bo,
           L1_ffn_gate_w, L1_ffn_lb_bias, L1_ffn_expert_gate_w, L1_ffn_expert_up_w, L1_ffn_expert_down_w,
           L1_ffn_shared_gate_w, L1_ffn_shared_up_w, L1_ffn_shared_down_w):
    import numpy as np
    import concourse.bacc as bacc
    from concourse.bass_utils import run_bass_kernel_spmd

    f = lambda a: np.asarray(a)
    arr = {}
    arr["x"] = f(x).reshape(P, ROWS, SIDE)
    arr["txt"] = f(txt).reshape(IMGS, TXT_T, RG, D).transpose(0, 2, 1, 3).reshape(P, TXT_T, D)
    for n, w in enumerate((L0_tok_Wd3, L0_tok_Wd2, L0_tok_Wd1)):
        r, c = ROWS >> (n + 1), SIDE >> (n + 1)
        arr[f"wd{n}"] = f(w).reshape(3, RG, r, c, 3).transpose(1, 4, 0, 2, 3).reshape(RG, 3, 3 * r * c)
    arr["wa"] = f(L0_tok_Wa).reshape(RG, (ROWS // 8) * (SIDE // 8))
    arr["lbias"] = np.concatenate([f(L0_tok_bd1), f(L0_tok_bd2), f(L0_tok_bd3), f(L0_tok_ba)])[None]
    p = np.arange(P)
    consts = np.zeros((P, 3, P), np.float32)
    consts[:, 0] = np.eye(P)
    consts[:, 1] = p[:, None] // RG == p[None, :] // RG
    consts[:, 2] = np.where(p[:, None] % RG == p[None, :] % RG, 0.0, BIG)
    arr["consts"] = consts
    gather = np.zeros((P, NGQ, NGQ * HPG), np.float32)
    spread = np.zeros((NGQ * HPG, NGQ, P), np.float32)
    for g in range(NGQ):
        for hh in range(HPG):
            gather[32 * hh + HD, g, HPG * g + hh] = 1.0
            spread[HPG * g + hh, g, 32 * hh:32 * hh + 32] = 1.0
    arr["gather"], arr["spread"] = gather, spread
    arr["lt"] = (np.arange(NE)[None, :] < np.arange(NE)[:, None]).astype(np.float32).reshape(1, NE * NE)

    def rows_in(w):
        return w.reshape(KC, P, w.shape[-1]).transpose(1, 0, 2)

    arr["qkv0"] = np.stack([rows_in(f(w).T) for w in (L0_attn_Wq, L0_attn_Wk, L0_attn_Wv)], 1)
    arr["bqk0"] = np.stack([f(L0_attn_bq)[:P], f(L0_attn_bq)[P:], f(L0_attn_bk)[:P], f(L0_attn_bk)[P:]], 1)
    arr["bv0"] = f(L0_attn_bv)[None]
    arr["cb0"] = f(L0_ffn_correction_bias)[None]
    arr["lb1"] = f(L1_ffn_lb_bias)[None]
    arr["bo1"] = f(L1_attn_bo)[None]
    arr["rw0"] = rows_in(f(L0_ffn_router_weight).T)
    arr["rw1"] = rows_in(f(L1_ffn_gate_w).T)

    def ffn(gate, up, down):
        ge = lambda w: w.reshape(w.shape[0], KC, P, P).transpose(2, 0, 1, 3).reshape(P, -1)
        return np.concatenate([ge(gate), ge(up), down.transpose(1, 0, 2).reshape(P, -1)], 1)

    arr["w0"] = ffn(np.concatenate([f(L0_ffn_w_gate), f(L0_ffn_sw_gate)[None]]),
                    np.concatenate([f(L0_ffn_w_up), f(L0_ffn_sw_up)[None]]),
                    np.concatenate([f(L0_ffn_w_down), f(L0_ffn_sw_down)[None]]))
    two = lambda w: w.reshape(2, P, D)
    arr["w1"] = ffn(np.concatenate([f(L1_ffn_expert_gate_w), two(f(L1_ffn_shared_gate_w))]).transpose(0, 2, 1),
                    np.concatenate([f(L1_ffn_expert_up_w), two(f(L1_ffn_shared_up_w))]).transpose(0, 2, 1),
                    np.concatenate([f(L1_ffn_expert_down_w), f(L1_ffn_shared_down_w).reshape(D, 2, P).transpose(1, 0, 2)]).transpose(0, 2, 1))
    arr["a1"] = rows_in(np.concatenate([f(L1_attn_Wq), f(L1_attn_Wk), f(L1_attn_Wv)]).T)
    arr["bq1"] = np.stack([f(L1_attn_bq)[:P], f(L1_attn_bq)[P:], np.concatenate([f(L1_attn_bk), f(L1_attn_bv)])], 1)
    wo = np.zeros((HPG, 32, NGQ, D), np.float32)
    wo[:, 0:HD] = f(L1_attn_Wo).T.reshape(NGQ, HPG, HD, D).transpose(1, 2, 0, 3)
    arr["wo1"] = wo.reshape(P, NGQ, D)

    nc = bacc.Bacc("TRN2", target_bir_lowering=False, num_devices=1)
    ins, A = {}, {}
    for name, a in arr.items():
        a = np.ascontiguousarray(a)
        ins["in_" + name] = a
        A[name] = nc.dram_tensor("in_" + name, a.shape, mybir.dt.from_np(a.dtype), kind="ExternalInput").ap()
    out = nc.dram_tensor("out_tokens", (P, NT, D), F32, kind="ExternalOutput").ap()
    build(nc, A, out)
    got = run_bass_kernel_spmd(nc, [ins], core_ids=[0]).results[0]["out_tokens"]
    y = np.asarray(got).reshape(IMGS, RG, NT, D)
    image = y[:, :, :ROWS].reshape(IMGS, SIDE, D)
    text = y[:, :, ROWS:].transpose(0, 2, 1, 3).reshape(IMGS, TXT_T * RG, D)
    return np.concatenate([image, text], 1)
```

```python
from contextlib import ExitStack

import concourse.bass as bass
from concourse import mybir

ALU = mybir.AluOpType
ACT = mybir.ActivationFunctionType
AX_X = mybir.AxisListType.X
F32 = mybir.dt.float32
F32R = mybir.dt.float32r
ds = bass.ds

P = 128
IMGS = 8
RG = P // IMGS
SIDE = 256
D = 256
KC = D // P
ROWS = SIDE // RG
TXT_T = 2
NT = ROWS + TXT_T
TOK = NT * P
POS = TOK // IMGS
GT = 3
NG = NT // GT
GW = GT * P
REST = NT - GT
NE = 8
LN_EPS = 1e-5
BIG = 3.0e38
NGQ, HPG, HD = 4, 4, 16
HQ = HPG * POS
KT = 96
NKT = POS // KT
CW = 384
NCH = NGQ * NKT * (HQ // CW)
NU = NCH // 2
RING = 12
NS = NGQ * HQ // P
MROW = 96
NSH = NS // 2
NAV = NGQ * NKT
WCOLS = {0: (9 * KC * P, 9 * KC * P, 9 * D), 1: (10 * KC * P, 10 * KC * P, 10 * D)}


def wait(eng, sem, value):
    if isinstance(value, int) and value <= 0:
        return
    eng.wait_ge(sem, value)


class Own:

    def __init__(self, eng, sem):
        self.eng, self.sem, self.n, self.base = eng, sem, 0, 0

    def __call__(self, ins):
        ins.then_inc(self.sem, 1)
        self.n += 1

    def settle(self):
        self.eng.wait_ge(self.sem, self.base + self.n)

    def loop(self, lo, hi, per, body):
        start = self.base + self.n
        with self.eng.Fori(lo, hi) as i:
            self.base, self.n = start + (i - lo) * per, 0
            body(i)
            assert self.n == per, (self.n, per)
        self.base, self.n = start + (hi - lo) * per, 0


def build(nc, A, out):
    ctx = ExitStack()
    base0 = 16512
    end = 229344
    top = [base0]

    def at(name, shape, dt, off):
        size = 4
        for n in shape[1:]:
            size *= n
        assert off % 32 == 0 and off + size <= end, (name, off, size, end)
        return nc.alloc_sbuf_tensor_at(name, shape, dt, offset=off)

    def keep(name, shape, dt=F32):
        size = 4
        for n in shape[1:]:
            size *= n
        t = at(name, shape, dt, top[0])
        top[0] += (size + 31) // 32 * 32
        return t

    h = keep("h", [P, NT, D])
    xTh = keep("xTh", [P, KC, TOK], F32R)
    xTl = keep("xTl", [P, KC, TOK], F32R)
    ident = keep("ident", [P, P])
    same_img = keep("same_img", [P, P])
    far_mask = keep("far_mask", [P, P])
    spread = keep("spread", [P, 2, P])
    halves = keep("halves", [P, 2])
    ones = keep("ones", [P, P])
    stats = keep("stats", [P, NT, 6])
    mv = keep("mv", [P, NT, 2])
    mt = keep("mt", [P, 4, NT])
    rstd = keep("rstd", [P, NT])
    nmr = keep("nmr", [P, NT])
    minus_half = keep("minus_half", [P, 1])
    bqk0 = keep("bqk0", [P, 4])
    bv0 = keep("bv0", [P, D])
    bq1 = keep("bq1", [P, 3])
    bo1 = keep("bo1", [P, D])
    cb0 = keep("cb0", [P, NE])
    lb1 = keep("lb1", [P, NE])
    rw = [keep(f"rw{x}", [P, KC, NE]) for x in range(2)]
    rwh = [keep(f"rwh{x}", [P, KC, NE], F32R) for x in range(2)]
    rwl = [keep(f"rwl{x}", [P, KC, NE], F32R) for x in range(2)]
    cmb = keep("cmb", [P, NT, 10])
    R1 = top[0]

    o = [R1]

    def seq(name, shape, dt=F32, cur=o):
        size = 4
        for n in shape[1:]:
            size *= n
        t = at(name, shape, dt, cur[0])
        cur[0] += (size + 31) // 32 * 32
        return t

    NLV = 3
    rows = [ROWS >> (n + 1) for n in range(NLV)]
    cols = [SIDE >> (n + 1) for n in range(NLV)]
    x_in = seq("x_in", [P, ROWS, SIDE])
    lo = [seq(f"lo{n}", [P, 2 * rows[n], cols[n]]) for n in range(NLV)]
    hi = [seq(f"hi{n}", [P, 2 * rows[n], cols[n]]) for n in range(NLV)]
    app = [seq(f"app{n}", [P, rows[n], cols[n]]) for n in range(NLV)]
    det = [seq(f"det{n}", [P, 3, rows[n], cols[n]]) for n in range(NLV)]
    sizes = [3 * rows[n] * cols[n] for n in range(NLV)]
    wd0_at = o[0]
    wd0 = seq("wd0", [P, 3, sizes[0]])
    wd0_end = o[0]
    dsc = [seq(f"dsc{n}", [P, rows[n], cols[n]]) for n in range(NLV)]
    NWS = 3 * sizes[1] + 3 * sizes[2] + rows[2] * cols[2]
    wsmall = seq("wsmall", [RG, NWS])
    rep = seq("rep", [RG, P])
    junk = seq("junk", [P, sizes[0]])
    d1s = junk[:, 0:rows[0] * cols[0]].rearrange("p (r c) -> p r c", r=rows[0])
    dots = seq("dots", [P, 10])
    lg = seq("lg", [P, 10])
    lbias = seq("lbias", [P, 10])
    wmx = seq("wmx", [P, NLV])
    wex = seq("wex", [P, 10])
    wsm = seq("wsm", [P, 4])
    wts = seq("wts", [P, 10])

    wb = [base0 + NT * D * 4]
    qkv_raw = seq("qkv_raw", [P, 3, KC, D], cur=wb)
    qkv_h = seq("qkv_h", [P, 3, KC, D], F32R, cur=wb)
    qkv_l = seq("qkv_l", [P, 3, KC, D], F32R, cur=wb)
    prod = seq("prod", [P, sizes[0]], cur=wb)
    assert wb[0] <= base0 + NT * D * 4 + 2 * KC * TOK * 4
    FW = 3 * 10 * D * 4
    wk = [R1 + 3 * FW]
    xwh = seq("xwh", [P, KC, GW], F32R, cur=wk)
    xwl = seq("xwl", [P, KC, GW], F32R, cur=wk)
    xn = seq("xn", [P, GT, D], cur=wk)
    qT = seq("qT", [P, KC, GW], cur=wk)
    km2 = seq("km2", [P, KC, GW], cur=wk)
    qsq = seq("qsq", [P, KC, GW], cur=wk)
    ksq = seq("ksq", [P, KC, GW], cur=wk)
    qs = seq("qs", [P, GW], cur=wk)
    ks = seq("ks", [P, GW], cur=wk)
    v_sb = seq("v_sb", [P, GT, D], cur=wk)
    dm = seq("dm", [P, GT, P], cur=wk)
    Pm = seq("Pm", [P, GT, P], cur=wk)
    PT = seq("PT", [P, GT, P], cur=wk)
    mn = seq("mn", [P, GT], cur=wk)
    hb = seq("hb", [P, GT], cur=wk)
    rs = seq("rs", [P, GT], cur=wk)
    ri = seq("ri", [P, GT], cur=wk)

    W_raw, W_h, W_l = [], [], []
    assert wd0_at <= R1 + 2 * FW and R1 + 2 * FW + 4 * sum(WCOLS[0]) <= wd0_end
    for L in range(2):
        n = sum(WCOLS[L])
        h_, l_, r_ = ((0, 1, 2), (1, 2, 0))[L]
        W_h.append(at(f"W{L}h", [P, n], F32R, R1 + h_ * FW))
        W_l.append(at(f"W{L}l", [P, n], F32R, R1 + l_ * FW))
        W_raw.append(at(f"W{L}raw", [P, n], F32, R1 + r_ * FW))

    def w_part(t, L, part):
        ne = 9 + L
        a = sum(WCOLS[L][:part])
        v = t[:, a:a + WCOLS[L][part]]
        return v.rearrange("p (e k i) -> p e k i", e=ne, k=KC) if part < 2 else v.rearrange("p (e d) -> p e d", e=ne)

    fk = [R1 + 3 * FW]
    xnc = seq("xnc", [P, 2, GT, D], cur=fk)
    sc = seq("sc", [P, NT, NE], cur=fk)
    sv = seq("sv", [P, NT, NE], cur=fk)
    ra = seq("ra", [P, NT, NE, NE], cur=fk)
    t1 = seq("t1", [P, NT, NE], cur=fk)
    t2 = seq("t2", [P, NT, NE], cur=fk)
    t3 = seq("t3", [P, NT, NE], cur=fk)
    tot = seq("tot", [P, 2 * NE], cur=fk)
    hk = [fk[0]]
    sg = seq("sg", [P, 2, GW], cur=hk)
    aa = seq("aa", [P, 2, GW], cur=hk)
    ah = seq("ah", [P, 2, GW], F32R, cur=hk)
    al = seq("al", [P, 2, GW], F32R, cur=hk)

    k1 = [R1]
    QS = [seq(f"QS{p}", [P, NGQ * HQ], F32R, cur=k1) for p in range(2)]
    KS = [seq(f"KS{p}", [P, NGQ * POS], F32R, cur=k1) for p in range(2)]
    PR = seq("PR", [P, RING, CW], cur=k1)
    VA = [seq(f"VA{p}", [P, NKT, NGQ, 32], cur=k1) for p in range(2)]
    qf = [seq(f"qf{p}", [P, 3, POS], cur=k1) for p in range(2)]
    qh = seq("qh", [P, 3, POS], F32R, cur=k1)
    ql = seq("ql", [P, 3, POS], F32R, cur=k1)
    MX = seq("MX", [P, 2, P], cur=k1)
    Mh = seq("Mh", [NSH, 2, P], F32R, cur=k1)
    Ml = seq("Ml", [NSH, 2, P], F32R, cur=k1)
    xn1 = at("xn1", [P, 2, GT, D], F32, k1[0])
    yr = [seq(f"yr{p}", [P, NGQ, POS], cur=k1) for p in range(2)]
    SW = NGQ * HPG * POS // P
    sm = seq("sm", [P, SW], cur=k1)
    rec = seq("rec", [P, SW], cur=k1)
    neg1 = at("neg1", [2, NGQ * POS], F32, k1[0])
    assert k1[0] >= R1 + 3 * FW
    yT = seq("yT", [P, NGQ // 2, TOK], cur=k1)

    ak = [max(k1[0], o[0], wk[0], hk[0])]
    recb = at("recb", [P, NGQ, POS], F32, ak[0])
    a1raw = seq("a1raw", [P, KC, 3 * P], cur=ak)
    lgT = seq("lgT", [NE, 2, GW], cur=ak)
    assert ak[0] - 4 * NGQ * POS >= max(k1[0], o[0], wk[0], hk[0])
    xnp = at("xnp", [P, 2, GT, D], F32, ak[0])
    a1h = seq("a1h", [P, KC, 3 * P], F32R, cur=ak)
    a1l = seq("a1l", [P, KC, 3 * P], F32R, cur=ak)
    wo = seq("wo", [P, NGQ // 2, D], cur=ak)
    assert 6 * D * 4 <= 2 * KC * 3 * P * 4

    PS = ctx.enter_context(nc.psum_tensor("PS", [P, 8, 512], F32))
    scrH = nc.dram_tensor("scrH", (IMGS, P, 3, POS), F32, kind="Internal").ap()
    scrL = nc.dram_tensor("scrL", (IMGS, P, 3, POS), F32, kind="Internal").ap()
    scrS = nc.dram_tensor("scrS", (IMGS, HPG, NGQ, POS), F32, kind="Internal").ap()
    scrR = nc.dram_tensor("scrR", (IMGS, HPG, NGQ, POS), F32, kind="Internal").ap()
    scrM = nc.dram_tensor("scrM", (IMGS, 2, NS, P), F32, kind="Internal").ap()

    S = {}

    def sem(name):
        if name not in S:
            S[name] = ctx.enter_context(nc.semaphore(name))
        return S[name]

    names = """d_x0 d_x1 prod_ready dot_ready det_ready d_txt d_const d_wd d_wd0 d_wd1 d_wd2 d_bias d_qkv d_small d_w0 d_w1 d_a1 d_wo d_out
        dve_own act_own pool_own var_ready std_ready rstd_ready
        pool_hi ws_ready hv_ready dots_ready dots_sum wex_in wex_ready wts_ready dsc_ready img_done
        const_pool qkv_hi qkv_split rw_split0 rw_split1
        b_xn b_T b_hi b_x b_qk b_dqk b_aqk b_qs b_hb b_v b_vev b_d2 b_dm b_exp b_pt b_ptev b_av b_res
        w_hi0 w_split0 w_hi1 w_split1
       
        e_const e_a1h e_a1 e_bo
        e_pr e_prev e_split e_out e_in0 e_in1 e_vt e_va e_s e_mx e_mT e_msplit e_mout e_min0 e_min1
        e_st e_exp e_avt e_yr e_so e_sums e_ro e_rb e_rec p_nm e_y e_yt e_sb e_yl e_hi3
        g_wo g_res""".split()
    for n in names:
        sem(n)
    for c in "cep":
        for n in ("xn", "T", "hi", "lo"):
            sem(f"{c}_{n}")
    for L in range(2):
        for n in ("lg", "lgT", "lgt", "st", "sig", "lraw", "tot", "sum", "cmb", "gu", "silu", "mul", "ah", "al", "dn", "acc"):
            sem(f"f{L}_{n}")
    assert len(S) < 200, len(S)
    s = S
    block = ctx.enter_context(nc.Block())

    def group_ps(bank):
        return PS[:, bank:bank + 2, :].rearrange("p b (t c) -> p (b t) c", t=2)[:, 0:GT, :]

    def img(t, i):
        return t.rearrange("p (j c) -> p j c", j=NT)[:, :, ds(i * RG, RG)]

    @block.sync
    def _(sp):
        sp.dma_start(wsmall[:, :], A["wsmall"]).then_inc(s["d_wd"], 16)
        sp.dma_start(rep[:, :], A["rep"]).then_inc(s["d_wd"], 16)
        for n in range(2):
            sp.dma_start(x_in[:, n * 8:n * 8 + 8, :], A["x"][:, n * 8:n * 8 + 8, :]).then_inc(s[f"d_x{n}"], 16)
        sp.dma_start(h[:, ROWS:NT, :], A["txt"]).then_inc(s["d_txt"], 16)
        for n, t in enumerate((ident, same_img, far_mask)):
            sp.dma_start(t[:, :], A["consts"][:, n, :]).then_inc(s["d_const"], 16)
        sp.dma_start(spread[:, :, :], A["spread"]).then_inc(s["d_const"], 16)
        sp.dma_start(halves[:, :], A["halves"]).then_inc(s["d_const"], 16)
        sp.dma_start(lbias[:, :], A["lbias"].broadcast_to([P, 10])).then_inc(s["d_bias"], 16)
        sp.dma_start(qkv_raw[:, :, :, :], A["qkv0"]).then_inc(s["d_qkv"], 16)
        sp.dma_start(bqk0[:, :], A["bqk0"]).then_inc(s["d_small"], 16)
        sp.dma_start(bv0[:, :], A["bv0"].broadcast_to([P, D])).then_inc(s["d_small"], 16)
        sp.dma_start(bq1[:, :], A["bq1"]).then_inc(s["d_small"], 16)
        sp.dma_start(bo1[:, :], A["bo1"].broadcast_to([P, D])).then_inc(s["d_small"], 16)
        sp.dma_start(cb0[:, :], A["cb0"].broadcast_to([P, NE])).then_inc(s["d_small"], 16)
        sp.dma_start(lb1[:, :], A["lb1"].broadcast_to([P, NE])).then_inc(s["d_small"], 16)
        for L in range(2):
            sp.dma_start(rw[L][:, :, :], A[f"rw{L}"]).then_inc(s["d_small"], 16)
        sp.dma_start(a1raw[:, :, :], A["a1"]).then_inc(s["d_a1"], 16)
        sp.dma_start(wo[:, :, :], A["wo1"]).then_inc(s["d_wo"], 16)
        sp.wait_ge(s["dots_ready"], 1)
        sp.dma_start(W_raw[0][:, :], A["w0"]).then_inc(s["d_w0"], 16)

        def minus_ones(p):
            sp.dma_start(KS[p][MROW:MROW + 2, :].bitcast(F32), neg1[:, :]).then_inc(s["d_wo"], 16)

        def stack_out(i):
            sp.wait_ge(s["e_split"], 3 * (i + 1))
            sp.dma_start(scrH[ds(i, 1)].rearrange("o p m q -> (o p) m q"), qh[:, :, :].bitcast(F32)).then_inc(s["e_out"], 16)
            sp.dma_start(scrL[ds(i, 1)].rearrange("o p m q -> (o p) m q"), ql[:, :, :].bitcast(F32)).then_inc(s["e_out"], 16)

        def stack_in(i, p, m):
            if m == 0:
                sp.wait_ge(s["e_out"], 32 * (i + 1))
            if not (isinstance(i, int) and i < 2):
                sp.wait_ge(s["e_st"], (i - 2) * NU + NU // 2 * (m + 1))
            for n, src in enumerate((scrH, scrH, scrL)):
                sp.dma_start(QS[p][n * HD:n * HD + HD, m * 8 * POS:(m + 1) * 8 * POS].bitcast(F32).rearrange("d (h q) -> d h q", h=8),
                             src[ds(i, 1), :, m, :].rearrange("o (h d) q -> d (o h) q", d=HD)).then_inc(s[f"e_in{m}"], 16)
            for n, src in enumerate((scrH, scrL, scrH)):
                sp.dma_start(KS[p][n * HD:n * HD + HD, m * 2 * POS:(m + 1) * 2 * POS].bitcast(F32).rearrange("d (g q) -> d g q", g=2),
                             src[ds(i, 1), m * 2 * HD:(m + 1) * 2 * HD, 2, :].rearrange("o (g d) q -> d (o g) q", d=HD)).then_inc(s[f"e_in{m}"], 16)

        def max_rows(i, p, b):
            sp.wait_ge(s["e_msplit"], 2 * i + b + 1)
            for n, src in enumerate((Mh, Ml)):
                sp.dma_start(scrM[ds(i, 1), n, b * NSH:(b + 1) * NSH].rearrange("o c r -> (o c) r"), src[:, b].bitcast(F32)).then_inc(s["e_mout"], 16)
            sp.wait_ge(s["e_mout"], 32 * (2 * i + b + 1))
            sp.dma_start(QS[p][MROW:MROW + 2, b * NSH * P:(b + 1) * NSH * P].bitcast(F32),
                         scrM[ds(i, 1), :, b * NSH:(b + 1) * NSH].rearrange("o n c r -> (o n) (c r)")).then_inc(s[f"e_min{b}"], 16)

        def turn(it, p, pr, sp_, st):
            if pr:
                stack_out(it)
                if early(it):
                    stack_in(it, p, 0)
            if sp_:
                max_rows(it - 1, 1 - p, 0)
            if pr and not early(it):
                stack_in(it, p, 0)
            if sp_:
                max_rows(it - 1, 1 - p, 1)
            if pr:
                stack_in(it, p, 1)

        sp.wait_ge(s["e_const"], 3)
        turn(0, 0, True, False, False)
        sp.wait_ge(s["e_const"], 4)
        minus_ones(0)
        minus_ones(1)
        turn(1, 1, True, True, False)
        turn(2, 0, True, True, True)
        turn(3, 1, True, True, True)
        with sp.Fori(2, 4) as r:
            turn(2 * r, 0, True, True, True)
            turn(2 * r + 1, 1, True, True, True)
        turn(8, 0, False, True, True)
        sp.wait_ge(s["e_st"], NU * IMGS)
        sp.wait_ge(s["e_rb"], 16 * 2 * HPG * (IMGS - 1))
        sp.dma_start(W_raw[1][:, :], A["w1"]).then_inc(s["d_w1"], 16)
        with sp.Fori(0, NG) as g:
            sp.wait_ge(s["f1_acc"], 10 * (g + 1))
            sp.dma_start(out[:, ds(g * GT, GT), :], h[:, ds(g * GT, GT), :]).then_inc(s["d_out"], 16)
        sp.wait_ge(s["d_out"], 16 * NG)

    @block.gpsimd
    def _(pool):
        own = Own(pool, s["pool_own"])
        nc.gpsimd.memset(ones[:, :], 1.0).then_inc(s["const_pool"], 1)
        nc.gpsimd.memset(minus_half[:, :], -0.5).then_inc(s["const_pool"], 1)
        nc.gpsimd.memset(cmb[:, :, :], 1.0).then_inc(s["const_pool"], 1)
        def root(g):
            z = slice(g * GT, g * GT + GT)
            pool.wait_ge(s["var_ready"], 6 + g + 1)
            nc.gpsimd.tensor_tensor(rstd[:, z], mt[:, 0, z], minus_half[:, 0:1].broadcast_to([P, GT]), ALU.pow).then_inc(s["rstd_ready"], 1)

        pool.wait_ge(s["const_pool"], 3)
        xv = x_in[:, :, :].rearrange("p r (c t) -> p r c t", t=2)
        for n in range(2):
            z = slice(n * ROWS // 2, (n + 1) * ROWS // 2)
            pool.wait_ge(s[f"d_x{n}"], 16)
            own(nc.gpsimd.tensor_tensor(hi[0][:, z, :], xv[:, z, :, 0], xv[:, z, :, 1], ALU.subtract))
        own.settle()
        hv = hi[0][:, :, :].rearrange("p (r t) c -> p r t c", t=2)
        nc.gpsimd.tensor_tensor(det[0][:, 1], hv[:, :, 0, :], hv[:, :, 1, :], ALU.add)
        nc.gpsimd.tensor_tensor(det[0][:, 2], hv[:, :, 0, :], hv[:, :, 1, :], ALU.subtract).then_inc(s["pool_hi"], 1)
        pool.wait_ge(s["d_wd0"], 16 * IMGS)
        pool.wait_ge(s["det_ready"], 1)
        pool.wait_ge(s["pool_hi"], 1)
        nc.gpsimd.tensor_tensor(prod[:, :], det[0][:, :, :, :].rearrange("p b r c -> p (b r c)"), wd0[:, 0, :], ALU.mult).then_inc(s["prod_ready"], 1)
        pool.wait_ge(s["qkv_hi"], 1)
        nc.gpsimd.tensor_tensor(qkv_l[:, :, :, :], qkv_raw[:, :, :, :], qkv_h[:, :, :, :].bitcast(F32), ALU.subtract).then_inc(s["qkv_split"], 1)
        pool.wait_ge(s["d_small"], 16 * 8)
        pool.wait_ge(s["qkv_hi"], 2)
        for L in range(2):
            nc.gpsimd.tensor_tensor(rwl[L][:, :, :], rw[L][:, :, :], rwh[L][:, :, :].bitcast(F32), ALU.subtract).then_inc(s["rw_split0"], 1)

        pool.wait_ge(s["dsc_ready"], 4)
        nc.gpsimd.tensor_tensor(hv[:, :, 0, :], d1s, dsc[0][:, :, :], ALU.add)
        nc.gpsimd.tensor_tensor(hv[:, :, 1, :], d1s, dsc[0][:, :, :], ALU.subtract).then_inc(s["hv_ready"], 1)
        n0 = sum(WCOLS[0]) // NG

        def l0(i):
            pool.wait_ge(s["b_aqk"], 2 * i + 1)
            wait(pool, s["b_d2"], i)
            nc.gpsimd.tensor_tensor(qs[:, :], qsq[:, 0], qsq[:, 1], ALU.add)
            pool.wait_ge(s["b_aqk"], 2 * i + 2)
            nc.gpsimd.tensor_tensor(ks[:, :], ksq[:, 0], ksq[:, 1], ALU.add).then_inc(s["b_qs"], 1)
            pool.wait_ge(s["b_xn"], i + 1)
            for t in range(GT):
                nc.gpsimd.tensor_tensor(h[:, ds(i * GT + t, 1), :].squeeze(1), h[:, ds(i * GT + t, 1), :].squeeze(1), bv0[:, :], ALU.add).then_inc(s["b_hb"], 1)
            pool.wait_ge(s["w_hi0"], i + 1)
            nc.gpsimd.tensor_tensor(W_l[0][:, ds(i * n0, n0)], W_raw[0][:, ds(i * n0, n0)], W_h[0][:, ds(i * n0, n0)].bitcast(F32), ALU.subtract).then_inc(s["w_split0"], 1)

        l0(0)
        with pool.Fori(1, NG) as i:
            l0(i)

        pool.wait_ge(s["e_a1h"], 1)
        nc.gpsimd.tensor_tensor(a1l[:, :, :], a1raw[:, :, :], a1h[:, :, :].bitcast(F32), ALU.subtract).then_inc(s["e_a1"], 1)
        pool.wait_ge(s["f0_acc"], NG * 9)
        nc.gpsimd.memset(neg1[:, :], -1.0).then_inc(s["e_const"], 1)
        nc.gpsimd.memset(MX[:, :, :], 0.0).then_inc(s["e_const"], 1)

        def zeros(p):
            own(nc.gpsimd.memset(QS[p][:, :].bitcast(F32), 0.0))
            own(nc.gpsimd.memset(KS[p][:, :].bitcast(F32), 0.0))
            own.settle()
            pool.sem_inc(s["e_const"], 1)

        zeros(0)
        zeros(1)

        def low_halves(it, p):
            for m in range(3):
                pool.wait_ge(s["e_hi3"], 3 * it + m + 1)
                if m == 0:
                    wait(pool, s["e_out"], 32 * it)
                nc.gpsimd.tensor_tensor(ql[:, m], qf[p][:, m], qh[:, m].bitcast(F32), ALU.subtract).then_inc(s["e_split"], 1)

        low_halves(0, 0)
        for p in range(2):
            own(nc.gpsimd.memset(VA[p][:, :, :, :], 0.0))
        own.settle()
        for p in range(2):
            own(nc.gpsimd.memset(VA[p][0:KT, :, 0::2, HD:HD + 1], 1.0))
            own(nc.gpsimd.memset(VA[p][0:KT, :, 1::2, 0:1], 1.0))
        own(nc.gpsimd.memset(recb[:, :, :], 0.0))
        own.settle()
        pool.sem_inc(s["e_const"], 1)
        own(nc.gpsimd.memset(PR[96:P, :, :], 0.0))
        own.settle()
        pool.sem_inc(s["e_const"], 1)
        low_halves(1, 1)
        pool.wait_ge(s["e_xn"], NG)
        with pool.Fori(0, NT) as j:
            nc.gpsimd.tensor_tensor(h[:, ds(j, 1), :].squeeze(1), h[:, ds(j, 1), :].squeeze(1), bo1[:, :], ALU.add).then_inc(s["e_bo"], 1)

        def divide(it, p):
            i = it - 3
            pool.wait_ge(s["e_rb"], 16 * 2 * HPG * (i + 1))
            nc.gpsimd.tensor_tensor(recb[:, :, :], yr[1 - p][:, :, :], recb[:, :, :], ALU.mult).then_inc(s["e_y"], 1)
            pool.wait_ge(s["e_y"], i + 1)
            for q in range(NGQ // 2):
                nc.gpsimd.tensor_tensor(img(yT[:, q, :], i), recb[:, 2 * q, :].rearrange("p (j c) -> p j c", j=NT),
                                        recb[:, 2 * q + 1, :].rearrange("p (j c) -> p j c", j=NT), ALU.add).then_inc(s["e_yt"], 1)

        low_halves(2, 0)
        low_halves(3, 1)
        divide(3, 1)
        with pool.Fori(2, IMGS // 2) as r:
            low_halves(2 * r, 0)
            divide(2 * r, 0)
            low_halves(2 * r + 1, 1)
            divide(2 * r + 1, 1)
        for it in range(8, 10):
            divide(it, it % 2)
        pool.wait_ge(s["e_yl"], NGQ + 2)
        n1 = sum(WCOLS[1]) // NG
        root(0)
        for g in range(NG):
            if g + 1 < NG:
                root(g + 1)
            z = slice(g * n1, g * n1 + n1)
            pool.wait_ge(s["w_hi1"], g + 1)
            nc.gpsimd.tensor_tensor(W_l[1][:, z], W_raw[1][:, z], W_h[1][:, z].bitcast(F32), ALU.subtract).then_inc(s["w_split1"], 1)

    @block.scalar
    def _(act):
        A_ = nc.scalar.activation
        act.wait_ge(s["d_x0"], 16)
        act.wait_ge(s["d_x1"], 16)
        for k in range(3):
            for b in range(IMGS):
                act.dma_start(wd0[b * RG:b * RG + RG, k, :], A["wd0"][:, k, :]).then_inc(s[f"d_wd{k}"], 16)
        act.wait_ge(s["d_qkv"], 16)
        A_(qkv_h[:, :, :, :], qkv_raw[:, :, :, :], ACT.Copy).then_inc(s["qkv_hi"], 1)
        act.wait_ge(s["d_small"], 16 * 8)
        A_(rwh[0][:, :, :], rw[0][:, :, :], ACT.Copy)
        A_(rwh[1][:, :, :], rw[1][:, :, :], ACT.Copy).then_inc(s["qkv_hi"], 1)
        act.wait_ge(s["prod_ready"], 1)
        A_(prod[:, :], prod[:, :], ACT.Copy, accum_out=dots[:, 6:7]).then_inc(s["dot_ready"], 1)
        act.wait_ge(s["wex_in"], 1)
        A_(wex[:, 0:9], wex[:, 0:9], ACT.Exp)
        A_(wex[:, 9:10], lg[:, 9:10], ACT.Exp, scale=-1.0).then_inc(s["wex_ready"], 1)
        act.wait_ge(s["wts_ready"], 1)
        for n in (2, 1, 0):
            c = 3 * (2 - n) + 2
            A_(dsc[n][:, :, :], det[n][:, 2], ACT.Copy, scale=wts[:, c:c + 1]).then_inc(s["dsc_ready"], 1)
            if n == 0:
                A_(d1s, det[0][:, 1], ACT.Copy, scale=wts[:, c - 1:c]).then_inc(s["dsc_ready"], 1)

        roots = [0]

        def std(a, n):
            roots[0] += 1
            act.wait_ge(s["var_ready"], roots[0])
            A_(rstd[:, a:a + n], mt[:, 0, a:a + n], ACT.Sqrt).then_inc(s["std_ready"], 1)

        std(0, GT)
        n0 = sum(WCOLS[0]) // NG

        def ln_hi(i):
            act.wait_ge(s["b_T"], i + 1)
            wait(act, s["b_v"], i)
            A_(xwh[:, :, :].rearrange("p k (t c) -> p t k c", t=GT), group_ps(2).rearrange("p t (k c) -> p t k c", k=KC), ACT.Copy).then_inc(s["b_hi"], 1)

        def l0(i, prev, cur, nxt):
            if cur:
                wait(act, s["b_qs"], i)
                act.wait_ge(s["b_dqk"], 2 * i + 1)
                A_(qsq[:, :, :], qT[:, :, :], ACT.Square).then_inc(s["b_aqk"], 1)
            if prev:
                act.wait_ge(s["b_pt"], i)
                wait(act, s["b_av"], i - 1)
                A_(PT[:, :, :], PS[:, 7, 0:GW].rearrange("p (t c) -> p t c", t=GT), ACT.Copy).then_inc(s["b_ptev"], 1)
            if cur:
                act.wait_ge(s["b_dqk"], 2 * i + 2)
                A_(ksq[:, :, :], km2[:, :, :], ACT.Square, scale=0.5).then_inc(s["b_aqk"], 1)
                act.wait_ge(s["b_v"], i + 1)
                wait(act, s["b_av"], i)
                A_(v_sb[:, :, :], group_ps(4), ACT.Copy).then_inc(s["b_vev"], 1)
            if nxt:
                ln_hi(i + 1)
            if cur:
                if isinstance(i, int) and i == 0:
                    act.wait_ge(s["d_w0"], 16)
                A_(W_h[0][:, ds(i * n0, n0)], W_raw[0][:, ds(i * n0, n0)], ACT.Copy).then_inc(s["w_hi0"], 1)
                act.wait_ge(s["b_dm"], i + 1)
                wait(act, s["b_pt"], i)
                wait(act, s["b_res"], i)
                for t in range(GT):
                    ins = A_(Pm[:, t], dm[:, t], ACT.Exp, bias=hb[:, t:t + 1], scale=-0.5, accum_out=rs[:, t:t + 1])
                ins.then_inc(s["b_exp"], 1)

        ln_hi(0)
        std(GT, REST)
        l0(0, False, True, True)
        with act.Fori(1, NG - 1) as i:
            l0(i, True, True, True)
        l0(NG - 1, True, True, False)
        l0(NG, True, False, False)
        std(0, REST)

        def high(c, g, bank):
            act.wait_ge(s[f"{c}_T"], g + 1)
            A_(xTh[:, :, ds(g * GW, GW)].rearrange("p k (t c) -> p t k c", t=GT), group_ps(bank).rearrange("p t (k c) -> p t k c", k=KC), ACT.Copy).then_inc(s[f"{c}_hi"], 1)

        def logits(L, g, b, bank):
            act.wait_ge(s[f"f{L}_lg"], g + 1)
            A_(lgT[:, b], PS[0:NE, bank, 0:GW], ACT.Copy).then_inc(s[f"f{L}_lgT"], 1)

        def prep(c, off, L=None):
            for g in range(NG):
                high(c, g, g % 2 * 2 + off)
                if g == 1:
                    std(REST, GT)
                if L is not None and g:
                    logits(L, g - 1, (g - 1) % 2, 6)
            if L is not None:
                logits(L, NG - 1, 1, 6)

        def sigmoid(L, bank):
            if L == 0:
                act.wait_ge(s["f0_lgt"], NG)
                A_(sc[:, :, :], PS[:, bank, 0:NT * NE].rearrange("p (j e) -> p j e", e=NE), ACT.Sigmoid).then_inc(s["f0_sig"], 1)
            else:
                act.wait_ge(s["f1_lraw"], 1)
                A_(sc[:, :, :], sc[:, :, :], ACT.Sigmoid).then_inc(s["f1_sig"], 1)

        def experts(L, gu):
            ne = 9 + L
            def body(r):
                for k in range(gu * ne):
                    n = r * (gu * ne) + k
                    b = k % 2
                    act.wait_ge(s[f"f{L}_gu"], n + 1)
                    A_(sg[:, b], PS[:, b, 0:GW], ACT.Silu).then_inc(s[f"f{L}_silu"], 1)
                    act.wait_ge(s[f"f{L}_mul"], n + 1)
                    wait(act, s[f"f{L}_dn"], n - 1)
                    A_(ah[:, b], aa[:, b], ACT.Copy).then_inc(s[f"f{L}_ah"], 1)
            turns = NG // gu
            body(0)
            with act.Fori(1, turns) as r:
                body(r)

        act.wait_ge(s["d_a1"], 16)
        A_(a1h[:, :, :], a1raw[:, :, :], ACT.Copy).then_inc(s["e_a1h"], 1)
        prep("c", 2, 0)
        sigmoid(0, 7)
        experts(0, 2)
        std(0, REST)
        prep("e", 0)

        def turn(it, p):
            for U in range(NU):
                if live(it, 2):
                    i = it - 2
                    if U == 0 and isinstance(it, int) and it == 2:
                        act.wait_ge(s["e_const"], 6)
                    act.wait_ge(s["e_st"], i * NU + U + 1)
                    old = (2 * U + 1 - RING) // 3
                    wait(act, s["e_avt"], i * NAV + old + 1)
                    c0 = (2 * U) % RING
                    b = 2 * (U % 2)
                    A_(PR[0:KT, c0:c0 + 2, :], PS[0:KT, b:b + 2, 0:CW], ACT.Exp).then_inc(s["e_exp"], 1)
                if U in PR_U and live(it, 0):
                    m = PR_U.index(U)
                    act.wait_ge(s["e_prev"], 3 * it + m + 1)
                    if m == 0:
                        wait(act, s["e_out"], 32 * it)
                    A_(qh[:, m], qf[p][:, m], ACT.Copy).then_inc(s["e_hi3"], 1)
                if U == VT_U and live(it, 1):
                    if isinstance(it, int) and it == 1:
                        act.wait_ge(s["e_const"], 5)
                    act.wait_ge(s["e_vt"], it)
                    wait(act, s["e_avt"], (it - 2) * NAV)
                    for kt in range(NKT):
                        ins = A_(VA[1 - p][0:KT, kt, :, :].rearrange("p (a x) (b d) -> p a (x b) d", x=2, b=2)[:, :, 0:4:3, :],
                                 PS[0:KT, 7, kt * P + 64:kt * P + P].rearrange("p (a b d) -> p a b d", a=2, b=2), ACT.Copy)
                    ins.then_inc(s["e_va"], 1)
                for k, g in y_at(U):
                    if live(it, k):
                        y_raw(it - k, g, p ^ (k % 2), k)
                if live(it, 3) and not last_image(it - 3):
                    i = it - 3
                    if U in SUM_U:
                        b = SUM_U.index(U)
                        act.wait_ge(s["e_yr"], NGQ * (i + 1))
                        r = 0 if b else HD
                        act.dma_start(scrS[ds(i, 1), :, b::2].rearrange("o h g q -> (o h) g q"), yr[1 - p][r:P:32, b::2, :]).then_inc(s["e_so"], 16)
                    if U == SM_U:
                        act.wait_ge(s["e_so"], 32 * (i + 1))
                        wait(act, s["e_rec"], i)
                        act.dma_start(sm[:, :], scrS[ds(i, 1)].rearrange("o h g q -> (o h g q)").rearrange("(p c) -> p c", c=SW)).then_inc(s["e_sums"], 16)
                    if U == RO_U:
                        act.wait_ge(s["e_rec"], i + 1)
                        act.dma_start(scrR[ds(i, 1)].rearrange("o h g q -> (o h g q)").rearrange("(p c) -> p c", c=SW), rec[:, :]).then_inc(s["e_ro"], 16)
                    if U in RB_U:
                        hh, b = divmod(RB_U.index(U), 2)
                        if U == RB_U[0]:
                            act.wait_ge(s["e_ro"], 16 * (i + 1))
                            wait(act, s["e_yt"], NGQ // 2 * i)
                        r = 32 * hh + HD * b
                        act.dma_start(recb[r:r + HD, b::2, :], scrR[ds(i, 1), hh, b::2].broadcast_to([HD, NGQ // 2, POS])).then_inc(s["e_rb"], 16)

        def y_raw(i, g, p, k):
            act.wait_ge(s["e_avt"], NAV * i + NKT * (g + 1))
            if k == 2:
                wait(act, s["e_y"], i - 1)
            A_(yr[p][:, g], PS[:, 6, 0:POS], ACT.Copy).then_inc(s["e_yr"], 1)

        for it in range(4):
            turn(it, it % 2)
        with act.Fori(2, 4) as r:
            turn(2 * r, 0)
            turn(2 * r + 1, 1)
        for it in range(8, 11):
            turn(it, it % 2)
        n1 = sum(WCOLS[1]) // NG
        for g in range(NG + 3):
            for t in {NG: (NG - 2, NG - 1)}.get(g, (g - 2,) if 2 <= g < NG else ()):
                high("p", t, transpose_bank(t))
            for c in ((), (0,), (1,), (2,), (3,), (4, 5), (), (), ())[g]:
                if c == 0:
                    act.wait_ge(s["d_w1"], 16)
                z = slice(c * n1, c * n1 + n1)
                A_(W_h[1][:, z], W_raw[1][:, z], ACT.Copy).then_inc(s["w_hi1"], 1)
            if g < NG:
                act.wait_ge(s["p_nm"], g + 1)
                for t in range(GT):
                    j = g * GT + t
                    ins = A_(xnp[:, g % 2, t], h[:, j, :], ACT.Identity, bias=nmr[:, j:j + 1], scale=rstd[:, j:j + 1])
                ins.then_inc(s["p_xn"], 1)
            if g >= 3:
                logits(1, g - 3, (g - 3) % 2, router_bank(g - 3))
        sigmoid(1, 7)
        experts(1, 3)

    @block.vector
    def _(dve):
        V = nc.vector
        own = Own(dve, s["dve_own"])

        roots = [0]

        def moments(a, n):
            z = slice(a, a + n)
            me, mo = stats[:, z, 1], stats[:, z, 4]
            own(V.tensor_tensor(mt[:, 0, z], me, mo, ALU.add))
            own(V.tensor_tensor(mt[:, 1, z], me, mo, ALU.subtract))
            own(V.tensor_tensor(mt[:, 2, z], stats[:, z, 2], stats[:, z, 5], ALU.add))
            own.settle()
            own(V.tensor_scalar(mv[:, z, 0], mt[:, 0, z], 0.5, None, ALU.mult))
            own(V.scalar_tensor_tensor(out=mt[:, 3, z], in0=mt[:, 1, z], scalar=0.25, in1=mt[:, 1, z], op0=ALU.mult, op1=ALU.mult))
            own.settle()
            own(V.scalar_tensor_tensor(out=mv[:, z, 1], in0=mt[:, 2, z], scalar=1.0 / D, in1=mt[:, 3, z], op0=ALU.mult, op1=ALU.add))
            own.settle()
            V.tensor_scalar(mt[:, 0, z], mv[:, z, 1], LN_EPS, None, ALU.add).then_inc(s["var_ready"], 1)

        def invert(a, n):
            roots[0] += 1
            dve.wait_ge(s["std_ready"], roots[0])
            own(V.reciprocal(rstd[:, a:a + n], rstd[:, a:a + n]))
            own.settle()

        src = x_in[:, :, :]
        for n in range(NLV):
            sv4 = src.rearrange("p r (c t) -> p r c t", t=2)
            for a in range(2 if n == 0 else 1):
                z = slice(a * ROWS // 2, (a + 1) * ROWS // 2) if n == 0 else slice(None)
                if n == 0:
                    dve.wait_ge(s[f"d_x{a}"], 16)
                own(V.tensor_tensor(lo[n][:, z, :], sv4[:, z, :, 0], sv4[:, z, :, 1], ALU.add))
            if n:
                own(V.tensor_tensor(hi[n][:, :, :], sv4[:, :, :, 0], sv4[:, :, :, 1], ALU.subtract))
            own.settle()
            lv = lo[n][:, :, :].rearrange("p (r t) c -> p r t c", t=2)
            hv = hi[n][:, :, :].rearrange("p (r t) c -> p r t c", t=2)
            own(V.tensor_tensor(app[n][:, :, :], lv[:, :, 0, :], lv[:, :, 1, :], ALU.add))
            own(V.tensor_tensor(det[n][:, 0], lv[:, :, 0, :], lv[:, :, 1, :], ALU.subtract))
            if n:
                own(V.tensor_tensor(det[n][:, 1], hv[:, :, 0, :], hv[:, :, 1, :], ALU.add))
                own(V.tensor_tensor(det[n][:, 2], hv[:, :, 0, :], hv[:, :, 1, :], ALU.subtract))
            own.settle()
            if n == 0:
                dve.sem_inc(s["det_ready"], 1)
            src = app[n][:, :, :]
        dve.wait_ge(s["ws_ready"], 1)
        ws = PS[:, 0:6, :].rearrange("p b c -> p (b c)")
        own(V.tensor_tensor_reduce(junk[:, 0:rows[2] * cols[2]], app[2][:, :, :].rearrange("p r c -> p (r c)"), ws[:, NWS - rows[2] * cols[2]:NWS], 1.0, 0.0, ALU.mult, ALU.add, dots[:, 9:10]))
        for n in (2, 1, 0):
            for k in range(0 if n else 1, 3):
                own.settle()
                if n == 0:
                    dve.wait_ge(s["pool_hi"], 1)
                    dve.wait_ge(s[f"d_wd{k}"], 16 * IMGS)
                at_ = (2 - n) * 3 * sizes[2] + k * sizes[n]
                w = ws[:, at_:at_ + sizes[n]] if n else wd0[:, k, :]
                own(V.tensor_tensor_reduce(junk[:, 0:sizes[n]], det[n][:, :, :, :].rearrange("p b r c -> p (b r c)"), w, 1.0, 0.0,
                                           ALU.mult, ALU.add, dots[:, 3 * (2 - n) + k:3 * (2 - n) + k + 1]))
        own.settle()
        dve.wait_ge(s["dot_ready"], 1)
        V.tensor_copy(lg[:, :], dots[:, :]).then_inc(s["dots_ready"], 1)
        dve.wait_ge(s["dots_sum"], 1)
        dve.wait_ge(s["d_bias"], 16)
        for n, (a, b, f) in enumerate(((0, 3, 0.125), (3, 6, 0.25), (6, 9, 0.5), (9, 10, 0.125))):
            own(V.scalar_tensor_tensor(out=lg[:, a:b], in0=PS[:, 6, a:b], scalar=f, in1=lbias[:, a:b], op0=ALU.mult, op1=ALU.add))
        own.settle()
        l3 = lg[:, 0:9].rearrange("p (n k) -> p n k", n=3)
        e3 = wex[:, 0:9].rearrange("p (n k) -> p n k", n=3)
        own(V.tensor_reduce(wmx[:, :], l3, AX_X, ALU.max))
        own.settle()
        V.tensor_tensor(e3, l3, wmx[:, :].unsqueeze(2).broadcast_to([P, 3, 3]), ALU.subtract).then_inc(s["wex_in"], 1)
        dve.wait_ge(s["wex_ready"], 1)
        own(V.tensor_reduce(wsm[:, 0:3], e3, AX_X, ALU.add))
        own(V.tensor_scalar(wsm[:, 3:4], wex[:, 9:10], 1.0, None, ALU.add))
        own.settle()
        own(V.reciprocal(wsm[:, :], wsm[:, :]))
        own.settle()
        for n, f in enumerate((1 / 64, 1 / 16, 1 / 4)):
            own(V.tensor_scalar(wts[:, 3 * n:3 * n + 3], wex[:, 3 * n:3 * n + 3], wsm[:, n:n + 1], f, ALU.mult, ALU.mult))
        own(V.tensor_scalar(wts[:, 9:10], wsm[:, 3:4], 1 / 64, None, ALU.mult))
        own.settle()
        V.tensor_scalar(app[2][:, :, :], app[2][:, :, :], wts[:, 9:10], None, ALU.mult).then_inc(s["wts_ready"], 1)
        dve.wait_ge(s["wts_ready"], 1)
        for n in (2, 1, 0):
            c = 3 * (2 - n)
            u = app[n][:, :, :]
            lv = lo[n][:, :, :].rearrange("p (r t) c -> p r t c", t=2)
            hv = hi[n][:, :, :].rearrange("p (r t) c -> p r t c", t=2)
            own(V.scalar_tensor_tensor(out=lv[:, :, 0, :], in0=det[n][:, 0], scalar=wts[:, c:c + 1], in1=u, op0=ALU.mult, op1=ALU.add))
            own(V.scalar_tensor_tensor(out=lv[:, :, 1, :], in0=det[n][:, 0], scalar=wts[:, c:c + 1], in1=u, op0=ALU.mult, op1=ALU.subtract, reverse1=True))
            if n == 0:
                own.settle()
                dve.wait_ge(s["hv_ready"], 1)
            else:
                dve.wait_ge(s["dsc_ready"], 3 - n)
                own(V.scalar_tensor_tensor(out=hv[:, :, 0, :], in0=det[n][:, 1], scalar=wts[:, c + 1:c + 2], in1=dsc[n][:, :, :], op0=ALU.mult, op1=ALU.add))
                own(V.scalar_tensor_tensor(out=hv[:, :, 1, :], in0=det[n][:, 1], scalar=wts[:, c + 1:c + 2], in1=dsc[n][:, :, :], op0=ALU.mult, op1=ALU.subtract))
                own.settle()
            dst = app[n - 1][:, :, :] if n else h[:, 0:ROWS, :]
            dv = dst.rearrange("p r (c t) -> p r c t", t=2)
            own(V.tensor_tensor(dv[:, :, :, 0], lo[n][:, :, :], hi[n][:, :, :], ALU.add))
            own(V.tensor_tensor(dv[:, :, :, 1], lo[n][:, :, :], hi[n][:, :, :], ALU.subtract))
            own.settle()
        dve.sem_inc(s["img_done"], 1)
        dve.wait_ge(s["d_txt"], 16)
        def bn(j, tile):
            return V.bn_stats(stats[:, ds(j, 1), :].squeeze(1), tile)

        for j in range(GT):
            own(bn(j, h[:, j, :]))
        own.settle()
        moments(0, GT)

        def normalise(dst, j):
            return V.tensor_scalar(dst, h[:, ds(j, 1), :].squeeze(1), mv[:, ds(j, 1), 0:1].squeeze(1),
                                   rstd[:, ds(j, 1)], ALU.subtract, ALU.mult)

        def xn_group(i):
            wait(dve, s["b_T"], i)
            for t in range(GT):
                ins = normalise(xn[:, t], i * GT + t)
            ins.then_inc(s["b_xn"], 1)

        def ln_lo(i):
            dve.wait_ge(s["b_hi"], i + 1)
            V.tensor_tensor(xwl[:, :, :].rearrange("p k (t c) -> p t k c", t=GT), group_ps(2).rearrange("p t (k c) -> p t k c", k=KC),
                            xwh[:, :, :].rearrange("p k (t c) -> p t k c", t=GT).bitcast(F32), ALU.subtract).then_inc(s["b_x"], 1)

        def l0(i, prev, cur, nxt):
            if nxt:
                xn_group(i + 1)
            if cur:
                dve.wait_ge(s["b_qk"], i + 1)
                wait(dve, s["b_d2"], i)
                for m in range(2):
                    ins = V.tensor_scalar(qT[:, m], PS[:, m, 0:GW], bqk0[:, m:m + 1], None, ALU.add)
                ins.then_inc(s["b_dqk"], 1)
                for m in range(2):
                    ins = V.tensor_scalar(km2[:, m], PS[:, 2 + m, 0:GW], bqk0[:, 2 + m:3 + m], -2.0, ALU.add, ALU.mult)
                ins.then_inc(s["b_dqk"], 1)
            if prev:
                dve.wait_ge(s["b_exp"], i)
                own(V.reciprocal(ri[:, :], rs[:, :]))
                own.settle()
                dve.wait_ge(s["b_av"], i)
                dve.wait_ge(s["b_hb"], GT * i)
                for t in range(GT):
                    j = (i - 1) * GT + t
                    hj = h[:, ds(j, 1), :].squeeze(1)
                    own(V.scalar_tensor_tensor(out=hj, in0=PS[:, t // 2, (t % 2) * D:(t % 2) * D + D], scalar=ri[:, t:t + 1], in1=hj, op0=ALU.mult, op1=ALU.add))
                if cur:
                    own.settle()
                    dve.sem_inc(s["b_res"], 1)
            if nxt:
                ln_lo(i + 1)
            if prev:
                if not cur:
                    own.settle()
                for t in range(GT):
                    j = (i - 1) * GT + t
                    own(bn(j, h[:, ds(j, 1), :].squeeze(1)))
            if cur:
                dve.wait_ge(s["b_d2"], i + 1)
                wait(dve, s["b_exp"], i)
                for t in range(GT):
                    own(V.scalar_tensor_tensor(out=dm[:, t], in0=PS[:, 6, t * P:t * P + P], scalar=0.0, in1=far_mask[:, :], op0=ALU.max, op1=ALU.add))
                own.settle()
                own(V.tensor_reduce(mn[:, :], dm[:, :, :], AX_X, ALU.min))
                own.settle()
                V.tensor_scalar(hb[:, :], mn[:, :], 0.5, None, ALU.mult).then_inc(s["b_dm"], 1)

        dve.wait_ge(s["d_small"], 16 * 8)
        dve.wait_ge(s["d_const"], 16 * 5)
        invert(0, GT)
        xn_group(0)
        for j in range(GT, NT):
            if j == NT // 2:
                ln_lo(0)
            own(bn(j, h[:, j, :]))
        own.settle()
        moments(GT, REST)
        invert(GT, REST)
        l0(0, False, True, True)
        own.loop(1, NG - 1, 1 + 3 * GT + 1, lambda i: l0(i, True, True, True))
        l0(NG - 1, True, True, False)
        own.settle()
        moments(0, REST)

        def xn_(c, g, buf):
            for t in range(GT):
                ins = normalise(buf[:, t], g * GT + t)
            ins.then_inc(s[f"{c}_xn"], 1)

        def low(c, g, bank):
            dve.wait_ge(s[f"{c}_hi"], g + 1)
            V.tensor_tensor(xTl[:, :, ds(g * GW, GW)].rearrange("p k (t c) -> p t k c", t=GT), group_ps(bank).rearrange("p t (k c) -> p t k c", k=KC),
                            xTh[:, :, ds(g * GW, GW)].rearrange("p k (t c) -> p t k c", t=GT).bitcast(F32), ALU.subtract).then_inc(s[f"{c}_lo"], 1)

        def prep(c, buf, off):
            for g in range(NG):
                low(c, g, g % 2 * 2 + off)
                if g + 2 == NG - 1:
                    invert(REST, GT)
                if g + 2 < NG:
                    xn_(c, g + 2, buf[:, g % 2])

        def bias_logits():
            dve.wait_ge(s["f1_lgt"], NG)
            V.tensor_tensor(sc[:, :, :], PS[:, 7, 0:NT * NE].rearrange("p (j e) -> p j e", e=NE),
                            lb1[:, :].unsqueeze(1).broadcast_to([P, NT, NE]), ALU.add).then_inc(s["f1_lraw"], 1)

        def compare(L):
            if L == 0:
                dve.wait_ge(s["f0_sig"], 1)
                own(V.tensor_tensor(sv[:, :, :], sc[:, :, :], cb0[:, :].unsqueeze(1).broadcast_to([P, NT, NE]), ALU.add))
                own.settle()
                pr = sv[:, :, :].rearrange("p j (q t) -> p j q t", t=2)
                hiP, loP = t1[:, :, 0:4], t2[:, :, 0:4]
                own(V.tensor_tensor(hiP, pr[:, :, :, 0], pr[:, :, :, 1], ALU.max))
                own(V.tensor_tensor(loP, pr[:, :, :, 0], pr[:, :, :, 1], ALU.min))
                own.settle()
                hp = hiP.rearrange("p j (g t) -> p j g t", t=2)
                lp = loP.rearrange("p j (g t) -> p j g t", t=2)
                own(V.tensor_tensor(t3[:, :, 0:2], hp[:, :, :, 0], hp[:, :, :, 1], ALU.max))
                own(V.tensor_tensor(t3[:, :, 2:4], hp[:, :, :, 0], hp[:, :, :, 1], ALU.min))
                own(V.tensor_tensor(t3[:, :, 4:6], lp[:, :, :, 0], lp[:, :, :, 1], ALU.max))
                own.settle()
                own(V.tensor_tensor(t3[:, :, 6:8], t3[:, :, 2:4], t3[:, :, 4:6], ALU.max))
                own.settle()
                own(V.tensor_tensor(t1[:, :, 4:6], t3[:, :, 0:2], t3[:, :, 6:8], ALU.add))
                own.settle()
                own(V.tensor_tensor(t2[:, :, 4:5], t1[:, :, 4:5], t1[:, :, 5:6], ALU.is_ge))
                own(V.tensor_tensor(t2[:, :, 5:6], t1[:, :, 4:5], t1[:, :, 5:6], ALU.is_lt))
                own.settle()
                own(V.tensor_tensor(sv[:, :, :].rearrange("p j (g q) -> p j g q", g=2), sv[:, :, :].rearrange("p j (g q) -> p j g q", g=2),
                                    t2[:, :, 4:6].unsqueeze(3).broadcast_to([P, NT, 2, 4]), ALU.mult))
                own.settle()
                key = sv
            else:
                dve.wait_ge(s["f1_sig"], 1)
                key = sc
            for e in range(NE):
                if e:
                    own(V.tensor_tensor(ra[:, :, e, 0:e], key[:, :, 0:e], key[:, :, e:e + 1].broadcast_to([P, NT, e]), ALU.is_ge))
                own(V.tensor_tensor(ra[:, :, e, e:NE], key[:, :, e:NE], key[:, :, e:e + 1].broadcast_to([P, NT, NE - e]), ALU.is_gt))
            own.settle()

        def weigh(L):
            own(V.tensor_reduce(t1[:, :, :], ra[:, :, :, :], AX_X, ALU.add))
            own.settle()
            own(V.tensor_scalar(t2[:, :, :], t1[:, :, :], 1.5, None, ALU.is_lt))
            own.settle()
            own(V.tensor_tensor(t3[:, :, :], t2[:, :, :], sc[:, :, :], ALU.mult))
            own.settle()
            own(V.tensor_reduce(t1[:, :, 0:1].squeeze(2), t3[:, :, :], AX_X, ALU.add))
            own.settle()
            own(V.tensor_scalar(t1[:, :, 1:2].squeeze(2), t1[:, :, 0:1].squeeze(2), (1e-20, 1e-8)[L], None, ALU.add))
            own.settle()
            own(V.reciprocal(t1[:, :, 2:3].squeeze(2), t1[:, :, 1:2].squeeze(2)))
            own.settle()
            rcp = t1[:, :, 2:3].broadcast_to([P, NT, NE])
            if L == 0:
                own(V.tensor_tensor(cmb[:, :, 0:NE], t3[:, :, :], rcp, ALU.mult))
                own.settle()
                return
            own(V.tensor_tensor(sv[:, :, :], t3[:, :, :], rcp, ALU.mult))
            own.settle()
            own(V.tensor_reduce(tot[:, 0:NE], t2[:, :, :].rearrange("p j e -> p e j"), AX_X, ALU.add))
            own(V.tensor_reduce(tot[:, NE:2 * NE], sv[:, :, :].rearrange("p j e -> p e j"), AX_X, ALU.add))
            own.settle()
            dve.sem_inc(s["f1_tot"], 1)

        def average():
            dve.wait_ge(s["f1_sum"], 1)
            own(V.tensor_scalar(t1[:, 0, :], PS[:, 7, 0:NE], 1.0, None, ALU.max))
            own.settle()
            own(V.reciprocal(t1[:, 1, :], t1[:, 0, :]))
            own.settle()
            own(V.tensor_tensor(t1[:, 2, :], PS[:, 7, NE:2 * NE], t1[:, 1, :], ALU.mult))
            own.settle()
            own(V.tensor_tensor(cmb[:, :, 0:NE], t2[:, :, :], t1[:, 2:3, :].broadcast_to([P, NT, NE]), ALU.mult))
            own.settle()

        def experts(L, gu, before_last=None):
            ne = 9 + L
            per = gu * ne

            def gated(n, k):
                b = k % 2
                dve.wait_ge(s[f"f{L}_silu"], n + 1)
                wait(dve, s[f"f{L}_ah"], n - 1)
                V.tensor_tensor(aa[:, b], sg[:, b], PS[:, 2 + b, 0:GW], ALU.mult).then_inc(s[f"f{L}_mul"], 1)

            def low(n, k):
                b = k % 2
                dve.wait_ge(s[f"f{L}_ah"], n + 1)
                wait(dve, s[f"f{L}_dn"], n - 1)
                V.tensor_tensor(al[:, b], aa[:, b], ah[:, b].bitcast(F32), ALU.subtract).then_inc(s[f"f{L}_al"], 1)

            def tile_stats(n, g, t):
                dve.wait_ge(s["f0_acc"], n + 1 - t)
                bn(g * GT + t, h[:, ds(g * GT + t, 1), :].squeeze(1)).then_inc(s["f0_st"], 1)

            def accumulate(n, g, e, k):
                b = 4 + 2 * (k % 2)
                dve.wait_ge(s[f"f{L}_dn"], n + 1)
                wait(dve, s[f"f{L}_acc"], n)
                for t in range(GT):
                    hj = h[:, ds(g * GT + t, 1), :].squeeze(1)
                    ins = V.scalar_tensor_tensor(out=hj, in0=PS[:, b + t // 2, (t % 2) * D:(t % 2) * D + D],
                                                 scalar=cmb[:, ds(g * GT + t, 1), e:e + 1].squeeze(1), in1=hj, op0=ALU.mult, op1=ALU.add)
                ins.then_inc(s[f"f{L}_acc"], 1)

            def body(r, first=False):
                for k in range(per):
                    n = r * per + k
                    if first and k == 0:
                        compare(L)
                    gated(n, k)
                    if first and k == 1 and L == 1:
                        average()
                    low(n, k)
                    if first and k == 0:
                        weigh(L)
                    g = r * gu + (k - 1) // ne
                    if not first or k >= 1:
                        accumulate(n - 1, g, (k - 1) % ne, (k - 1) % per)
                    if L == 0 and (k - 1) % ne < GT and (not first or k >= 1 + ne):
                        tile_stats(n - 2, g - 1, (k - 1) % ne)
            assert per % 2 == 0
            body(0, True)
            with dve.Fori(1, NG // gu) as r:
                body(r)
            if before_last is not None:
                before_last()
            accumulate(NG * ne - 1, NG - 1, ne - 1, per - 1)
            dve.wait_ge(s[f"f{L}_acc"], NG * ne)

        def ahead(c, buf):
            invert(0, REST)
            xn_(c, 0, buf[:, 0])
            xn_(c, 1, buf[:, 1])

        ahead("c", xnc)
        l0(NG, True, False, False)
        own.settle()
        moments(REST, GT)
        prep("c", xnc, 2)

        def before_last():
            dve.wait_ge(s["f0_st"], REST)
            moments(0, REST)
            ahead("e", xn1)

        experts(0, 2, before_last)
        for t in range(GT):
            own(bn(REST + t, h[:, REST + t, :]))
        own.settle()
        moments(REST, GT)
        prep("e", xn1, 0)

        def turn(it, p):
            for U in range(NU):
                sc_ = [(k, c) for k, c in s_at(U) if live(it, k)]

                def reduce_max():
                    if not sc_:
                        return
                    k, c = sc_.pop(0)
                    i = it - k
                    dve.wait_ge(s["e_s"], NS * i + c + 1)
                    if c % NSH == 0:
                        wait(dve, s["e_mT"], 2 * i - 1 + c // NSH)
                    V.tensor_reduce(MX[:, c // NSH, c % NSH:c % NSH + 1], PS[:, max_bank(it, c), 0:POS], AX_X, ALU.max).then_inc(s["e_mx"], 1)

                reduce_max()
                if U in PR_U and live(it, 0):
                    m = PR_U.index(U)
                    dve.wait_ge(s["e_pr"], 3 * it + m + 1)
                    wait(dve, s["e_split"], 3 * (it - 1))
                    if m == 2:
                        wait(dve, s["e_vt"], it - 1)
                    V.tensor_scalar(qf[p][:, m], PS[:, project_bank(it, m), 0:POS], bq1[:, m:m + 1], (0.25, 0.25, 1.0)[m], ALU.add, ALU.mult).then_inc(s["e_prev"], 1)
                if U in MT_U and live(it, 1):
                    i, b = it - 1, MT_U.index(U)
                    dve.wait_ge(s["e_mT"], 2 * i + b + 1)
                    wait(dve, s["e_mout"], 32 * (2 * i + b - 1))
                    own(V.tensor_copy(Mh[:, b], PS[0:NSH, 7, 0:P]))
                    own.settle()
                    V.tensor_tensor(Ml[:, b], PS[0:NSH, 7, 0:P], Mh[:, b].bitcast(F32), ALU.subtract).then_inc(s["e_msplit"], 1)
                if U == REC_U and live(it, 3) and not last_image(it - 3):
                    i = it - 3
                    dve.wait_ge(s["e_sums"], 16 * (i + 1))
                    wait(dve, s["e_ro"], 16 * i)
                    V.reciprocal(rec[:, :], sm[:, :]).then_inc(s["e_rec"], 1)
                for g in last_at(it, U):
                    b = (qf[0][:, 0], qf[0][:, 1], qf[0][:, 2], qf[1][:, 0])[g]
                    if g == 0:
                        dve.wait_ge(s["e_split"], 3 * IMGS)
                    dve.wait_ge(s["e_sb"], g + 1)
                    own(V.reciprocal(b, PS[:, 7, 0:POS]))
                    own.settle()
                    dve.wait_ge(s["e_yr"], NGQ * (IMGS - 1) + g + 1)
                    V.scalar_tensor_tensor(out=b, in0=yr[(IMGS - 1) % 2][:, g], scalar=halves[:, g % 2:g % 2 + 1], in1=b, op0=ALU.mult, op1=ALU.mult)\
                        .then_inc(s["e_yl"], 1)
                    if g % 2:
                        a = (qf[0][:, 0], qf[0][:, 2])[g // 2]
                        dve.wait_ge(s["e_yl"], g + 1 + g // 2)
                        V.tensor_tensor(img(yT[:, g // 2, :], IMGS - 1), a.rearrange("p (j c) -> p j c", j=NT), b.rearrange("p (j c) -> p j c", j=NT), ALU.add)\
                            .then_inc(s["e_yl"], 1)
                reduce_max()

        for it in range(4):
            turn(it, it % 2)
        own.loop(2, 4, 4, lambda r: (turn(2 * r, 0), turn(2 * r + 1, 1)))
        for it in range(8, 11):
            turn(it, it % 2)
        dve.wait_ge(s["e_bo"], NT)
        dve.wait_ge(s["e_pr"], 3 * IMGS)
        for g in range(NG + 2):
            if g < NG:
                z = slice(g * GT, g * GT + GT)
                dve.wait_ge(s["g_wo"], g + 1)
                V.tensor_tensor(h[:, z, :], group_ps(2 * (g % 2)), h[:, z, :], ALU.add).then_inc(s["g_res"], 1)
                dve.wait_ge(s["g_res"], g + 1)
                for t in range(GT):
                    own(bn(g * GT + t, h[:, g * GT + t, :]))
                own.settle()
                moments(g * GT, GT)
            if g >= 2:
                low("p", g - 2, transpose_bank(g - 2))
            if g < NG:
                dve.wait_ge(s["rstd_ready"], g + 1)
                V.scalar_tensor_tensor(out=nmr[:, z], in0=mv[:, z, 0], scalar=-1.0, in1=rstd[:, z], op0=ALU.mult, op1=ALU.mult).then_inc(s["p_nm"], 1)
        bias_logits()
        experts(1, 3)

    @block.tensor
    def _(pe):
        M = nc.tensor.matmul

        def split3(out_, pairs, start=True, stop=True):
            n = len(pairs)
            for c, (wh, wl, xh, xl) in enumerate(pairs):
                M(out_, wh, xh, start=(start and c == 0), stop=False)
                M(out_, wl, xh, start=False, stop=False)
                ins = M(out_, wh, xl, start=False, stop=(stop and c == n - 1))
            return ins

        def warm_up(n):
            for _ in range(n):
                M(PS[:, 6, 0:GW].rearrange("p (t c) -> p t c", t=GT), ones[:, :], same_img[:, :].unsqueeze(1).broadcast_to([P, GT, P]), start=True, stop=True)

        pe.wait_ge(s["d_wd"], 16 * 2)
        for b in range(6):
            n = min(512, NWS - b * 512)
            ins = M(PS[:, b, 0:n], rep[:, :], wsmall[:, b * 512:b * 512 + n], start=True, stop=True)
        ins.then_inc(s["ws_ready"], 1)
        pe.wait_ge(s["dots_ready"], 1)
        pe.wait_ge(s["d_const"], 16 * 5)
        M(PS[:, 6, 0:10], same_img[:, :], lg[:, :], start=True, stop=True).then_inc(s["dots_sum"], 1)

        def transposes(i):
            pe.wait_ge(s["b_xn"], i + 1)
            wait(pe, s["b_dqk"], 2 * i)
            for t in range(GT):
                for k in range(KC):
                    c = (t % 2) * D + k * P
                    ins = nc.tensor.transpose(PS[:, 2 + t // 2, c:c + P], xn[:, t, k * P:k * P + P], ident[:, :])
            ins.then_inc(s["b_T"], 1)

        def l0(i, prev, cur, nxt):
            if cur:
                pe.wait_ge(s["b_x"], i + 1)
                wait(pe, s["b_res"], i - 1)
                for m in range(4):
                    c = (m % 2) * P
                    ins = split3(PS[:, m, 0:GW], [(qkv_h[:, m // 2, k, c:c + P], qkv_l[:, m // 2, k, c:c + P], xwh[:, k], xwl[:, k]) for k in range(KC)])
                ins.then_inc(s["b_qk"], 1)
            if prev:
                pe.wait_ge(s["b_exp"], i)
                for t in range(GT):
                    ins = nc.tensor.transpose(PS[:, 7, t * P:t * P + P], Pm[:, t], ident[:, :])
                ins.then_inc(s["b_pt"], 1)
            if cur:
                wait(pe, s["b_vev"], i)
                for t in range(GT):
                    ins = split3(PS[:, 4 + t // 2, (t % 2) * D:(t % 2) * D + D],
                                 [(xwh[:, k, t * P:t * P + P], xwl[:, k, t * P:t * P + P], qkv_h[:, 2, k], qkv_l[:, 2, k]) for k in range(KC)])
                ins.then_inc(s["b_v"], 1)
            if prev:
                pe.wait_ge(s["b_ptev"], i)
                pe.wait_ge(s["b_vev"], i)
                if cur:
                    pe.wait_ge(s["b_dqk"], 2 * i + 1)
                for t in range(GT):
                    ins = M(PS[:, t // 2, (t % 2) * D:(t % 2) * D + D], PT[:, t], v_sb[:, t], start=True, stop=True)
                ins.then_inc(s["b_av"], 1)
            if nxt:
                transposes(i + 1)
            if cur:
                pe.wait_ge(s["b_qs"], i + 1)
                wait(pe, s["b_dm"], i)
                for t in range(GT):
                    o_ = PS[:, 6, t * P:t * P + P]
                    c = slice(t * P, t * P + P)
                    M(o_, ones[:, :], ks[:, c], start=True, stop=False)
                    M(o_, qs[:, c], ones[:, :], start=False, stop=False)
                    M(o_, qT[:, 0, c], km2[:, 0, c], start=False, stop=False)
                    ins = M(o_, qT[:, 1, c], km2[:, 1, c], start=False, stop=True)
                ins.then_inc(s["b_d2"], 1)

        pe.wait_ge(s["qkv_split"], 1)
        pe.wait_ge(s["const_pool"], 3)
        pe.wait_ge(s["img_done"], 1)
        warm_up(3)
        transposes(0)
        l0(0, False, True, True)
        l0(1, True, True, True)
        with pe.Fori(2, NG - 1) as i:
            l0(i, True, True, True)
        l0(NG - 1, True, True, False)
        l0(NG, True, False, False)

        def transpose_group(c, g, buf, bank):
            pe.wait_ge(s[f"{c}_xn"], g + 1)
            for t in range(GT):
                for k in range(KC):
                    at_ = (t % 2) * D + k * P
                    ins = nc.tensor.transpose(PS[:, bank + t // 2, at_:at_ + P], buf[:, t, k * P:k * P + P], ident[:, :])
            ins.then_inc(s[f"{c}_T"], 1)

        def router(L, c, g, bank):
            pe.wait_ge(s[f"{c}_lo"], g + 1)
            pe.wait_ge(s[f"{c}_hi"], g + 1)
            if bank < 6:
                pe.wait_ge(s["g_res"], NG)
            else:
                wait(pe, s[f"f{L}_lgT"], g)
            split3(PS[0:NE, bank, 0:GW], [(rwh[L][:, k], rwl[L][:, k], xTh[:, k, ds(g * GW, GW)], xTl[:, k, ds(g * GW, GW)]) for k in range(KC)])\
                .then_inc(s[f"f{L}_lg"], 1)

        def router_back(L, g, b, bank):
            pe.wait_ge(s[f"f{L}_lgT"], g + 1)
            for t in range(GT):
                c = (g * GT + t) * NE
                ins = nc.tensor.transpose(PS[:, bank, c:c + NE], lgT[:, b, t * P:t * P + P], ident[0:NE, 0:NE])
            ins.then_inc(s[f"f{L}_lgt"], 1)

        def prep(c, buf, off, L=None):
            def two(r, first=False):
                for b in range(2):
                    g = 2 * r + b
                    if not first:
                        pe.wait_ge(s[f"{c}_lo"], g - 1)
                    transpose_group(c, g, buf[:, b], 2 * b + off)
                    if L is not None and not (first and b == 0):
                        router(L, c, g - 1, 6)
                    if L is not None and not first:
                        router_back(L, g - 2, b, 7)
            two(0, True)
            if L is None:
                with pe.Fori(1, NG // 2) as r:
                    two(r)
            else:
                for r in range(1, NG // 2):
                    two(r)
                router(L, c, NG - 1, 6)
                router_back(L, NG - 2, 0, 7)
                router_back(L, NG - 1, 1, 7)

        def experts(L, gu):
            ne = 9 + L
            per = gu * ne
            Gh, Gl = w_part(W_h[L], L, 0), w_part(W_l[L], L, 0)
            Uh, Ul = w_part(W_h[L], L, 1), w_part(W_l[L], L, 1)
            Dh, Dl = w_part(W_h[L], L, 2), w_part(W_l[L], L, 2)

            def gate_up(n, g, e, k):
                b = k % 2
                wait(pe, s[f"f{L}_mul"], n - 1)
                xs = [(xTh[:, c, ds(g * GW, GW)], xTl[:, c, ds(g * GW, GW)]) for c in range(KC)]
                split3(PS[:, b, 0:GW], [(Gh[:, e, c], Gl[:, e, c], *xs[c]) for c in range(KC)])
                split3(PS[:, 2 + b, 0:GW], [(Uh[:, e, c], Ul[:, e, c], *xs[c]) for c in range(KC)]).then_inc(s[f"f{L}_gu"], 1)

            def down(n, e, k):
                b = k % 2
                pe.wait_ge(s[f"f{L}_al"], n + 1)
                wait(pe, s[f"f{L}_acc"], n - 1)
                for t in range(GT):
                    c = slice(t * P, t * P + P)
                    ins = split3(PS[:, 4 + 2 * b + t // 2, (t % 2) * D:(t % 2) * D + D], [(ah[:, b, c], al[:, b, c], Dh[:, e], Dl[:, e])])
                ins.then_inc(s[f"f{L}_dn"], 1)

            def body(r, first=False):
                for k in range(per):
                    n = r * per + k
                    gate_up(n, r * gu + k // ne, k % ne, k)
                    if L == 1 and first and k == 2:
                        pe.wait_ge(s["f1_tot"], 1)
                        M(PS[:, 7, 0:2 * NE], ones[:, :], tot[:, :], start=True, stop=True).then_inc(s["f1_sum"], 1)
                    if not first or k >= 1:
                        down(n - 1, (k - 1) % ne, (k - 1) % per)

            body(0, True)
            with pe.Fori(1, NG // gu) as r:
                body(r)
            down(NG * ne - 1, ne - 1, per - 1)

        pe.wait_ge(s["rw_split0"], 2)
        prep("c", xnc, 2, 0)
        pe.wait_ge(s["w_split0"], NG)
        experts(0, 2)
        prep("e", xn1, 0)

        last = [None]

        def wait_misc():
            if last[0] is not None:
                wait(pe, s[last[0][0]], last[0][1])

        def project(i, m, it):
            if not early(it):
                wait_misc()
            split3(PS[:, project_bank(it, m), 0:POS].rearrange("p (j c) -> p j c", j=NT),
                   [(a1h[:, k, m * P:m * P + P], a1l[:, k, m * P:m * P + P], img(xTh[:, k, :], i), img(xTl[:, k, :], i)) for k in range(KC)]).then_inc(s["e_pr"], 1)
            if project_bank(it, m) == 7:
                last[0] = ("e_prev", 3 * i + m + 1)

        def turn(it, p):
            for U in range(NU):
                sc_ = [(k, c) for k, c in s_at(U) if live(it, k)]

                def score_max():
                    if not sc_:
                        return
                    k, c = sc_.pop(0)
                    i = it - k
                    q = p ^ (k % 2)
                    if c % (NS // 2) == 0:
                        pe.wait_ge(s[f"e_in{c // (NS // 2)}"], 16 * 6 * (i + 1))
                    wait(pe, s["e_mx"], NS * i + c - (3 if early(it) else 1))
                    M(PS[:, max_bank(it, c), 0:POS], QS[q][0:MROW, c * P:c * P + P], KS[q][0:MROW, c // 9 * POS:c // 9 * POS + POS],
                      start=True, stop=True).then_inc(s["e_s"], 1)

                if live(it, 2):
                    i = it - 2
                    if U == 0:
                        pe.wait_ge(s["e_min0"], 16 * (i + 1))
                        if isinstance(it, int) and it == 2:
                            pe.wait_ge(s["d_wo"], 48)
                            pe.wait_ge(s["e_mx"], NS + S_LEAD)
                            pe.wait_ge(s["e_prev"], 3 * 2)
                    if U == NU // 2:
                        pe.wait_ge(s["e_min1"], 16 * (i + 1))
                    wait(pe, s["e_exp"], i * NU + U - 1)
                    for n in (2 * U, 2 * U + 1):
                        g, kt, cc = n // 9, n % 9 // 3, n % 3
                        ins = M(PS[0:KT, n % 4, 0:CW], KS[p][:, g * POS + kt * KT:g * POS + kt * KT + KT],
                                QS[p][:, g * HQ + cc * CW:g * HQ + cc * CW + CW], start=True, stop=True)
                    ins.then_inc(s["e_st"], 1)
                score_max()
                for k, m in av_at(U):
                    if live(it, k):
                        values(it - k, m, p ^ (k % 2))
                if U in PR_U and live(it, 0):
                    project(it, PR_U.index(U), it)
                if U == VT_U and live(it, 1):
                    pe.wait_ge(s["e_prev"], 3 * it)
                    wait_misc()
                    for kt in range(NKT):
                        ins = nc.tensor.transpose(PS[0:KT, 7, kt * P:kt * P + P], qf[1 - p][:, 2, kt * KT:kt * KT + KT], ident[:, :])
                    ins.then_inc(s["e_vt"], 1)
                    last[0] = ("e_va", it)
                for g in last_at(it, U):
                    pe.wait_ge(s["e_yr"], NGQ * (IMGS - 1) + g + 1)
                    if g:
                        pe.wait_ge(s["e_yl"], g + g // 2)
                    else:
                        wait_misc()
                    M(PS[:, 7, 0:POS], spread[:, g % 2], yr[(IMGS - 1) % 2][:, g], start=True, stop=True).then_inc(s["e_sb"], 1)
                if U in MT_U and live(it, 1):
                    b = MT_U.index(U)
                    pe.wait_ge(s["e_mx"], NS * (it - 1) + NSH * (b + 1))
                    wait_misc()
                    nc.tensor.transpose(PS[:, 7, 0:P], MX[:, b], ident[:, :]).then_inc(s["e_mT"], 1)
                    last[0] = ("e_msplit", 2 * (it - 1) + b + 1)
                score_max()

        def values(i, m, p):
            g, kt = m // NKT, m % NKT
            pe.wait_ge(s["e_exp"], i * NU + (3 * m + 2) // 2 + 1)
            if m == 0:
                pe.wait_ge(s["e_va"], i + 1)
            if kt == 0:
                wait(pe, s["e_yr"], NGQ * i + g)
            c0 = (3 * m) % RING
            for hh in range(HPG):
                ins = M(PS[32 * hh:32 * hh + 32, 6, 0:POS], VA[p][:, kt, g, :],
                        PR[:, c0:c0 + 3, :].rearrange("p c w -> p (c w)")[:, hh * POS:hh * POS + POS],
                        start=(kt == 0), stop=(kt == NKT - 1), tile_position=(0, 32 * hh))
            ins.then_inc(s["e_avt"], 1)

        pe.wait_ge(s["e_a1"], 1)
        pe.wait_ge(s["e_lo"], NG)
        pe.wait_ge(s["e_hi"], NG)
        for it in range(4):
            turn(it, it % 2)
        with pe.Fori(2, 4) as r:
            last[0] = ("e_msplit", 2 * (2 * r - 1))
            turn(2 * r, 0)
            turn(2 * r + 1, 1)
        last[0] = ("e_msplit", 14)
        for it in range(8, 11):
            turn(it, it % 2)
        warm_up(3)
        pe.wait_ge(s["e_yt"], NGQ // 2 * (IMGS - 1))
        pe.wait_ge(s["e_yl"], NGQ + 2)
        for g in range(NG + 3):
            if g < NG:
                wait(pe, s["g_res"], g - 1)
                for t in range(GT):
                    j = g * GT + t
                    b = 2 * (g % 2) + t // 2
                    for q in range(NGQ // 2):
                        ins = M(PS[:, b, (t % 2) * D:(t % 2) * D + D], yT[:, q, j * P:j * P + P], wo[:, q, :], start=(q == 0), stop=(q == NGQ // 2 - 1))
                ins.then_inc(s["g_wo"], 1)
            for t in {NG: (NG - 2, NG - 1)}.get(g, (g - 2,) if 2 <= g < NG else ()):
                if transpose_bank(t) == 4:
                    wait(pe, s["p_lo"], t)
                else:
                    pe.wait_ge(s["g_res"], NG - 1)
                transpose_group("p", t, xnp[:, t % 2], transpose_bank(t))
            if 4 <= g < NG + 1:
                router_back(1, g - 4, g % 2, 7)
            if g == NG + 2:
                router_back(1, NG - 3, 1, 7)
            if 3 <= g < NG + 3:
                router(1, "p", g - 3, router_bank(g - 3))
        router_back(1, NG - 2, 0, 7)
        router_back(1, NG - 1, 1, 7)
        pe.wait_ge(s["w_split1"], NG)
        experts(1, 3)

    ctx.close()


PR_U = [0, 1, 2]
VT_U = 3
MT_U = [5, 14]
SUM_U, SM_U, REC_U, RO_U, RB_U = [1, 2], 4, 7, 8, list(range(10, 18))
S_LEAD = 8


def s_at(U):
    c = S_LEAD + 2 * U
    return [(1, c), (1, c + 1)] if c < NS else [(0, c - NS), (0, c - NS + 1)]


def av_at(U):
    at = [(3 * m + 2) // 2 + 2 for m in range(NAV)]
    return [(3, m) for m in range(NAV) if at[m] == U + NU] + [(2, m) for m in range(NAV) if at[m] == U]


def y_at(U):
    return [(k, m // NKT) for k, m in av_at(U) if m % NKT == NKT - 1]


def last_image(i):
    return isinstance(i, int) and i == IMGS - 1


def last_at(it, U):
    if not isinstance(it, int) or it < IMGS + 1:
        return []
    return [g for k in (2, 3) if last_image(it - k) for kk, g in y_at(U - 2) if kk == k]


def transpose_bank(g):
    return 4 if g < NG - 1 else 0


def router_bank(g):
    return 6 if g < NG - 2 else 2 + g - (NG - 2)


def early(it):
    return isinstance(it, int) and it < 2


def max_bank(it, c):
    return (4, 5, 0, 1)[c % 4] if early(it) else 4 + c % 2


def project_bank(it, m):
    return (2, 3, 7)[m] if early(it) else 7


def live(it, back):
    return not isinstance(it, int) or 0 <= it - back < IMGS


def kernel(x, txt, L0_tok_Wa, L0_tok_ba, L0_tok_Wd1, L0_tok_bd1, L0_tok_Wd2, L0_tok_bd2, L0_tok_Wd3, L0_tok_bd3,
           L0_attn_Wq, L0_attn_bq, L0_attn_Wk, L0_attn_bk, L0_attn_Wv, L0_attn_bv,
           L0_ffn_router_weight, L0_ffn_correction_bias, L0_ffn_w_gate, L0_ffn_w_up, L0_ffn_w_down,
           L0_ffn_sw_gate, L0_ffn_sw_up, L0_ffn_sw_down,
           L1_attn_Wq, L1_attn_bq, L1_attn_Wk, L1_attn_bk, L1_attn_Wv, L1_attn_bv, L1_attn_Wo, L1_attn_bo,
           L1_ffn_gate_w, L1_ffn_lb_bias, L1_ffn_expert_gate_w, L1_ffn_expert_up_w, L1_ffn_expert_down_w,
           L1_ffn_shared_gate_w, L1_ffn_shared_up_w, L1_ffn_shared_down_w):
    import numpy as np
    import concourse.bacc as bacc
    from concourse.bass_utils import run_bass_kernel_spmd

    f = lambda a: np.asarray(a)
    arr = {}
    arr["x"] = f(x).reshape(P, ROWS, SIDE)
    arr["txt"] = f(txt).reshape(IMGS, TXT_T, RG, D).transpose(0, 2, 1, 3).reshape(P, TXT_T, D)
    small = []
    for n, w in enumerate((L0_tok_Wd3, L0_tok_Wd2, L0_tok_Wd1)):
        r, c = ROWS >> (n + 1), SIDE >> (n + 1)
        small.insert(0, f(w).reshape(3, RG, r, c, 3).transpose(1, 4, 0, 2, 3).reshape(RG, 3 * 3 * r * c))
    arr["wd0"] = small.pop().reshape(RG, 3, -1)
    small.append(f(L0_tok_Wa).reshape(RG, (ROWS // 8) * (SIDE // 8)))
    arr["wsmall"] = np.concatenate(small, 1)
    arr["rep"] = (np.arange(P)[None, :] % RG == np.arange(RG)[:, None]).astype(np.float32)
    arr["lbias"] = np.concatenate([f(L0_tok_bd1), f(L0_tok_bd2), f(L0_tok_bd3), f(L0_tok_ba)])[None]
    p = np.arange(P)
    consts = np.zeros((P, 3, P), np.float32)
    consts[:, 0] = np.eye(P)
    consts[:, 1] = p[:, None] // RG == p[None, :] // RG
    consts[:, 2] = np.where(p[:, None] % RG == p[None, :] % RG, 0.0, BIG)
    arr["consts"] = consts
    arr["spread"] = np.stack([p[:, None] == p[None, :] // 32 * 32 + r for r in (HD, 0)], 1).astype(np.float32)
    arr["halves"] = np.stack([p // HD % 2 == b for b in range(2)], 1).astype(np.float32)

    def rows_in(w):
        return w.reshape(KC, P, w.shape[-1]).transpose(1, 0, 2)

    arr["qkv0"] = np.stack([rows_in(f(w).T) for w in (L0_attn_Wq, L0_attn_Wk, L0_attn_Wv)], 1)
    arr["bqk0"] = np.stack([f(L0_attn_bq)[:P], f(L0_attn_bq)[P:], f(L0_attn_bk)[:P], f(L0_attn_bk)[P:]], 1)
    arr["bv0"] = f(L0_attn_bv)[None]
    arr["cb0"] = f(L0_ffn_correction_bias)[None]
    arr["lb1"] = f(L1_ffn_lb_bias)[None]
    arr["bo1"] = f(L1_attn_bo)[None]
    arr["rw0"] = rows_in(f(L0_ffn_router_weight).T)
    arr["rw1"] = rows_in(f(L1_ffn_gate_w).T)

    def ffn(gate, up, down):
        ge = lambda w: w.reshape(w.shape[0], KC, P, P).transpose(2, 0, 1, 3).reshape(P, -1)
        return np.concatenate([ge(gate), ge(up), down.transpose(1, 0, 2).reshape(P, -1)], 1)

    arr["w0"] = ffn(np.concatenate([f(L0_ffn_w_gate), f(L0_ffn_sw_gate)[None]]),
                    np.concatenate([f(L0_ffn_w_up), f(L0_ffn_sw_up)[None]]),
                    np.concatenate([f(L0_ffn_w_down), f(L0_ffn_sw_down)[None]]))
    two = lambda w: w.reshape(2, P, D)
    arr["w1"] = ffn(np.concatenate([f(L1_ffn_expert_gate_w), two(f(L1_ffn_shared_gate_w))]).transpose(0, 2, 1),
                    np.concatenate([f(L1_ffn_expert_up_w), two(f(L1_ffn_shared_up_w))]).transpose(0, 2, 1),
                    np.concatenate([f(L1_ffn_expert_down_w), f(L1_ffn_shared_down_w).reshape(D, 2, P).transpose(1, 0, 2)]).transpose(0, 2, 1))
    arr["a1"] = rows_in(np.concatenate([f(L1_attn_Wq), f(L1_attn_Wk), f(L1_attn_Wv)]).T)
    arr["bq1"] = np.stack([f(L1_attn_bq)[:P], f(L1_attn_bq)[P:], np.concatenate([f(L1_attn_bk), f(L1_attn_bv)])], 1)
    arr["wo1"] = f(L1_attn_Wo).T.reshape(NGQ // 2, 2, HPG, HD, D).transpose(2, 1, 3, 0, 4).reshape(P, NGQ // 2, D)

    nc = bacc.Bacc("TRN2", target_bir_lowering=False, num_devices=1)
    ins, A = {}, {}
    for name, a in arr.items():
        a = np.ascontiguousarray(a)
        ins["in_" + name] = a
        A[name] = nc.dram_tensor("in_" + name, a.shape, mybir.dt.from_np(a.dtype), kind="ExternalInput").ap()
    out = nc.dram_tensor("out_tokens", (P, NT, D), F32, kind="ExternalOutput").ap()
    build(nc, A, out)
    got = run_bass_kernel_spmd(nc, [ins], core_ids=[0]).results[0]["out_tokens"]
    y = np.asarray(got).reshape(IMGS, RG, NT, D)
    image = y[:, :, :ROWS].reshape(IMGS, SIDE, D)
    text = y[:, :, ROWS:].transpose(0, 2, 1, 3).reshape(IMGS, TXT_T * RG, D)
    return np.concatenate([image, text], 1)
```
